# Optimizing a Trainium2 kernel written in Bass

```python
import numpy as np
import jax
import jax.numpy as jnp

def _softmax(x, axis=-1):
    return jax.nn.softmax(x, axis=axis)

def _gelu(x):
    return jax.nn.gelu(x, approximate=True)

def _silu(x):
    return jax.nn.silu(x)

def _sigmoid(x):
    return jax.nn.sigmoid(x)

def _layernorm(x, axis=-1, eps=1e-05):
    m = jnp.mean(x, axis=axis, keepdims=True)
    v = jnp.var(x, axis=axis, keepdims=True)
    return (x - m) / jnp.sqrt(v + eps)

def _scatter_add(tgt, idx, src, axis=0):
    return tgt.at[idx].add(src)

def _segment_sum(src, seg, n):
    return jax.ops.segment_sum(src, seg, n)
kernel_name = 'mk_adj_resnorm_d4_adj_r2_8eb38a'

def setup_inputs(seed: int=0):
    np.random.seed(seed)
    _w = jnp.asarray

    def _rec_inputs():
        import jax
        import jax.numpy as jnp
        _gk = jax.random.key(seed)
        x = -0.0003929 + 0.9999 * jax.random.normal(jax.random.fold_in(_gk, 1), (32, 256, 128), jnp.float32)
        _a = jax.random.bernoulli(jax.random.fold_in(_gk, 2), 0.0625, (256, 256))
        _a = jnp.logical_or(_a, jnp.swapaxes(_a, -1, -2))
        _a = jnp.logical_or(_a, jnp.eye(256, dtype=bool))
        _af = _a.astype(jnp.float32)
        _af = _af * jax.random.uniform(jax.random.fold_in(_gk, 3), (256, 256), jnp.float32, 0.05, 1)
        adj = _af
        return (x, adj)
    x, adj = _rec_inputs()

    def _L0_gnn_setup():
        import jax, jax.numpy as jnp
        import numpy as np
        EPS = 1e-05

        def _batchnorm(x, gamma, beta):
            mu = jnp.mean(x, axis=0)
            var = jnp.var(x, axis=0)
            return (x - mu) * jax.lax.rsqrt(var + EPS) * gamma + beta
        key = jax.random.key(seed)
        ks = jax.random.split(key, 4)
        b, n, d, h, o = (32, 1024, 128, 256, 128)
        features = jax.random.normal(ks[0], (b, n, d), dtype=jnp.float32)
        A = jax.random.uniform(ks[1], (n, n), dtype=jnp.float32)
        lim1 = float(np.sqrt(6.0 / (d + h)))
        W1 = jax.random.uniform(ks[2], (h, d), minval=-lim1, maxval=lim1, dtype=jnp.float32)
        b1 = jnp.zeros((h,), jnp.float32)
        lim2 = float(np.sqrt(6.0 / (h + o)))
        W2 = jax.random.uniform(ks[3], (o, h), minval=-lim2, maxval=lim2, dtype=jnp.float32)
        b2 = jnp.zeros((o,), jnp.float32)
        g1 = jnp.ones((h,), jnp.float32)
        be1 = jnp.zeros((h,), jnp.float32)
        g2 = jnp.ones((o,), jnp.float32)
        be2 = jnp.zeros((o,), jnp.float32)
        return {'features': features, 'A': A, 'W1': W1, 'b1': b1, 'g1': g1, 'be1': be1, 'W2': W2, 'b2': b2, 'g2': g2, 'be2': be2}
    _L0_gnn_all = _L0_gnn_setup()
    _L0_gnn_in = {k: v for k, v in _L0_gnn_all.items() if k in ('W1', 'b1', 'g1', 'be1', 'W2', 'b2', 'g2', 'be2')}
    del _L0_gnn_all

    def _L1_gnn_setup():
        import jax, jax.numpy as jnp
        import numpy as np
        B, T, D, H = (64, 1024, 128, 128)
        MAX_SKIP = 4

        def _lstm_last(Wih, Whh, bih, bhh, xs):
            N, _, Hd = xs.shape
            bias = bih + bhh

            def step(carry, x_t):
                h, c = carry
                g = x_t @ Wih.T + h @ Whh.T + bias
                i, f, gg, o = jnp.split(g, 4, axis=-1)
                c = jax.nn.sigmoid(f) * c + jax.nn.sigmoid(i) * jnp.tanh(gg)
                h = jax.nn.sigmoid(o) * jnp.tanh(c)
                return ((h, c), None)
            init = (jnp.zeros((N, Hd), xs.dtype), jnp.zeros((N, Hd), xs.dtype))
            (h_last, _), _ = jax.lax.scan(step, init, jnp.swapaxes(xs, 0, 1))
            return h_last
        key = jax.random.key(seed)
        ks = jax.random.split(key, 8)
        s = 0.05
        x = jax.random.normal(ks[0], (B, T, D), jnp.float32)
        adj = jax.random.uniform(ks[1], (T, T), jnp.float32) / T
        Wg0 = jax.random.normal(ks[2], (D, H), jnp.float32) * s
        bg0 = jnp.zeros((H,), jnp.float32)
        Wg1 = jax.random.normal(ks[3], (H, H), jnp.float32) * s
        bg1 = jnp.zeros((H,), jnp.float32)
        Wih = jax.random.normal(ks[4], (MAX_SKIP, 4 * H, H), jnp.float32) * s
        Whh = jax.random.normal(ks[5], (MAX_SKIP, 4 * H, H), jnp.float32) * s
        bih = jax.random.normal(ks[6], (MAX_SKIP, 4 * H), jnp.float32) * s
        bhh = jax.random.normal(ks[7], (MAX_SKIP, 4 * H), jnp.float32) * s
        return dict(x=x, adj=adj, Wg0=Wg0, bg0=bg0, Wg1=Wg1, bg1=bg1, Wih=Wih, Whh=Whh, bih=bih, bhh=bhh)
    _L1_gnn_all = _L1_gnn_setup()
    _L1_gnn_in = {k: v for k, v in _L1_gnn_all.items() if k in ('Wg0', 'bg0', 'Wg1', 'bg1', 'Wih', 'Whh', 'bih', 'bhh')}
    del _L1_gnn_all

    def _L2_gnn_setup():
        import jax, jax.numpy as jnp
        import numpy as np
        B, N, IN_DIM, OUT_DIM, H = (2, 2048, 128, 128, 4)
        HEAD_DIM = OUT_DIM // H
        EDGE_P = 0.01
        key = jax.random.key(seed)
        k1, k2, k3 = jax.random.split(key, 3)
        h = jax.random.normal(k1, (B, N, IN_DIM), dtype=jnp.float32)
        W = jax.random.normal(k2, (IN_DIM, 3 * OUT_DIM), dtype=jnp.float32) / np.sqrt(IN_DIM)
        adj = (jax.random.uniform(k3, (N, N)) < EDGE_P).astype(jnp.float32)
        adj = jnp.maximum(adj, jnp.eye(N, dtype=jnp.float32))
        return {'h': h, 'W': W, 'adj': adj}
    _L2_gnn_all = _L2_gnn_setup()
    _L2_gnn_in = {k: v for k, v in _L2_gnn_all.items() if k in ('W',)}
    del _L2_gnn_all

    def _L3_gnn_setup():
        import jax, jax.numpy as jnp
        import numpy as np
        BT, N, D, HEADS, E = (512, 64, 128, 4, 256)
        LRELU_SLOPE = 0.2
        EPS = 1e-08
        key = jax.random.key(seed)
        ks = jax.random.split(key, 8)
        d = D
        return {'H': jax.random.normal(ks[0], (BT, N, d), jnp.float32), 'W_lin': jax.random.normal(ks[1], (d, d), jnp.float32) / np.sqrt(d).astype(np.float32), 'W_val': jax.random.normal(ks[2], (d, d), jnp.float32) / np.sqrt(d).astype(np.float32), 'a': jax.random.normal(ks[3], (HEADS, d // HEADS), jnp.float32), 'W_out': jax.random.normal(ks[4], (d, d), jnp.float32) / np.sqrt(d).astype(np.float32), 'A0': jax.random.uniform(ks[5], (N, N), jnp.float32), 'src': jax.random.randint(ks[6], (E,), 0, N, jnp.int32), 'dst': jax.random.randint(ks[7], (E,), 0, N, jnp.int32)}
    _L3_gnn_all = _L3_gnn_setup()
    _L3_gnn_in = {k: v for k, v in _L3_gnn_all.items() if k in ('W_lin', 'W_val', 'a', 'W_out', 'src', 'dst')}
    del _L3_gnn_all
    return {'x': x, 'adj': adj, 'L0_gnn_W1': _L0_gnn_in['W1'], 'L0_gnn_b1': _L0_gnn_in['b1'], 'L0_gnn_g1': _L0_gnn_in['g1'], 'L0_gnn_be1': _L0_gnn_in['be1'], 'L0_gnn_W2': _L0_gnn_in['W2'], 'L0_gnn_b2': _L0_gnn_in['b2'], 'L0_gnn_g2': _L0_gnn_in['g2'], 'L0_gnn_be2': _L0_gnn_in['be2'], 'L1_gnn_Wg0': _L1_gnn_in['Wg0'], 'L1_gnn_bg0': _L1_gnn_in['bg0'], 'L1_gnn_Wg1': _L1_gnn_in['Wg1'], 'L1_gnn_bg1': _L1_gnn_in['bg1'], 'L1_gnn_Wih': _L1_gnn_in['Wih'], 'L1_gnn_Whh': _L1_gnn_in['Whh'], 'L1_gnn_bih': _L1_gnn_in['bih'], 'L1_gnn_bhh': _L1_gnn_in['bhh'], 'L2_gnn_W': _L2_gnn_in['W'], 'L3_gnn_W_lin': _L3_gnn_in['W_lin'], 'L3_gnn_W_val': _L3_gnn_in['W_val'], 'L3_gnn_a': _L3_gnn_in['a'], 'L3_gnn_W_out': _L3_gnn_in['W_out'], 'L3_gnn_src': _L3_gnn_in['src'], 'L3_gnn_dst': _L3_gnn_in['dst']}

def reference(x, adj, L0_gnn_W1, L0_gnn_b1, L0_gnn_g1, L0_gnn_be1, L0_gnn_W2, L0_gnn_b2, L0_gnn_g2, L0_gnn_be2, L1_gnn_Wg0, L1_gnn_bg0, L1_gnn_Wg1, L1_gnn_bg1, L1_gnn_Wih, L1_gnn_Whh, L1_gnn_bih, L1_gnn_bhh, L2_gnn_W, L3_gnn_W_lin, L3_gnn_W_val, L3_gnn_a, L3_gnn_W_out, L3_gnn_src, L3_gnn_dst):
    import jax
    import jax.numpy as jnp

    def _L0_gnn_ref(features, A, W1, b1, g1, be1, W2, b2, g2, be2):
        import jax, jax.numpy as jnp
        import numpy as np
        EPS = 1e-05

        def _batchnorm(x, gamma, beta):
            mu = jnp.mean(x, axis=0)
            var = jnp.var(x, axis=0)
            return (x - mu) * jax.lax.rsqrt(var + EPS) * gamma + beta
        b, n, d = features.shape
        A_norm = A + jnp.eye(n, dtype=A.dtype)
        deg = jnp.sum(A_norm, axis=0) + jnp.sum(A_norm, axis=1) - jnp.diagonal(A_norm)
        dinv = jax.lax.rsqrt(deg)
        A_hat = A_norm * dinv[:, None] * dinv[None, :]
        agg = jnp.einsum('nm,bmd->bnd', A_hat, features)
        x = agg.reshape(-1, d)
        h = jax.nn.relu(_batchnorm(x @ W1.T + b1, g1, be1))
        out = h @ W2.T + b2
        out = _batchnorm(out, g2, be2)
        return out.reshape(b, n, -1)

    def _L1_gnn_ref(x, adj, Wg0, bg0, Wg1, bg1, Wih, Whh, bih, bhh):
        import jax, jax.numpy as jnp
        import numpy as np
        B, T, D, H = (64, 1024, 128, 128)
        MAX_SKIP = 4

        def _lstm_last(Wih, Whh, bih, bhh, xs):
            N, _, Hd = xs.shape
            bias = bih + bhh

            def step(carry, x_t):
                h, c = carry
                g = x_t @ Wih.T + h @ Whh.T + bias
                i, f, gg, o = jnp.split(g, 4, axis=-1)
                c = jax.nn.sigmoid(f) * c + jax.nn.sigmoid(i) * jnp.tanh(gg)
                h = jax.nn.sigmoid(o) * jnp.tanh(c)
                return ((h, c), None)
            init = (jnp.zeros((N, Hd), xs.dtype), jnp.zeros((N, Hd), xs.dtype))
            (h_last, _), _ = jax.lax.scan(step, init, jnp.swapaxes(xs, 0, 1))
            return h_last
        h = jax.nn.relu(jnp.einsum('ts,bsh->bth', adj, x @ Wg0 + bg0))
        h = jax.nn.relu(jnp.einsum('ts,bsh->bth', adj, h @ Wg1 + bg1))
        Bv, Tv, Hd = h.shape
        for p in range(1, MAX_SKIP + 1):
            nw = Tv // p
            wins = h[:, :nw * p, :].reshape(Bv * nw, p, Hd)
            last = _lstm_last(Wih[p - 1], Whh[p - 1], bih[p - 1], bhh[p - 1], wins)
            idx = jnp.arange(nw) * p + (p - 1)
            h = h.at[:, idx, :].set(last.reshape(Bv, nw, Hd))
        return h

    def _L2_gnn_ref(h, W, adj):
        import jax, jax.numpy as jnp
        import numpy as np
        B, N, IN_DIM, OUT_DIM, H = (2, 2048, 128, 128, 4)
        HEAD_DIM = OUT_DIM // H
        EDGE_P = 0.01
        Bn, Nn, _ = h.shape
        qkv = h @ W
        qkv = qkv.reshape(Bn, Nn, 3, H, HEAD_DIM).transpose(2, 0, 3, 1, 4)
        q, k, v = (qkv[0], qkv[1], qkv[2])
        mask = jnp.where(adj == 0, -jnp.inf, 0.0)
        scores = jnp.einsum('bhid,bhjd->bhij', q, k) / np.sqrt(HEAD_DIM) + mask
        attn = jax.nn.softmax(scores, axis=-1)
        out = jnp.einsum('bhij,bhjd->bhid', attn, v)
        return out.transpose(0, 2, 1, 3).reshape(Bn, Nn, OUT_DIM)

    def _L3_gnn_ref(H, W_lin, W_val, a, W_out, A0, src, dst):
        import jax, jax.numpy as jnp
        import numpy as np
        BT, N, D, HEADS, E = (512, 64, 128, 4, 256)
        LRELU_SLOPE = 0.2
        EPS = 1e-08
        bt, n, d = H.shape
        h, dh = a.shape
        Xq = (H @ W_lin.T).reshape(bt, n, h, dh)
        Xv = (H @ W_val.T).reshape(bt, n, h, dh)
        Qs = Xq[:, src]
        Kt = Xq[:, dst]
        e = jnp.einsum('behd,hd->beh', jax.nn.leaky_relu(Qs + Kt, LRELU_SLOPE), a)
        e = e + jnp.log(A0[src, dst] + EPS)[None, :, None]
        e_t = e.transpose(1, 0, 2)
        m = jax.ops.segment_max(e_t, src, num_segments=n)
        ex = jnp.exp(e_t - m[src])
        denom = jax.ops.segment_sum(ex, src, num_segments=n)
        attn = ex / denom[src]
        Vt = Xv[:, dst].transpose(1, 0, 2, 3)
        Y = jax.ops.segment_sum(attn[..., None] * Vt, src, num_segments=n)
        Y = Y.transpose(1, 0, 2, 3).reshape(bt, n, d)
        return Y @ W_out.T
    x = _layernorm(x + _L0_gnn_ref(x, adj, L0_gnn_W1, L0_gnn_b1, L0_gnn_g1, L0_gnn_be1, L0_gnn_W2, L0_gnn_b2, L0_gnn_g2, L0_gnn_be2), axis=-1)
    x = _layernorm(x + _L1_gnn_ref(x, adj, L1_gnn_Wg0, L1_gnn_bg0, L1_gnn_Wg1, L1_gnn_bg1, L1_gnn_Wih, L1_gnn_Whh, L1_gnn_bih, L1_gnn_bhh), axis=-1)
    x = _layernorm(x + _L2_gnn_ref(x, L2_gnn_W, adj), axis=-1)
    x = _layernorm(x + _L3_gnn_ref(x, L3_gnn_W_lin, L3_gnn_W_val, L3_gnn_a, L3_gnn_W_out, adj, L3_gnn_src, L3_gnn_dst), axis=-1)
    return x

_drawn_inputs = setup_inputs


def setup_inputs(seed=0):
    import zlib

    import numpy as np

    out = dict(_drawn_inputs(seed))
    spreads = {'L0_gnn_b1': (0.0, 0.8),
     'L0_gnn_g1': (1.0, 0.2),
     'L0_gnn_be1': (0.0, 0.1),
     'L0_gnn_b2': (0.0, 0.8),
     'L0_gnn_g2': (1.0, 0.2),
     'L0_gnn_be2': (0.0, 0.1),
     'L1_gnn_bg0': (0.0, 0.1),
     'L1_gnn_bg1': (0.0, 0.1)}
    factors = {'L1_gnn_Whh': 6.667, 'L1_gnn_bih': 2.671, 'L1_gnn_bhh': 2.782}
    for name, (base, spread) in spreads.items():
        noise = np.random.default_rng([zlib.crc32(name.encode()), seed]).standard_normal(out[name].shape)
        drawn = base * np.exp(spread * noise) if base else spread * noise
        out[name] = jnp.asarray(drawn.astype(out[name].dtype))
    for name, factor in factors.items():
        out[name] = (out[name] * factor).astype(out[name].dtype)
    return out
```

```python
from contextlib import ExitStack

import concourse.bass as bass
from concourse import mybir

F32 = mybir.dt.float32
BF16 = mybir.dt.bfloat16
I32 = mybir.dt.int32
ALU = mybir.AluOpType
ACT = mybir.ActivationFunctionType
AX_X = mybir.AxisListType.X

P = 128
EPS = 1e-5
LOG_EPS = 1e-8
NEG = -1e30
PAIR = 2
SLOPE = 0.2


def past(t, k):
    return not isinstance(t, int) or t >= k


def over(eng, total, lag, body, ahead=None):
    ahead = ahead or (lag + 3) // 2 * 2
    for t in range(ahead):
        body(t, t % 2, t // 2)
    with eng.Fori(ahead // 2, total // 2) as k:
        for u in range(2):
            body(k * 2 + u, u, k)
    for t in range(total, total + lag):
        body(t, t % 2, t // 2)


def inside(t, total):
    return not isinstance(t, int) or 0 <= t < total


def older(t, u, k, lag, total):
    if isinstance(t, int):
        if not 0 <= t - lag < total:
            return None
        return t - lag, (t - lag) % 2, (t - lag) // 2
    return t - lag, (u - lag) % 2, k + (u - lag) // 2


def cols(t, n):
    return slice(t * n, (t + 1) * n) if isinstance(t, int) else bass.ds(t * n, n)


def build_program(nc, x_tok, x_feat, adj, adj_t, w1_t, w2_t, cols1, cols2, wg0, bg0, wg1, bg1,
                  wih_t, whh_t, bih, bhh, w_qkv, w_lin_t, w_val_t, a, w_out_t, src, dst, edge_cols, out):
    B, N, D = x_tok.shape
    H1 = w1_t.shape[1]
    HB = H1 // P
    NB = N // P
    TOK = B * N
    T = B // PAIR
    W = PAIR * N
    STEPS = wih_t.shape[0]
    HEADS, DH = a.shape
    E = src.shape[0]
    EB = E // P
    assert D == P and W == 512 and HEADS * DH == P and B * HEADS == P and E == N

    with ExitStack() as ctx:
        def sb(name, shape, dt=F32):
            return ctx.enter_context(nc.sbuf_tensor(name, shape, dt))

        def sem(name):
            return ctx.enter_context(nc.semaphore(name))

        bank = [ctx.enter_context(nc.psum_tensor(f"bank{i}", [P, 512], F32)) for i in range(8)]

        X = sb("X", [P, TOK])
        HID = sb("HID", [P, HB, TOK])
        HL = HID[:, 0, :]
        CELL = HID[:, 1, :]
        HST = HID[:, 1, TOK // 2:TOK]
        VV = HID[:, 0, :]
        O = sb("O", [P, TOK])

        w1 = sb("w1", [P, H1])
        w2 = sb("w2", [P, HB, D])
        wg = sb("wg", [P, 2, D])
        bgb = sb("bgb", [P, 2, 1, D])
        wih = sb("wih", [P, STEPS, 4 * D])
        whh = sb("whh", [P, STEPS, 4 * D])
        bi = sb("bi", [P, STEPS, 4])
        bh = sb("bh", [P, STEPS, 4])
        bl = sb("bl", [P, STEPS, 4])
        wqkv = sb("wqkv", [P, 3 * D])
        wlin = sb("wlin", [P, D])
        wval = sb("wval", [P, D])
        wout = sb("wout", [P, D])
        abd = sb("abd", [P, HEADS])
        col1 = sb("col1", [P, 3, HB])
        col2 = sb("col2", [P, 3])
        adjs = sb("adjs", [P, NB, N])
        adjt = sb("adjt", [P, NB, N])
        aht = sb("aht", [P, NB, N])
        ident = sb("ident", [P, P])
        identb = sb("identb", [P, P], BF16)
        cent = sb("cent", [P, P])
        mean1 = sb("mean1", [P, P])
        ones = sb("ones", [P, P])
        mbias = sb("mbias", [P, NB, 2, N], BF16)
        hmask = sb("hmask", [P, HEADS])
        cst = sb("cst", [P, 4])
        deg = sb("deg", [P, 8])
        dinv = sb("dinv", [P, NB])
        ttr = sb("ttr", [P, N])

        ring = sb("ring", [P, 16, 512])
        st1 = sb("st1", [P, HB, T * 6])
        st2 = sb("st2", [P, T * 6])
        bn = sb("bn", [P, 3, 8])

        eci = sb("eci", [P, 2, EB], I32)
        ec = sb("ec", [P, 2, EB])
        iof = sb("iof", [P, E])
        ioi = sb("ioi", [P, E], I32)
        ioc = sb("ioc", [P, EB])
        ioci = sb("ioci", [P, EB], I32)
        keyc = sb("keyc", [P, EB])
        rank = sb("rank", [P, EB])
        scol = sb("scol", [P, 2, EB])
        dst1 = sb("dst1", [P, NB, E])
        sum1 = sb("sum1", [P, NB, E])
        src1 = sb("src1", [P, EB, N])
        early = lambda i: O[:, i * 512:(i + 1) * 512].rearrange("p (a e) -> p a e", a=2)
        ei = early(0).bitcast(I32)
        er, perm, srct, dstc, srow = (early(i) for i in range(1, 6))
        keyr = O[:, 6 * 512:6 * 512 + E]
        bc = O[:, 7 * 512:8 * 512].rearrange("p (j e c) -> p j e c", j=2, e=EB)
        lacol = sb("lacol", [P, 4])
        larow = sb("larow", [P, E])
        srk = sb("srk", [P, E])
        same = ring[:, 2:5, :].rearrange("p a (b e) -> p (a b) e", b=2)
        ET = aht[:, 0, :].rearrange("p (e c) -> p e c", e=EB)
        AT = aht[:, 1, :].rearrange("p (e c) -> p e c", e=EB)
        den = sb("den", [P, 2, 8])
        dgs = sb("dgs", [P, 2, P])
        bst = sb("bst", [P, 4, 6])
        mv = sb("mv", [P, 4, 2])

        names = ["in_w", "in_e", "pool_c", "setup_pe", "dch", "ach", "xa0", "xa1",
                 "agg_ready", "agg_copied", "hpre_ready", "h_stored", "stat1", "bn1", "relu_ready", "w2_done",
                 "o_stored", "stat2", "bn2", "tmp_ready"]
        for r in "123":
            names += [f"v{r}", f"cen{r}", f"sq{r}", f"var{r}", f"lg{r}", f"rs{r}", f"ln{r}"]
        names += ["xs_g", "y0_done", "y0_copied", "z0_done", "z0_copied", "y1_done", "y1_copied", "z1_done",
                  "z1_copied", "gates_ready", "gates_read", "prod", "c_done", "tc_ready", "h_done"]
        names += ["xs_a", "qkv", "q_c", "k_c", "v_c", "s_done", "mx", "ex", "rc", "nrm", "tp", "tp_c", "av", "av_c"]
        names += ["xs_e", "xqv", "xq_c", "xv_c", "z_done", "z_c", "lr", "e_done", "e_c",
                  "tr_e", "sm_e", "exd", "att", "tr_a", "at_c",
                  "xs_o", "vt", "vt_c", "yt", "yt_c", "o_pe", "bs", "aggr_on", "st3", "lgo", "rso", "o_fin", "out0", "out1"]
        s = {n: sem(n) for n in names}
        block = ctx.enter_context(nc.Block())

        sm = ring[:, 0:2, :].rearrange("p a (b e) -> p (a b) e", b=2)
        agg_t = lambda u: ring[:, u, :]
        h_r = lambda u, j: ring[:, 2 + 2 * u + j, :]
        x_r = lambda u: ring[:, 6 + u, :].rearrange("p (b m f) -> p b m f", b=PAIR, m=NB)
        rows4 = lambda v: v.rearrange("p (q f) -> p q f", q=4)
        v_r = lambda u: ring[:, u, :]
        sq_r = lambda u: ring[:, 2 + u, :]
        lg_r = lambda u: ring[:, 4 + u, :]
        rs_r = lambda u: ring[:, 6 + u, :]
        xs_r = lambda u: ring[:, 8 + u, :]

        qm = lambda u, h: O[:, (4 * u + h) * 512:(4 * u + h + 1) * 512]
        kr = lambda u: O[:, (8 + u) * 512:(9 + u) * 512]
        vr = lambda u: O[:, (10 + u) * 512:(11 + u) * 512]
        pr = lambda u: O[:, (12 + u) * 512:(13 + u) * 512]
        pt = lambda u: O[:, (14 + u) * 512:(15 + u) * 512]

        def unit(t, u, j, lag, total):
            if j >= lag:
                return (t, u, j - lag) if inside(t, total) else None
            if isinstance(t, int) and not 0 < t <= total:
                return None
            return t - 1, 1 - u, j - lag + 8

        def win(p, i, c):
            if p == 1:
                return HL[:, cols(c, 512)]
            if p == 3:
                v = HL[:, cols(c, 4 * N)].rearrange("f (b w) -> f b w", b=4)
                return v[:, :, i:3 * (N // 3):3]
            return HL[:, cols(c, 512 * p)].rearrange("f (w p) -> f w p", p=p)[:, :, i]

        LOOPS = []
        n_item = n_prod = 0
        for p in range(1, STEPS + 1):
            chunks = {1: TOK // 512, 2: TOK // 1024, 3: B // 4, 4: TOK // 2048}[p]
            width = 4 * (N // 3) if p == 3 else 512
            for i in range(p):
                LOOPS.append((p, i, chunks, width, n_item, n_prod))
                n_item += chunks
                n_prod += chunks if i else 0

        def shaped(ap, p, width):
            ap = ap[:, 0:width]
            return ap.rearrange("f (b w) -> f b w", b=4) if p == 3 else ap

        N_W = 16 * 16
        N_E = 16 * (9 + HEADS)
        pool_steps = 0

        @block.sync
        def _(sp):
            for d, v in ((adjs[:, :, :], adj.rearrange("(b p) m -> p b m", p=P)),
                         (adjt[:, :, :], adj_t.rearrange("(b p) m -> p b m", p=P)),
                         (w1[:, :], w1_t), (w2[:, :, :], w2_t.rearrange("(b p) m -> p b m", p=P)),
                         (wg[:, 0, :], wg0), (wg[:, 1, :], wg1),
                         (wih[:, :, :], wih_t.rearrange("s p g -> p s g")),
                         (whh[:, :, :], whh_t.rearrange("s p g -> p s g")),
                         (wqkv[:, :], w_qkv), (wlin[:, :], w_lin_t), (wval[:, :], w_val_t), (wout[:, :], w_out_t)):
                sp.dma_start(d, v).then_inc(s["in_w"], 16)
            for c in range(4):
                sp.dma_start(X[:, c * TOK // 4:(c + 1) * TOK // 4],
                             x_feat[:, c * TOK // 4:(c + 1) * TOK // 4]).then_inc(s["in_w"], 16)

            def load(t, u, k):
                if past(t, 2):
                    sp.wait_ge(s["agg_ready"], t - 1)
                src_ap = x_tok[t * PAIR:(t + 1) * PAIR] if isinstance(t, int) else x_tok[bass.ds(t * PAIR, PAIR)]
                for b in range(PAIR):
                    sp.dma_start(x_r(u)[:, b], src_ap[b].rearrange("(m p) f -> p m f", p=P)).then_inc(s[f"xa{u}"], 16)
            over(sp, T, 0, load)

            def store(t, u, k):
                sp.wait_ge(s["o_fin"], t + 1)
                dst_ap = out[t * PAIR:(t + 1) * PAIR] if isinstance(t, int) else out[bass.ds(t * PAIR, PAIR)]
                for b in range(PAIR):
                    sp.dma_start(dst_ap[b].rearrange("(m p) f -> p m f", p=P),
                                 ring[:, 14 + u, :].rearrange("p (b m f) -> p b m f", b=PAIR, m=NB)[:, b])\
                        .then_inc(s[f"out{u}"], 16)
            over(sp, T, 0, store)
            for u in range(2):
                sp.wait_ge(s[f"out{u}"], 16 * PAIR * T // 2)

        @block.gpsimd
        def _(pool):
            nonlocal pool_steps
            n = 0

            def made(ins):
                nonlocal n
                n += 1
                ins.then_inc(s["pool_c"], 1)
                pool.wait_ge(s["pool_c"], n)

            for d, v in ((col1[:, :, :], cols1), (col2[:, :], cols2), (bi[:, :, :], bih), (bh[:, :, :], bhh),
                         (eci[:, :, :], edge_cols)):
                pool.dma_start(d, v).then_inc(s["in_e"], 16)
            for j, v in enumerate((bg0, bg1)):
                pool.dma_start(bgb[:, j, 0, :], v.rearrange("(a f) -> a f", a=1).to_broadcast([P, D]))\
                    .then_inc(s["in_e"], 16)
            for j, v in enumerate((src, dst)):
                pool.dma_start(ei[:, j, :], v.rearrange("(a f) -> a f", a=1).to_broadcast([P, E]))\
                    .then_inc(s["in_e"], 16)
            made(pool.memset(abd[:, :], 0.0))
            for h in range(HEADS):
                pool.dma_start(abd[h * DH:(h + 1) * DH, h:h + 1], a[h].rearrange("(p o) -> p o", o=1))\
                    .then_inc(s["in_e"], 16)
            made(pool.memset(ident[:, :], 0.0))
            made(pool.affine_select(out=ident[:, :], in_=ident[:, :], compare_op=ALU.not_equal, fill=1.0, base=0,
                                    pattern=[[-1, P]], channel_multiplier=1))
            made(pool.memset(ones[:, :], 1.0))
            made(pool.memset(mean1[:, :], 1.0 / D))
            made(pool.memset(hmask[:, :], 0.0))
            for h in range(HEADS):
                made(pool.memset(hmask[h * DH:(h + 1) * DH, h:h + 1], float(DH) ** -0.5))
            made(pool.memset(cst[:, 0:1], EPS))
            made(pool.memset(cst[:, 1:2], LOG_EPS))
            made(pool.iota(ioi[:, :], pattern=[[1, E]], base=0, channel_multiplier=0))
            made(pool.iota(ioci[:, :], pattern=[[P, EB]], base=0, channel_multiplier=1))
            pool_steps = n

            def copies(ln, slot_free, ready):
                def body(t, u, k):
                    pool.wait_ge(s[ln], t + 1)
                    if past(t, 2):
                        pool.wait_ge(s[slot_free], t - 1)
                    pool.tensor_copy(xs_r(u), X[:, cols(t, W)]).then_inc(s[ready], 1)
                over(pool, T, 0, body)
            copies("ln1", "y0_done", "xs_g")
            copies("ln2", "qkv", "xs_a")
            copies("ln3", "xqv", "xs_e")
            pool.wait_ge(s["xqv"], T)
            copies("ln3", "o_pe", "xs_o")


        at = {}

        @block.vector
        def _(dve):
            n = 0

            def link(ins, name=None):
                nonlocal n
                n += 1
                ins.then_inc(s["dch"], 1)
                dve.wait_ge(s["dch"], n)
                if name:
                    at[name] = n

            dve.wait_ge(s["in_w"], N_W)
            dve.wait_ge(s["in_e"], N_E)
            dve.wait_ge(s["pool_c"], pool_steps)

            link(dve.tensor_reduce(deg[:, 0:2], adjs[:, :, :], AX_X, ALU.add))
            link(dve.tensor_reduce(deg[:, 2:4], adjt[:, :, :], AX_X, ALU.add))
            for m in range(NB):
                link(dve.tensor_tensor_reduce(ttr[:, 0:P], adjs[:, m, m * P:(m + 1) * P], ident[:, :], 1.0, 0.0,
                                              ALU.mult, ALU.add, deg[:, 4 + m:5 + m]))
            link(dve.tensor_tensor(deg[:, 0:2], deg[:, 0:2], deg[:, 2:4], ALU.add))
            link(dve.tensor_tensor(deg[:, 0:2], deg[:, 0:2], deg[:, 4:6], ALU.subtract))
            link(dve.tensor_scalar(deg[:, 4:6], deg[:, 0:2], 1.0, None, ALU.add), "deg")
            dve.wait_ge(s["ach"], 1)
            link(dve.reciprocal(dinv[:, :], deg[:, 6:8]))
            for m in range(NB):
                link(dve.tensor_scalar(dgs[:, m, :], ident[:, :], dinv[:, m:m + 1], None, ALU.mult), "diag")
            for m in range(NB):
                link(dve.tensor_copy(aht[:, m, :], adjt[:, m, :]))
                link(dve.tensor_tensor(aht[:, m, m * P:(m + 1) * P], adjt[:, m, m * P:(m + 1) * P], ident[:, :],
                                       ALU.add))
            dve.wait_ge(s["setup_pe"], 1)
            for m in range(NB):
                link(dve.scalar_tensor_tensor(aht[:, m, :], aht[:, m, :], dinv[:, m:m + 1], bank[7][:, 0:N],
                                              ALU.mult, ALU.mult), "aht")

            for m in range(NB):
                for h in range(2):
                    link(dve.tensor_scalar(mbias[:, m, h, :], adjs[:, m, :], 0.0, NEG, ALU.is_equal, ALU.mult))
            link(dve.tensor_copy(identb[:, :], ident[:, :]))
            link(dve.tensor_tensor(cent[:, :], ident[:, :], mean1[:, :], ALU.subtract))
            link(dve.tensor_tensor(bl[:, :, :], bi[:, :, :], bh[:, :, :], ALU.add))

            for j in range(2):
                link(dve.tensor_copy(er[:, j, :], ei[:, j, :]))
                link(dve.tensor_copy(ec[:, j, :], eci[:, j, :]))
            link(dve.tensor_copy(iof[:, :], ioi[:, :]))
            link(dve.tensor_copy(ioc[:, :], ioci[:, :]))
            link(dve.scalar_tensor_tensor(keyr[:, :], er[:, 0, :], float(E), iof[:, :], ALU.mult, ALU.add))
            link(dve.scalar_tensor_tensor(keyc[:, :], ec[:, 0, :], float(E), ioc[:, :], ALU.mult, ALU.add))
            for e in range(EB):
                link(dve.tensor_scalar(ttr[:, :], keyr[:, :], keyc[:, e:e + 1], None, ALU.is_lt, ALU.add,
                                       accum_out=rank[:, e:e + 1]))
                link(dve.tensor_scalar(perm[:, e, :], iof[:, :], rank[:, e:e + 1], None, ALU.is_equal))
                for j in range(2):
                    link(dve.tensor_scalar(bc[:, j, e, :], ones[:, :], ec[:, j, e:e + 1], None, ALU.mult), "perm")
            dve.wait_ge(s["setup_pe"], 2)
            for j in range(2):
                link(dve.tensor_copy(srow[:, j, :], bank[6][:, j * E:(j + 1) * E]))
                link(dve.tensor_copy(scol[:, j, :], bank[5][:, j * EB:(j + 1) * EB]))
            for m in range(NB):
                link(dve.tensor_scalar(srct[:, m, :], srow[:, 0, :], ioc[:, m:m + 1], None, ALU.is_equal))
                link(dve.tensor_scalar(dst1[:, m, :], srow[:, 1, :], ioc[:, m:m + 1], None, ALU.is_equal))
                link(dve.tensor_tensor(sum1[:, m, :], srct[:, m, :], dst1[:, m, :], ALU.add), "srct")
            for e in range(EB):
                link(dve.tensor_scalar(src1[:, e, :], iof[:, :], scol[:, 0, e:e + 1], None, ALU.is_equal))
                link(dve.tensor_scalar(dstc[:, e, :], iof[:, :], scol[:, 1, e:e + 1], None, ALU.is_equal))
            dve.wait_ge(s["setup_pe"], 3)
            for e in range(EB):
                link(dve.tensor_tensor(ttr[:, :], bank[7][:, e * N:(e + 1) * N], dstc[:, e, :], ALU.mult))
                link(dve.tensor_reduce(lacol[:, e:e + 1], ttr[:, :], AX_X, ALU.add), "adje")
            dve.wait_ge(s["ach"], 2)
            for e in range(EB):
                link(dve.tensor_scalar(dgs[:, e, :], ident[:, :], lacol[:, 2 + e:3 + e], None, ALU.mult), "ladiag")
            dve.wait_ge(s["setup_pe"], 4)
            link(dve.tensor_copy(larow[:, :], bank[5][:, 0:E]))
            link(dve.tensor_copy(srk[:, :], srow[:, 0, :]), "edges")

            def stats1(t, u, k):
                dve.wait_ge(s["h_stored"], t + 1)
                for j in range(HB):
                    ins = dve.bn_stats(st1[:, j, cols(t, 6)], HID[:, j, cols(t, W)])
                ins.then_inc(s["stat1"], 1)
            over(dve, T, 0, stats1)
            dve.wait_ge(s["stat1"], T)
            for j in range(HB):
                ins = dve.bn_aggr(bn[:, j, 0:2], st1[:, j, :])
            ins.then_inc(s["stat1"], 1)
            dve.wait_ge(s["ach"], 3)
            link(dve.reciprocal(bn[:, 0:2, 3], bn[:, 0:2, 2]))
            link(dve.tensor_tensor(bn[:, 0:2, 4], bn[:, 0:2, 3], col1[:, 1, :], ALU.mult))
            link(dve.tensor_tensor(bn[:, 0:2, 6], bn[:, 0:2, 0], bn[:, 0:2, 4], ALU.mult))
            dve.tensor_tensor(bn[:, 0:2, 5], col1[:, 2, :], bn[:, 0:2, 6], ALU.subtract).then_inc(s["bn1"], 1)

            def stats2(t, u, k):
                dve.wait_ge(s["o_stored"], t + 1)
                dve.bn_stats(st2[:, cols(t, 6)], O[:, cols(t, W)]).then_inc(s["stat2"], 1)
            over(dve, T, 0, stats2)
            dve.wait_ge(s["stat2"], T)
            dve.bn_aggr(bn[:, 2, 0:2], st2[:, :]).then_inc(s["stat2"], 1)
            dve.wait_ge(s["ach"], 4)
            link(dve.reciprocal(bn[:, 2, 3:4], bn[:, 2, 2:3]))
            link(dve.tensor_tensor(bn[:, 2, 4:5], bn[:, 2, 3:4], col2[:, 1:2], ALU.mult))
            link(dve.tensor_tensor(bn[:, 2, 6:7], bn[:, 2, 0:1], bn[:, 2, 4:5], ALU.mult))
            link(dve.tensor_tensor(bn[:, 2, 5:6], col2[:, 2:3], bn[:, 2, 6:7], ALU.subtract))

            def norm(r, add):
                def body(t, u, k):
                    if inside(t, T):
                        if past(t, 2):
                            dve.wait_ge(s["cen" + r], t - 1)
                        add(t, u).then_inc(s["v" + r], 1)
                    old = older(t, u, k, 1, T)
                    if old:
                        t1, u1, _ = old
                        dve.wait_ge(s["rs" + r], t1 + 1)
                        dve.tensor_tensor(X[:, cols(t1, W)], bank[u1][:, :], rs_r(u1), ALU.mult)\
                            .then_inc(s["ln" + r], 1)
                over(dve, T, 1, body)

            def add1(t, u):
                dve.tensor_scalar(ring[:, 14 + u, :], O[:, cols(t, W)], bn[:, 2, 4:5], bn[:, 2, 5:6], ALU.mult, ALU.add)\
                    .then_inc(s["tmp_ready"], 1)
                dve.wait_ge(s["tmp_ready"], t + 1)
                return dve.tensor_tensor(v_r(u), ring[:, 14 + u, :], X[:, cols(t, W)], ALU.add)
            norm("1", add1)

            def gcn(t, u, k):
                old = older(t, u, k, 2, T)
                if old:
                    t2, u2, _ = old
                    dve.wait_ge(s["y1_done"], t2 + 1)
                    if past(t2, 2):
                        dve.wait_ge(s["z1_done"], t2 - 1)
                    dve.tensor_tensor(rows4(ring[:, 14 + u2, :]), rows4(bank[4 + u2][:, :]),
                                      bgb[:, 1].to_broadcast([P, 4, D]), ALU.add).then_inc(s["y1_copied"], 1)
                if inside(t, T):
                    dve.wait_ge(s["y0_done"], t + 1)
                    if past(t, 2):
                        dve.wait_ge(s["z0_done"], t - 1)
                    dve.tensor_tensor(rows4(ring[:, 10 + u, :]), rows4(bank[u][:, :]),
                                      bgb[:, 0].to_broadcast([P, 4, D]), ALU.add).then_inc(s["y0_copied"], 1)
            over(dve, T, 2, gcn)

            def lstm(p, i, chunks, width, base, base2):
                def body(c, u, k):
                    if inside(c, chunks):
                        dve.wait_ge(s["gates_read"], c + (base + 1))
                        cell = CELL[:, cols(c, width)]
                        ig, gg, fg = (ring[:, 2 * g + u, 0:width] for g in (0, 2, 1))
                        if i == 0:
                            dve.tensor_tensor(cell, ig, gg, ALU.mult).then_inc(s["c_done"], 1)
                        else:
                            dve.tensor_tensor(ring[:, 10 + u, 0:width], fg, cell, ALU.mult).then_inc(s["prod"], 1)
                            dve.tensor_tensor(ring[:, 12 + u, 0:width], ig, gg, ALU.mult).then_inc(s["prod"], 1)
                            dve.wait_ge(s["prod"], c * 2 + (2 * base2 + 2))
                            dve.tensor_tensor(cell, ring[:, 10 + u, 0:width], ring[:, 12 + u, 0:width], ALU.add)\
                                .then_inc(s["c_done"], 1)
                    old = older(c, u, k, 1, chunks)
                    if old:
                        c1, u1, _ = old
                        dve.wait_ge(s["tc_ready"], c1 + (base + 1))
                        o = win(p, i, c1) if i == p - 1 else HST[:, cols(c1, width)]
                        q = p if i == p - 1 else 1
                        dve.tensor_tensor(o, shaped(ring[:, 6 + u1, :], q, width), shaped(ring[:, 8 + u1, :], q, width),
                                          ALU.mult).then_inc(s["h_done"], 1)
                over(dve, chunks, 1, body, 2)
            for loop in LOOPS:
                lstm(*loop)
            dve.wait_ge(s["h_done"], n_item)
            norm("2", lambda t, u: dve.tensor_tensor(v_r(u), X[:, cols(t, W)], HL[:, cols(t, W)], ALU.add))

            def attend(t, u, k):
                if inside(t, T):
                    dve.wait_ge(s["qkv"], t + 1)
                    if past(t, 2):
                        dve.wait_ge(s["av"], 8 * (t - 1))
                    dve.tensor_copy(kr(u), bank[1][:, :]).then_inc(s["k_c"], 1)
                    dve.tensor_copy(vr(u), bank[2][:, :]).then_inc(s["v_c"], 1)
                for j in range(8):
                    w = unit(t, u, j, 0, T)
                    if w:
                        t0, _, j0 = w
                        dve.wait_ge(s["s_done"], 8 * t0 + (j0 + 1))
                        dve.tensor_reduce(den[:, j0 % 2, 0:2], bank[3 + j0 % 2][:, :].rearrange("p (h n) -> p h n", h=2),
                                          AX_X, ALU.max, negate=True).then_inc(s["mx"], 1)
                    w = unit(t, u, j, 1, T)
                    if w:
                        t1, _, j1 = w
                        dve.wait_ge(s["ex"], 8 * t1 + (j1 + 1))
                        dve.reciprocal(den[:, j1 % 2, 4:6], den[:, j1 % 2, 2:4]).then_inc(s["rc"], 1)
                        dve.wait_ge(s["rc"], 8 * t1 + (j1 + 1))
                        for h in range(2):
                            ins = dve.tensor_scalar(pr(j1 % 2)[:, h * N:(h + 1) * N], pr(j1 % 2)[:, h * N:(h + 1) * N],
                                                    den[:, j1 % 2, 4 + h:5 + h], None, ALU.mult)
                        ins.then_inc(s["nrm"], 1)
                    if j == 3:
                        old = older(t, u, k, 1, T)
                        if old:
                            dve.wait_ge(s["av"], 8 * old[0] + 8)
                            dve.tensor_copy(HL[:, cols(old[0], W)], bank[7][:, :]).then_inc(s["av_c"], 1)
            over(dve, T, 1, attend, 2)
            dve.wait_ge(s["av_c"], T)
            norm("3", lambda t, u: dve.tensor_tensor(v_r(u), X[:, cols(t, W)], HL[:, cols(t, W)], ALU.add))

            def edges(t, u, k):
                if inside(t, T):
                    dve.wait_ge(s["xqv"], t + 1)
                    dve.tensor_copy(VV[:, cols(t, W)], bank[1][:, :]).then_inc(s["xv_c"], 1)
                    dve.wait_ge(s["z_c"], t + 1)
                    if past(t, 1):
                        dve.wait_ge(s["e_done"], t)
                    dve.tensor_tensor(ring[:, 12, :], bank[4][:, :], ring[:, 11, :], ALU.max).then_inc(s["lr"], 1)
                    dve.wait_ge(s["e_done"], t + 1)
                    dve.tensor_copy(ET[:, :, cols(t, PAIR * HEADS)],
                                    bank[5][:, 0:EB * PAIR * HEADS].rearrange("p (e c) -> p e c", e=EB))\
                        .then_inc(s["e_c"], 1)
            over(dve, T, 0, edges)

            link(dve.tensor_tensor(same[:, 5, 1:E], srk[:, 1:E], srk[:, 0:E - 1], ALU.not_equal))
            for j in range(2):
                link(dve.memset(same[:, j, :], NEG))
                link(dve.memset(same[:, 2 + j, :], 0.0))
            link(dve.tensor_scalar(same[:, 0, 1:E], same[:, 5, 1:E], NEG, None, ALU.mult))
            link(dve.tensor_scalar(same[:, 1, 0:E - 1], same[:, 5, 1:E], NEG, None, ALU.mult))
            link(dve.tensor_scalar(same[:, 2, 1:E], same[:, 5, 1:E], -1.0, 1.0, ALU.mult, ALU.add))
            link(dve.tensor_scalar(same[:, 3, 0:E - 1], same[:, 5, 1:E], -1.0, 1.0, ALU.mult, ALU.add))
            link(dve.tensor_scalar(same[:, 4, :], same[:, 3, :], -1.0, 1.0, ALU.mult, ALU.add))

            def scan(o, x, y, first, op0, op1, back):
                v = (lambda z: z[:, ::-1]) if back else (lambda z: z)
                return dve.tensor_tensor_scan(v(o), v(x), v(y), first, op0, op1)
            dve.wait_ge(s["tr_e"], 1)
            link(dve.tensor_tensor(sm[:, 0, :], bank[0][:, 0:E], larow[:, :], ALU.add))
            link(scan(sm[:, 1, :], same[:, 0, :], sm[:, 0, :], NEG, ALU.add, ALU.max, False))
            link(scan(sm[:, 2, :], same[:, 1, :], sm[:, 1, :], NEG, ALU.add, ALU.max, True))
            dve.tensor_tensor(sm[:, 1, :], sm[:, 0, :], sm[:, 2, :], ALU.subtract).then_inc(s["sm_e"], 1)
            dve.wait_ge(s["exd"], 1)
            link(scan(sm[:, 0, :], same[:, 2, :], sm[:, 2, :], 0.0, ALU.mult, ALU.add, False))
            link(dve.tensor_tensor(sm[:, 1, :], sm[:, 0, :], same[:, 4, :], ALU.mult))
            link(scan(sm[:, 0, :], same[:, 3, :], sm[:, 1, :], 0.0, ALU.mult, ALU.add, True))
            link(dve.reciprocal(sm[:, 1, :], sm[:, 0, :]))
            dve.tensor_tensor(sm[:, 3, :], sm[:, 2, :], sm[:, 1, :], ALU.mult).then_inc(s["att"], 1)
            dve.wait_ge(s["tr_a"], 1)
            dve.tensor_copy(AT[:, :, :], bank[1][:, 0:EB * P].rearrange("p (e c) -> p e c", e=EB)).then_inc(s["at_c"], 1)
            dve.wait_ge(s["at_c"], 1)

            def rows(t, u, k):
                if inside(t, T):
                    dve.wait_ge(s["vt"], t + 1)
                    if past(t, 1):
                        dve.wait_ge(s["yt"], t)
                    for e in range(EB):
                        w = AT[:, e, cols(t, PAIR * HEADS)].rearrange("p (c o) -> p c o", o=1)
                        ins = dve.tensor_tensor(ring[:, 12, e * 256:(e + 1) * 256].rearrange("p (c d) -> p c d", d=DH),
                                                bank[2][:, e * 256:(e + 1) * 256].rearrange("p (c d) -> p c d", d=DH),
                                                w.to_broadcast([P, PAIR * HEADS, DH]), ALU.mult)
                    ins.then_inc(s["vt_c"], 1)
                    dve.wait_ge(s["o_pe"], t + 1)
                    if past(t, 1):
                        dve.wait_ge(s["o_fin"], t)
                    for q in range(4):
                        ins = dve.bn_stats(bst[:, q, :], bank[6 + u][:, q * P:(q + 1) * P])
                    ins.then_inc(s["bs"], 1)
                    dve.wait_ge(s["bs"], 2 * t + 1)
                    dve.sem_inc(s["aggr_on"], 1)
                    for q in range(4):
                        ins = dve.bn_aggr(mv[:, q, :], bst[:, q, :])
                    ins.then_inc(s["st3"], 1)
                    dve.wait_ge(s["rso"], t + 1)
                    dve.scalar_tensor_tensor(den[:, 1, 4:8], mv[:, :, 0], -1.0, den[:, 1, 0:4], ALU.mult, ALU.mult)\
                        .then_inc(s["bs"], 1)
                    dve.wait_ge(s["bs"], 2 * t + 2)
                    if past(t, 2):
                        dve.wait_ge(s[f"out{u}"], 16 * PAIR * k)
                    for q in range(4):
                        ins = dve.tensor_scalar(ring[:, 14 + u, q * P:(q + 1) * P], bank[6 + u][:, q * P:(q + 1) * P],
                                                den[:, 1, q:q + 1], den[:, 1, 4 + q:5 + q], ALU.mult, ALU.add)
                    ins.then_inc(s["o_fin"], 1)
            over(dve, T, 0, rows)

        @block.scalar
        def _(act):
            n = 0

            def link(ins):
                nonlocal n
                n += 1
                ins.then_inc(s["ach"], 1)
                act.wait_ge(s["ach"], n)

            act.wait_ge(s["dch"], at["deg"])
            link(act.activation(deg[:, 6:8], deg[:, 4:6], ACT.Sqrt))
            act.wait_ge(s["dch"], at["adje"])
            link(act.activation(lacol[:, 2:4], lacol[:, 0:2], ACT.Ln, bias=cst[:, 1:2]))

            def agg(t, u, k):
                if inside(t, T):
                    act.wait_ge(s["agg_ready"], t + 1)
                    if past(t, 2):
                        act.wait_ge(s["hpre_ready"], t - 1)
                    act.activation(agg_t(u), bank[u][:, :], ACT.Copy).then_inc(s["agg_copied"], 1)
                old = older(t, u, k, 1, T)
                if old:
                    t1, u1, _ = old
                    act.wait_ge(s["hpre_ready"], t1 + 1)
                    for j in range(HB):
                        ins = act.activation(HID[:, j, cols(t1, W)], bank[2 + 2 * u1 + j][:, :], ACT.Identity,
                                             bias=col1[:, 0, j:j + 1])
                    ins.then_inc(s["h_stored"], 1)
            act.wait_ge(s["in_e"], N_E)
            over(act, T, 1, agg)

            act.wait_ge(s["stat1"], T + 1)
            link(act.activation(bn[:, 0:2, 2], bn[:, 0:2, 1], ACT.Sqrt, bias=cst[:, 0:1]))
            act.wait_ge(s["bn1"], 1)

            def layer2(t, u, k):
                if inside(t, T):
                    if past(t, 2):
                        act.wait_ge(s["w2_done"], t - 1)
                    for j in range(HB):
                        ins = act.activation(h_r(u, j), HID[:, j, cols(t, W)], ACT.Relu, scale=bn[:, j, 4:5],
                                             bias=bn[:, j, 5:6])
                    ins.then_inc(s["relu_ready"], 1)
                old = older(t, u, k, 1, T)
                if old:
                    t1, u1, _ = old
                    act.wait_ge(s["w2_done"], t1 + 1)
                    act.activation(O[:, cols(t1, W)], bank[u1][:, :], ACT.Identity, bias=col2[:, 0:1])\
                        .then_inc(s["o_stored"], 1)
            over(act, T, 1, layer2)

            act.wait_ge(s["stat2"], T + 1)
            link(act.activation(bn[:, 2, 2:3], bn[:, 2, 1:2], ACT.Sqrt, bias=cst[:, 0:1]))

            def norm(r):
                def body(t, u, k):
                    if inside(t, T):
                        act.wait_ge(s["cen" + r], t + 1)
                        if past(t, 2):
                            act.wait_ge(s["var" + r], t - 1)
                        act.activation(sq_r(u), bank[u][:, :], ACT.Square).then_inc(s["sq" + r], 1)
                    old = older(t, u, k, 1, T)
                    if old:
                        t1, u1, _ = old
                        act.wait_ge(s["var" + r], t1 + 1)
                        if past(t1, 2):
                            act.wait_ge(s["ln" + r], t1 - 1)
                        act.activation(lg_r(u1), bank[2 + u1][:, :], ACT.Ln, bias=cst[:, 0:1])\
                            .then_inc(s["lg" + r], 1)
                        act.wait_ge(s["lg" + r], t1 + 1)
                        act.activation(rs_r(u1), lg_r(u1), ACT.Exp, scale=-0.5).then_inc(s["rs" + r], 1)
                over(act, T, 1, body)
            norm("1")

            def gcn(t, u, k):
                old = older(t, u, k, 3, T)
                if old:
                    t3, u3, _ = old
                    act.wait_ge(s["z1_done"], t3 + 1)
                    act.activation(HL[:, cols(t3, W)], bank[6 + u3][:, :], ACT.Relu).then_inc(s["z1_copied"], 1)
                old = older(t, u, k, 1, T)
                if old:
                    t1, u1, _ = old
                    act.wait_ge(s["z0_done"], t1 + 1)
                    if past(t1, 2):
                        act.wait_ge(s["y1_done"], t1 - 1)
                    act.activation(ring[:, 12 + u1, :], bank[2 + u1][:, :], ACT.Relu).then_inc(s["z0_copied"], 1)
            over(act, T, 3, gcn)

            def lstm(p, i, chunks, width, base, _):
                order = (0, 2, 3) if i == 0 else (0, 2, 1, 3)

                def body(c, u, k):
                    if inside(c, chunks):
                        act.wait_ge(s["gates_ready"], c + (base + 1))
                        if past(c, 2) or base:
                            act.wait_ge(s["h_done"], c + (base - 1))
                        for g in order:
                            ins = act.activation(shaped(ring[:, 2 * g + u, :], p, width),
                                                 shaped(bank[2 * g + u][:, :], p, width),
                                                 ACT.Tanh if g == 2 else ACT.Sigmoid, bias=bl[:, p - 1, g:g + 1])
                        ins.then_inc(s["gates_read"], 1)
                    old = older(c, u, k, 1, chunks)
                    if old:
                        c1, u1, _ = old
                        act.wait_ge(s["c_done"], c1 + (base + 1))
                        act.activation(ring[:, 8 + u1, 0:width], CELL[:, cols(c1, width)], ACT.Tanh)\
                            .then_inc(s["tc_ready"], 1)
                over(act, chunks, 1, body, 2)
            for loop in LOOPS:
                lstm(*loop)
            norm("2")

            def attend(t, u, k):
                if inside(t, T):
                    act.wait_ge(s["qkv"], t + 1)
                    if past(t, 2):
                        act.wait_ge(s["s_done"], 8 * (t - 1))
                    for h in range(HEADS):
                        ins = act.activation(qm(u, h), bank[0][:, :], ACT.Copy, scale=hmask[:, h:h + 1])
                    ins.then_inc(s["q_c"], 1)
                for j in range(8):
                    w = unit(t, u, j, 0, T)
                    if w:
                        t0, _, j0 = w
                        act.wait_ge(s["mx"], 8 * t0 + (j0 + 1))
                        if j0 >= 2 or past(t0, 1):
                            act.wait_ge(s["tp"], 8 * t0 + (j0 - 1))
                        for h in range(2):
                            ins = act.activation(pr(j0 % 2)[:, h * N:(h + 1) * N],
                                                 bank[3 + j0 % 2][:, h * N:(h + 1) * N], ACT.Exp,
                                                 bias=den[:, j0 % 2, h:h + 1], accum_out=den[:, j0 % 2, 2 + h:3 + h])
                        ins.then_inc(s["ex"], 1)
                    w = unit(t, u, j, 2, T)
                    if w:
                        t2, _, j2 = w
                        act.wait_ge(s["tp"], 8 * t2 + (j2 + 1))
                        if j2 >= 2 or past(t2, 1):
                            act.wait_ge(s["av"], 8 * t2 + (j2 - 1))
                        act.activation(pt(j2 % 2), bank[5 + j2 % 2][:, :], ACT.Copy).then_inc(s["tp_c"], 1)
            over(act, T, 1, attend, 2)
            norm("3")

            def edges(t, u, k):
                if inside(t, T):
                    act.wait_ge(s["xqv"], t + 1)
                    if past(t, 1):
                        act.wait_ge(s["z_done"], t)
                    act.activation(ring[:, 10, :], bank[0][:, :], ACT.Copy).then_inc(s["xq_c"], 1)
                    act.wait_ge(s["z_done"], t + 1)
                    if past(t, 1):
                        act.wait_ge(s["lr"], t)
                    act.activation(ring[:, 11, :], bank[4][:, :], ACT.Copy, scale=SLOPE).then_inc(s["z_c"], 1)
            over(act, T, 0, edges)

            act.wait_ge(s["sm_e"], 1)
            act.activation(sm[:, 2, :], sm[:, 1, :], ACT.Exp).then_inc(s["exd"], 1)

            def rows(t, u, k):
                if inside(t, T):
                    act.wait_ge(s["yt"], t + 1)
                    if past(t, 1):
                        act.wait_ge(s["o_pe"], t)
                    act.activation(ring[:, 13, :], bank[4][:, :], ACT.Copy).then_inc(s["yt_c"], 1)
                    act.wait_ge(s["st3"], t + 1)
                    act.activation(den[:, 0, 0:4], mv[:, :, 1], ACT.Ln, bias=cst[:, 0:1]).then_inc(s["lgo"], 1)
                    act.wait_ge(s["lgo"], t + 1)
                    if past(t, 1):
                        act.wait_ge(s["o_fin"], t)
                    act.activation(den[:, 1, 0:4], den[:, 0, 0:4], ACT.Exp, scale=-0.5).then_inc(s["rso"], 1)
            over(act, T, 0, rows)

        @block.tensor
        def _(pe):
            def mm(o, l, r, first=True, last=True):
                return pe.matmul(o, l, r, start=first, stop=last)

            pe.wait_ge(s["dch"], at["diag"])
            for m in range(NB):
                ins = mm(bank[7][:, m * P:(m + 1) * P], ones[:, :], dgs[:, m, :])
            ins.then_inc(s["setup_pe"], 1)
            pe.wait_ge(s["dch"], at["perm"])
            for j in range(2):
                for e in range(EB):
                    mm(bank[6][:, j * E:(j + 1) * E], bc[:, j, e, :], perm[:, e, :], e == 0, e == EB - 1)
                for q in range(EB):
                    for e in range(EB):
                        ins = mm(bank[5][:, j * EB + q:j * EB + q + 1], perm[:, e, q * P:(q + 1) * P], ec[:, j, e:e + 1],
                                 e == 0, e == EB - 1)
            ins.then_inc(s["setup_pe"], 1)
            pe.wait_ge(s["dch"], at["srct"])
            for e in range(EB):
                for m in range(NB):
                    ins = mm(bank[7][:, e * N:(e + 1) * N], srct[:, m, e * P:(e + 1) * P], adjs[:, m, :],
                             m == 0, m == NB - 1)
            ins.then_inc(s["setup_pe"], 1)
            pe.wait_ge(s["dch"], at["ladiag"])
            for e in range(EB):
                ins = mm(bank[5][:, e * P:(e + 1) * P], ones[:, :], dgs[:, e, :])
            ins.then_inc(s["setup_pe"], 1)
            pe.wait_ge(s["dch"], at["edges"])

            def agg(t, u, k):
                if inside(t, T):
                    pe.wait_ge(s[f"xa{u}"], 16 * PAIR * k + 16 * PAIR)
                    if past(t, 2):
                        pe.wait_ge(s["agg_copied"], t - 1)
                    for b in range(PAIR):
                        for m in range(NB):
                            ins = mm(bank[u][:, b * N:(b + 1) * N], x_r(u)[:, b, m, :], aht[:, m, :], m == 0, m == NB - 1)
                    ins.then_inc(s["agg_ready"], 1)
                old = older(t, u, k, 1, T)
                if old:
                    t1, u1, _ = old
                    pe.wait_ge(s["agg_copied"], t1 + 1)
                    if past(t1, 2):
                        pe.wait_ge(s["h_stored"], t1 - 1)
                    for j in range(HB):
                        ins = mm(bank[2 + 2 * u1 + j][:, :], w1[:, j * P:(j + 1) * P], agg_t(u1))
                    ins.then_inc(s["hpre_ready"], 1)
            over(pe, T, 1, agg)

            def layer2(t, u, k):
                if inside(t, T):
                    pe.wait_ge(s["relu_ready"], t + 1)
                    if past(t, 2):
                        pe.wait_ge(s["o_stored"], t - 1)
                    for j in range(HB):
                        ins = mm(bank[u][:, :], w2[:, j, :], h_r(u, j), j == 0, j == HB - 1)
                    ins.then_inc(s["w2_done"], 1)
            over(pe, T, 0, layer2)

            def norm(r):
                def body(t, u, k):
                    if inside(t, T):
                        pe.wait_ge(s["v" + r], t + 1)
                        if past(t, 2):
                            pe.wait_ge(s["ln" + r], t - 1)
                        mm(bank[u][:, :], cent[:, :], v_r(u)).then_inc(s["cen" + r], 1)
                    old = older(t, u, k, 1, T)
                    if old:
                        t1, u1, _ = old
                        pe.wait_ge(s["sq" + r], t1 + 1)
                        if past(t1, 2):
                            pe.wait_ge(s["lg" + r], t1 - 1)
                        mm(bank[2 + u1][:, :], mean1[:, :], sq_r(u1)).then_inc(s["var" + r], 1)
                over(pe, T, 1, body)
            pe.wait_ge(s["o_stored"], T)
            norm("1")

            def gcn(t, u, k):
                old = older(t, u, k, 3, T)
                if old:
                    t3, u3, _ = old
                    pe.wait_ge(s["y1_copied"], t3 + 1)
                    if past(t3, 2):
                        pe.wait_ge(s["z1_copied"], t3 - 1)
                    for b in range(PAIR):
                        for m in range(NB):
                            ins = mm(bank[6 + u3][:, b * N:(b + 1) * N],
                                     ring[:, 14 + u3, (b * NB + m) * P:(b * NB + m + 1) * P], adjt[:, m, :],
                                     m == 0, m == NB - 1)
                    ins.then_inc(s["z1_done"], 1)
                old = older(t, u, k, 2, T)
                if old:
                    t2, u2, _ = old
                    pe.wait_ge(s["z0_copied"], t2 + 1)
                    if past(t2, 2):
                        pe.wait_ge(s["y1_copied"], t2 - 1)
                    for q in range(4):
                        ins = mm(bank[4 + u2][:, q * P:(q + 1) * P], ring[:, 12 + u2, q * P:(q + 1) * P], wg[:, 1, :])
                    ins.then_inc(s["y1_done"], 1)
                old = older(t, u, k, 1, T)
                if old:
                    t1, u1, _ = old
                    pe.wait_ge(s["y0_copied"], t1 + 1)
                    if past(t1, 2):
                        pe.wait_ge(s["z0_copied"], t1 - 1)
                    for b in range(PAIR):
                        for m in range(NB):
                            ins = mm(bank[2 + u1][:, b * N:(b + 1) * N],
                                     ring[:, 10 + u1, (b * NB + m) * P:(b * NB + m + 1) * P], adjt[:, m, :],
                                     m == 0, m == NB - 1)
                    ins.then_inc(s["z0_done"], 1)
                if inside(t, T):
                    pe.wait_ge(s["xs_g"], t + 1)
                    if past(t, 2):
                        pe.wait_ge(s["y0_copied"], t - 1)
                    for q in range(4):
                        ins = mm(bank[u][:, q * P:(q + 1) * P], xs_r(u)[:, q * P:(q + 1) * P], wg[:, 0, :])
                    ins.then_inc(s["y0_done"], 1)
            pe.wait_ge(s["ln1"], T)
            over(pe, T, 3, gcn)

            def lstm(p, i, chunks, width, base, _):
                order = (0, 2, 3) if i == 0 else (0, 2, 1, 3)

                def body(c, u, k):
                    if p == 1:
                        pe.wait_ge(s["z1_copied"], c + 1)
                    elif i == 0 and p == 3:
                        pe.wait_ge(s["h_done"], c + (base - chunks + 1))
                    elif i == 0:
                        pe.wait_ge(s["h_done"], c * 2 + (base - 2 * chunks + 2))
                    if i:
                        pe.wait_ge(s["h_done"], c + (base - chunks + 1))
                    if past(c, 2) or base:
                        pe.wait_ge(s["gates_read"], c + (base - 1))
                    for g in order:
                        o = shaped(bank[2 * g + u][:, :], p, width)
                        ins = mm(o, wih[:, p - 1, g * D:(g + 1) * D], win(p, i, c), True, i == 0)
                        if i:
                            ins = mm(bank[2 * g + u][:, 0:width], whh[:, p - 1, g * D:(g + 1) * D],
                                     HST[:, cols(c, width)], False, True)
                    ins.then_inc(s["gates_ready"], 1)
                over(pe, chunks, 0, body)
            pe.wait_ge(s["z1_copied"], T)
            for loop in LOOPS:
                lstm(*loop)
            pe.wait_ge(s["gates_read"], n_item)
            norm("2")

            def attend(t, u, k):
                if inside(t, T):
                    pe.wait_ge(s["xs_a"], t + 1)
                    if past(t, 1):
                        pe.wait_ge(s["q_c"], t)
                        pe.wait_ge(s["k_c"], t)
                        pe.wait_ge(s["v_c"], t)
                    mm(bank[0][:, :], wqkv[:, 0:D], xs_r(u))
                    mm(bank[1][:, :], wqkv[:, D:2 * D], xs_r(u))
                    for q in range(4):
                        ins = mm(bank[2][:, q * P:(q + 1) * P], xs_r(u)[:, q * P:(q + 1) * P], wqkv[:, 2 * D:3 * D])
                    ins.then_inc(s["qkv"], 1)
                    pe.wait_ge(s["q_c"], t + 1)
                    pe.wait_ge(s["k_c"], t + 1)
                    pe.wait_ge(s["v_c"], t + 1)
                for j in range(8):
                    w = unit(t, u, j, 0, T)
                    if w:
                        t0, u0, j0 = w
                        b, r, hp = j0 // 4, j0 // 2 % 2, j0 % 2
                        if j0 >= 2 or past(t0, 1):
                            pe.wait_ge(s["ex"], 8 * t0 + (j0 - 1))
                        o = bank[3 + j0 % 2]
                        mm(o[:, :], identb[:, :], mbias[:, r].rearrange("p a n -> p (a n)"), True, False)
                        for h in range(2):
                            ins = mm(o[:, h * N:(h + 1) * N], qm(u0, 2 * hp + h)[:, b * N + r * P:b * N + (r + 1) * P],
                                     kr(u0)[:, b * N:(b + 1) * N], False, h == 1)
                        ins.then_inc(s["s_done"], 1)
                    w = unit(t, u, j, 2, T)
                    if w:
                        t2, u2, j2 = w
                        pe.wait_ge(s["nrm"], 8 * t2 + (j2 + 1))
                        if j2 >= 2 or past(t2, 1):
                            pe.wait_ge(s["tp_c"], 8 * t2 + (j2 - 1))
                        for q in range(4):
                            ins = pe.transpose(bank[5 + j2 % 2][:, q * P:(q + 1) * P],
                                               pr(j2 % 2)[:, q * P:(q + 1) * P], ident[:, :])
                        ins.then_inc(s["tp"], 1)
                    w = unit(t, u, j, 3, T)
                    if w:
                        t3, u3, j3 = w
                        b, r, hp = j3 // 4, j3 // 2 % 2, j3 % 2
                        pe.wait_ge(s["tp_c"], 8 * t3 + (j3 + 1))
                        if j3 == 0 and past(t3, 1):
                            pe.wait_ge(s["av_c"], t3)
                        for h in range(2):
                            c = DH * (2 * hp + h)
                            for m in range(NB):
                                ins = mm(bank[7][c:c + DH, b * N + r * P:b * N + (r + 1) * P],
                                         vr(u3)[:, (b * NB + m) * D + c:(b * NB + m) * D + c + DH],
                                         pt(j3 % 2)[:, (h * NB + m) * P:(h * NB + m + 1) * P], m == 0, m == NB - 1)
                        ins.then_inc(s["av"], 1)
            pe.wait_ge(s["ln2"], T)
            over(pe, T, 1, attend, 2)
            pe.wait_ge(s["tp_c"], 8 * T)
            norm("3")

            def edges(t, u, k):
                if inside(t, T):
                    pe.wait_ge(s["xs_e"], t + 1)
                    if past(t, 1):
                        pe.wait_ge(s["xq_c"], t)
                        pe.wait_ge(s["xv_c"], t)
                    for q in range(4):
                        mm(bank[0][:, q * P:(q + 1) * P], xs_r(u)[:, q * P:(q + 1) * P], wlin[:, :])
                    for q in range(4):
                        ins = mm(bank[1][:, q * P:(q + 1) * P], xs_r(u)[:, q * P:(q + 1) * P], wval[:, :])
                    ins.then_inc(s["xqv"], 1)
                    pe.wait_ge(s["xq_c"], t + 1)
                    if past(t, 1):
                        pe.wait_ge(s["lr"], t)
                    for b in range(PAIR):
                        for m in range(NB):
                            ins = mm(bank[4][:, b * E:(b + 1) * E], ring[:, 10, (b * NB + m) * P:(b * NB + m + 1) * P],
                                     sum1[:, m, :], m == 0, m == NB - 1)
                    ins.then_inc(s["z_done"], 1)
                    pe.wait_ge(s["lr"], t + 1)
                    if past(t, 1):
                        pe.wait_ge(s["e_c"], t)
                    for e in range(EB):
                        for b in range(PAIR):
                            c = (e * PAIR + b) * HEADS
                            ins = mm(bank[5][:, c:c + HEADS], ring[:, 12, b * E + e * P:b * E + (e + 1) * P], abd[:, :])
                    ins.then_inc(s["e_done"], 1)
            pe.wait_ge(s["ln3"], T)
            over(pe, T, 0, edges)
            pe.wait_ge(s["e_c"], T)
            for e in range(EB):
                ins = pe.transpose(bank[0][:, e * P:(e + 1) * P], ET[:, e, :], ident[:, :])
            ins.then_inc(s["tr_e"], 1)
            pe.wait_ge(s["att"], 1)
            for e in range(EB):
                ins = pe.transpose(bank[1][:, e * P:(e + 1) * P], sm[:, 3, e * P:(e + 1) * P], ident[:, :])
            ins.then_inc(s["tr_a"], 1)
            pe.wait_ge(s["at_c"], 1)

            def rows(t, u, k):
                if inside(t, T):
                    if past(t, 1):
                        pe.wait_ge(s["vt_c"], t)
                    v = VV[:, cols(t, W)].rearrange("p (b m f) -> p b m f", b=PAIR, m=NB)
                    for e in range(EB):
                        for m in range(NB):
                            ins = mm(bank[2][:, e * 256:(e + 1) * 256].rearrange("p (b f) -> p b f", b=PAIR),
                                     dst1[:, m, e * P:(e + 1) * P], v[:, :, m, :], m == 0, m == NB - 1)
                    ins.then_inc(s["vt"], 1)
                    pe.wait_ge(s["vt_c"], t + 1)
                    if past(t, 1):
                        pe.wait_ge(s["yt_c"], t)
                    for b in range(PAIR):
                        for e in range(EB):
                            ins = mm(bank[4][:, b * N:(b + 1) * N],
                                     ring[:, 12, (e * PAIR + b) * P:(e * PAIR + b + 1) * P], src1[:, e, :],
                                     e == 0, e == EB - 1)
                    ins.then_inc(s["yt"], 1)
                    pe.wait_ge(s["yt_c"], t + 1)
                    pe.wait_ge(s["xs_o"], t + 1)
                    if past(t, 2):
                        pe.wait_ge(s["o_fin"], t - 1)
                    for q in range(4):
                        mm(bank[6 + u][:, q * P:(q + 1) * P], xs_r(u)[:, q * P:(q + 1) * P], ident[:, :], True, False)
                        ins = mm(bank[6 + u][:, q * P:(q + 1) * P], ring[:, 13, q * P:(q + 1) * P], wout[:, :], False, True)
                    ins.then_inc(s["o_pe"], 1)
            over(pe, T, 0, rows)

    return nc


def kernel(**inputs):
    import numpy as np
    import concourse.bacc as bacc
    from concourse.bass_utils import run_bass_kernel_spmd

    a = {k: np.asarray(v) for k, v in inputs.items()}
    x = a["x"]
    laid = {
        "x_tok": x,
        "x_feat": x.transpose(2, 0, 1).reshape(x.shape[2], -1),
        "adj": a["adj"],
        "adj_t": a["adj"].T,
        "w1_t": a["L0_gnn_W1"].T, "w2_t": a["L0_gnn_W2"].T,
        "cols1": np.stack([a["L0_gnn_b1"], a["L0_gnn_g1"], a["L0_gnn_be1"]]).reshape(3, -1, P).transpose(2, 0, 1),
        "cols2": np.stack([a["L0_gnn_b2"], a["L0_gnn_g2"], a["L0_gnn_be2"]]).T,
        "wg0": a["L1_gnn_Wg0"], "bg0": a["L1_gnn_bg0"], "wg1": a["L1_gnn_Wg1"], "bg1": a["L1_gnn_bg1"],
        "wih_t": a["L1_gnn_Wih"].transpose(0, 2, 1), "whh_t": a["L1_gnn_Whh"].transpose(0, 2, 1),
        "bih": a["L1_gnn_bih"].reshape(4, 4, P).transpose(2, 0, 1),
        "bhh": a["L1_gnn_bhh"].reshape(4, 4, P).transpose(2, 0, 1),
        "w_qkv": a["L2_gnn_W"],
        "w_lin_t": a["L3_gnn_W_lin"].T, "w_val_t": a["L3_gnn_W_val"].T, "a": a["L3_gnn_a"],
        "w_out_t": a["L3_gnn_W_out"].T, "src": a["L3_gnn_src"], "dst": a["L3_gnn_dst"],
        "edge_cols": np.stack([a["L3_gnn_src"], a["L3_gnn_dst"]]).reshape(2, -1, P).transpose(2, 0, 1),
    }
    nc = bacc.Bacc("TRN2", target_bir_lowering=False, num_devices=1)
    arrays, aps = {}, {}
    for name, v in laid.items():
        arrays["in_" + name] = np.ascontiguousarray(v)
        aps[name] = nc.dram_tensor("in_" + name, v.shape, mybir.dt.from_np(v.dtype), kind="ExternalInput").ap()
    aps["out"] = nc.dram_tensor("out_x", x.shape, F32, kind="ExternalOutput").ap()
    build_program(nc, **aps)
    r = run_bass_kernel_spmd(nc, [arrays], core_ids=[0])
    return r.results[0]["out_x"]
```

```python
from contextlib import ExitStack

import concourse.bass as bass
from concourse import mybir

F32 = mybir.dt.float32
F32R = mybir.dt.float32r
BF16 = mybir.dt.bfloat16
I32 = mybir.dt.int32
ALU = mybir.AluOpType
ACT = mybir.ActivationFunctionType
AX_X = mybir.AxisListType.X

P = 128
EPS = 1e-5
LOG_EPS = 1e-8
NEG = -1e30
PAIR = 2
SLOPE = 0.2


def past(t, k):
    return not isinstance(t, int) or t >= k


def over(eng, total, lag, body, ahead=None, unroll=2):
    ahead = ahead or -(-(lag + 2) // unroll) * unroll
    for t in range(ahead):
        body(t, t % unroll, t // unroll)
    with eng.Fori(ahead // unroll, total // unroll) as k:
        for u in range(unroll):
            body(k * unroll + u, u, k)
    for t in range(total, total + lag):
        body(t, t % unroll, t // unroll)


def inside(t, total):
    return not isinstance(t, int) or 0 <= t < total


def older(t, u, k, lag, total, unroll=2):
    if isinstance(t, int):
        if not 0 <= t - lag < total:
            return None
        return t - lag, (t - lag) % unroll, (t - lag) // unroll
    return t - lag, (u - lag) % unroll, k + (u - lag) // unroll


def cols(t, n):
    return slice(t * n, (t + 1) * n) if isinstance(t, int) else bass.ds(t * n, n)


def build_program(nc, x_tok, x_feat, adj, adj_t, w1_t, w2_t, cols1, cols2, wg0, bg0, wg1, bg1,
                  wih_t, whh_t, bih, bhh, w_qkv, w_lin_t, w_val_t, a, w_out_t, src, dst, edge_cols, out):
    B, N, D = x_tok.shape
    H1 = w1_t.shape[1]
    HB = H1 // P
    NB = N // P
    TOK = B * N
    T = B // PAIR
    W = PAIR * N
    STEPS = wih_t.shape[0]
    HEADS, DH = a.shape
    E = src.shape[0]
    EB = E // P
    assert D == P and W == 512 and HEADS * DH == P and B * HEADS == P and E == N

    with ExitStack() as ctx:
        def sb(name, shape, dt=F32):
            return ctx.enter_context(nc.sbuf_tensor(name, shape, dt))

        def sem(name):
            return ctx.enter_context(nc.semaphore(name))

        bank = [ctx.enter_context(nc.psum_tensor(f"bank{i}", [P, 512], F32)) for i in range(8)]

        X = sb("X", [P, TOK])
        HL = sb("HL", [P, TOK])
        VV = HL

        w1 = sb("w1", [P, H1])
        w2 = sb("w2", [P, HB, D])
        wg = sb("wg", [P, 2, D])
        bgb = sb("bgb", [P, 2, 1, D])
        wih = sb("wih", [P, STEPS, 4 * D])
        whh = sb("whh", [P, STEPS, 4 * D])
        bi = sb("bi", [P, STEPS, 4])
        bh = sb("bh", [P, STEPS, 4])
        bl = sb("bl", [P, STEPS, 4])
        wqkv = sb("wqkv", [P, 3 * D])
        wlin = sb("wlin", [P, D])
        wval = sb("wval", [P, D])
        wout = sb("wout", [P, D])
        abd = sb("abd", [P, HEADS])
        col1 = sb("col1", [P, 3, HB])
        col2 = sb("col2", [P, 3])
        adjs = sb("adjs", [P, NB, N])
        adjt = sb("adjt", [P, NB, N])
        aht = sb("aht", [P, NB, N])
        ident = sb("ident", [P, P])
        identb = sb("identb", [P, P], BF16)
        cent = sb("cent", [P, P])
        mean1 = sb("mean1", [P, P])
        ones = sb("ones", [P, P])
        mbias = sb("mbias", [P, NB, 2, N], BF16)
        cst = sb("cst", [P, 4])
        deg = sb("deg", [P, 8])
        dinv = sb("dinv", [P, NB])
        ttr = sb("ttr", [P, N])

        ring = sb("ring", [P, 16, 512])
        st1 = sb("st1", [P, HB, T * 6])
        st2 = sb("st2", [P, T * 6])
        bn = sb("bn", [P, 3, 8])

        eci = sb("eci", [P, 2, EB], I32)
        ec = sb("ec", [P, 2, EB])
        iof = sb("iof", [P, E])
        ioi = sb("ioi", [P, E], I32)
        ioc = sb("ioc", [P, EB])
        ioci = sb("ioci", [P, EB], I32)
        keyc = sb("keyc", [P, EB])
        rank = sb("rank", [P, EB])
        scol = sb("scol", [P, 2, EB])
        dst1 = sb("dst1", [P, NB, E])
        sum1 = sb("sum1", [P, NB, E])
        src1 = sb("src1", [P, EB, N])
        early = lambda i: ring[:, 8 + i, :].rearrange("p (a e) -> p a e", a=2)
        ei = early(0).bitcast(I32)
        er, perm, srow, srct, dstc = (early(i) for i in range(1, 6))
        keyr = ring[:, 15, 0:E]
        bc = ring[:, 14, :].rearrange("p (j e c) -> p j e c", j=2, e=EB)
        lacol = sb("lacol", [P, 4])
        larow = sb("larow", [P, E])
        srk = sb("srk", [P, E])
        same = ring[:, 2:5, :].rearrange("p a (b e) -> p (a b) e", b=2)
        ET = aht[:, 0, :].rearrange("p (e c) -> p e c", e=EB)
        AT = aht[:, 1, :].rearrange("p (e c) -> p e c", e=EB)
        den = sb("den", [P, 8, 6])
        dgs = sb("dgs", [P, 2, P])
        bst = sb("bst", [P, 2, 4, 6])
        mv = sb("mv", [P, 2, 4, 2])
        fin = sb("fin", [P, 2, 12])

        with ExitStack() as first:
            H1B = first.enter_context(nc.sbuf_tensor("H1B", [P, TOK], F32))
            O = first.enter_context(nc.sbuf_tensor("O", [P, TOK], F32))
        HID = (HL, H1B)
        CELL = H1B[:, :]
        HST = H1B[:, TOK // 2:TOK]
        stk = sb("stk", [P, 2, 2, HEADS, 512], F32R)
        spl = sb("spl", [P, 2, 4, 512], F32R)

        names = ["in_adj", "in_w1", "in_w2", "in_x", "in_w", "in_e", "pool_c", "setup_pe", "dch", "ach", "xa0", "xa1",
                 "agg_ready", "agg_copied", "hpre_ready", "h_stored", "stat1", "bn1", "relu_ready", "w2_done",
                 "o_stored", "stat2", "bn2", "tmp_ready"]
        for r in "123":
            names += [f"v{r}", f"cen{r}", f"sq{r}", f"var{r}", f"lg{r}", f"rs{r}", f"ln{r}"]
        names += ["xs_g", "y0_done", "y0_copied", "z0_done", "z0_copied", "y1_done", "y1_copied", "z1_done",
                  "z1_copied", "gates_ready", "gates_read", "prod", "c_done", "tc_ready", "h_done"]
        names += ["xs_a", "q_pe", "k_pe", "v_pe", "q_hi", "k_hi", "q_lo", "k_lo", "v_c", "stk00", "stk01", "stk10", "stk11", "s_done",
                  "mx", "ex", "tp", "tp_c", "av", "rc", "nrm", "av_c"]
        names += ["xs_e", "xqv", "xq_c", "xv_c", "z_done", "z_c", "lr", "e_done", "e_c",
                  "tr_e", "sm_e", "exd", "att", "tr_a", "at_c",
                  "xs_o", "vt", "vt_c", "yt", "yt_c", "o_pe", "bs", "nm", "aggr_on", "st3", "lgo", "rso", "o_fin", "out0", "out1"]
        s = {n: sem(n) for n in names}
        block = ctx.enter_context(nc.Block())

        sm = ring[:, 0:2, :].rearrange("p a (b e) -> p (a b) e", b=2)
        agg_t = lambda u: ring[:, u, :]
        h_r = lambda u, j: ring[:, 2 + 2 * u + j, :]
        x_r = lambda u: ring[:, 6 + u, :].rearrange("p (b m f) -> p b m f", b=PAIR, m=NB)
        rows4 = lambda v: v.rearrange("p (q f) -> p q f", q=4)
        v_r = lambda u: ring[:, u, :]
        sq_r = lambda u: ring[:, 4 + u, :]
        xs_r = lambda u: ring[:, 8 + u, :]

        pr = lambda j: ring[:, j % 4, :]
        pt = lambda j: ring[:, 4 + j % 4, :]
        vr = lambda u: ring[:, 10 + u, :]

        Q_AT, K_AT, V_AT, OUT_AT, V_COPY_AT = 0, 1, 3, 5, 6
        EXP_LAG, NORM_LAG, TURN_LAG, TURN_COPY_LAG, AV_LAG = 1, 2, 3, 3, 5

        def unit(t, u, j, lag, total):
            back = 1 if j >= lag else 2
            if isinstance(t, int) and not 0 <= t - back < total:
                return None
            return t - back, (u - back) % 2, (j - lag) % 8

        def win(p, i, c):
            if p == 1:
                return HL[:, cols(c, 512)]
            if p == 3:
                v = HL[:, cols(c, 4 * N)].rearrange("f (b w) -> f b w", b=4)
                return v[:, :, i:3 * (N // 3):3]
            return HL[:, cols(c, 512 * p)].rearrange("f (w p) -> f w p", p=p)[:, :, i]

        LOOPS = []
        n_item = n_prod = 0
        for p in range(1, STEPS + 1):
            chunks = {1: TOK // 512, 2: TOK // 1024, 3: B // 4, 4: TOK // 2048}[p]
            width = 4 * (N // 3) if p == 3 else 512
            for i in range(p):
                LOOPS.append((p, i, chunks, width, n_item, n_prod))
                n_item += chunks
                n_prod += chunks if i else 0

        def shaped(ap, p, width):
            ap = ap[:, 0:width]
            return ap.rearrange("f (b w) -> f b w", b=4) if p == 3 else ap

        N_E = 16 * (9 + HEADS)
        pool_steps = 0

        @block.sync
        def _(sp):
            for d, v in ((adjs[:, :, :], adj.rearrange("(b p) m -> p b m", p=P)),
                         (adjt[:, :, :], adj_t.rearrange("(b p) m -> p b m", p=P))):
                sp.dma_start(d, v).then_inc(s["in_adj"], 16)
            sp.dma_start(w1[:, :], w1_t).then_inc(s["in_w1"], 16)


            def load(t, u, k):
                if past(t, 2):
                    sp.wait_ge(s["agg_ready"], t - 1)
                src_ap = x_tok[t * PAIR:(t + 1) * PAIR] if isinstance(t, int) else x_tok[bass.ds(t * PAIR, PAIR)]
                for b in range(PAIR):
                    sp.dma_start(x_r(u)[:, b], src_ap[b].rearrange("(m p) f -> p m f", p=P)).then_inc(s[f"xa{u}"], 16)
            over(sp, T, 0, load)
            for d, v in ((w2[:, :, :], w2_t.rearrange("(b p) m -> p b m", p=P)),
                         (wg[:, 0, :], wg0), (wg[:, 1, :], wg1)):
                sp.dma_start(d, v).then_inc(s["in_w2"], 16)
            for c in range(4):
                sp.dma_start(X[:, c * TOK // 4:(c + 1) * TOK // 4],
                             x_feat[:, c * TOK // 4:(c + 1) * TOK // 4]).then_inc(s["in_x"], 16)
            for d, v in ((wih[:, :, :], wih_t.rearrange("s p g -> p s g")),
                         (whh[:, :, :], whh_t.rearrange("s p g -> p s g")),
                         (wqkv[:, :], w_qkv), (wlin[:, :], w_lin_t), (wval[:, :], w_val_t), (wout[:, :], w_out_t)):
                sp.dma_start(d, v).then_inc(s["in_w"], 16)

            def stack(t, u, k):
                for name in ("q_hi", "k_hi", "q_lo", "k_lo"):
                    sp.wait_ge(s[name], t + 1)
                for h in range(HEADS):
                    if h % 2 == 0 and past(t, 2):
                        sp.wait_ge(s["s_done"], 8 * t + (4 * (h // 2) - 12))
                    for r, (q, w) in enumerate(((0, 2), (0, 3), (1, 2), (1, 3))):
                        sp.dma_start(stk[r * DH:(r + 1) * DH, u, :, h, :].bitcast(F32),
                                     spl[h * DH:(h + 1) * DH, u, q:w + 1:w - q, :].bitcast(F32))\
                            .then_inc(s[f"stk{h // 2}{u}"], 16)
            over(sp, T, 0, stack)

            def store(t, u, k):
                sp.wait_ge(s["o_fin"], t + 1)
                dst_ap = out[t * PAIR:(t + 1) * PAIR] if isinstance(t, int) else out[bass.ds(t * PAIR, PAIR)]
                for b in range(PAIR):
                    sp.dma_start(dst_ap[b].rearrange("(m p) f -> p m f", p=P),
                                 ring[:, 14 + u, :].rearrange("p (b m f) -> p b m f", b=PAIR, m=NB)[:, b])\
                        .then_inc(s[f"out{u}"], 16)
            over(sp, T, 0, store)
            for u in range(2):
                sp.wait_ge(s[f"out{u}"], 16 * PAIR * T // 2)

        @block.gpsimd
        def _(pool):
            nonlocal pool_steps
            n = 0

            def made(ins):
                nonlocal n
                n += 1
                ins.then_inc(s["pool_c"], 1)
                pool.wait_ge(s["pool_c"], n)

            for d, v in ((col1[:, :, :], cols1), (col2[:, :], cols2), (bi[:, :, :], bih), (bh[:, :, :], bhh),
                         (eci[:, :, :], edge_cols)):
                pool.dma_start(d, v).then_inc(s["in_e"], 16)
            for j, v in enumerate((bg0, bg1)):
                pool.dma_start(bgb[:, j, 0, :], v.rearrange("(a f) -> a f", a=1).to_broadcast([P, D]))\
                    .then_inc(s["in_e"], 16)
            for j, v in enumerate((src, dst)):
                pool.dma_start(ei[:, j, :], v.rearrange("(a f) -> a f", a=1).to_broadcast([P, E]))\
                    .then_inc(s["in_e"], 16)
            made(pool.memset(abd[:, :], 0.0))
            for h in range(HEADS):
                pool.dma_start(abd[h * DH:(h + 1) * DH, h:h + 1], a[h].rearrange("(p o) -> p o", o=1))\
                    .then_inc(s["in_e"], 16)
            made(pool.memset(ident[:, :], 0.0))
            made(pool.affine_select(out=ident[:, :], in_=ident[:, :], compare_op=ALU.not_equal, fill=1.0, base=0,
                                    pattern=[[-1, P]], channel_multiplier=1))
            made(pool.memset(ones[:, :], 1.0))
            made(pool.memset(mean1[:, :], 1.0 / D))
            made(pool.memset(cst[:, 0:1], EPS))
            made(pool.memset(cst[:, 1:2], LOG_EPS))
            made(pool.iota(ioi[:, :], pattern=[[1, E]], base=0, channel_multiplier=0))
            made(pool.iota(ioci[:, :], pattern=[[P, EB]], base=0, channel_multiplier=1))
            pool_steps = n

            def copies(ln, slot_free, ready):
                def body(t, u, k):
                    pool.wait_ge(s[ln], t + 1)
                    if past(t, 2):
                        pool.wait_ge(s[slot_free], t - 1)
                    pool.tensor_copy(xs_r(u), X[:, cols(t, W)]).then_inc(s[ready], 1)
                over(pool, T, 0, body)
            copies("ln1", "y0_done", "xs_g")
            copies("ln2", "v_pe", "xs_a")
            copies("ln3", "xqv", "xs_e")
            pool.wait_ge(s["xqv"], T)
            copies("ln3", "o_pe", "xs_o")


        at = {}

        @block.vector
        def _(dve):
            n = 0

            def link(ins, name=None):
                nonlocal n
                n += 1
                ins.then_inc(s["dch"], 1)
                dve.wait_ge(s["dch"], n)
                if name:
                    at[name] = n

            dve.wait_ge(s["in_adj"], 32)
            dve.wait_ge(s["in_e"], N_E)
            dve.wait_ge(s["pool_c"], pool_steps)

            link(dve.tensor_reduce(deg[:, 0:2], adjs[:, :, :], AX_X, ALU.add))
            link(dve.tensor_reduce(deg[:, 2:4], adjt[:, :, :], AX_X, ALU.add))
            for m in range(NB):
                link(dve.tensor_tensor_reduce(ttr[:, 0:P], adjs[:, m, m * P:(m + 1) * P], ident[:, :], 1.0, 0.0,
                                              ALU.mult, ALU.add, deg[:, 4 + m:5 + m]))
            link(dve.tensor_tensor(deg[:, 0:2], deg[:, 0:2], deg[:, 2:4], ALU.add))
            link(dve.tensor_tensor(deg[:, 0:2], deg[:, 0:2], deg[:, 4:6], ALU.subtract))
            link(dve.tensor_scalar(deg[:, 4:6], deg[:, 0:2], 1.0, None, ALU.add), "deg")
            dve.wait_ge(s["ach"], 1)
            link(dve.reciprocal(dinv[:, :], deg[:, 6:8]))
            for m in range(NB):
                link(dve.tensor_scalar(dgs[:, m, :], ident[:, :], dinv[:, m:m + 1], None, ALU.mult), "diag")
            for m in range(NB):
                link(dve.tensor_copy(aht[:, m, :], adjt[:, m, :]))
                link(dve.tensor_tensor(aht[:, m, m * P:(m + 1) * P], adjt[:, m, m * P:(m + 1) * P], ident[:, :],
                                       ALU.add))
            dve.wait_ge(s["setup_pe"], 1)
            for m in range(NB):
                link(dve.scalar_tensor_tensor(aht[:, m, :], aht[:, m, :], dinv[:, m:m + 1], bank[7][:, 0:N],
                                              ALU.mult, ALU.mult), "aht")

            for m in range(NB):
                for h in range(2):
                    link(dve.tensor_scalar(mbias[:, m, h, :], adjs[:, m, :], 0.0, NEG, ALU.is_equal, ALU.mult))
            link(dve.tensor_copy(identb[:, :], ident[:, :]))
            link(dve.tensor_tensor(cent[:, :], ident[:, :], mean1[:, :], ALU.subtract))
            link(dve.tensor_tensor(bl[:, :, :], bi[:, :, :], bh[:, :, :], ALU.add))

            for j in range(2):
                link(dve.tensor_copy(er[:, j, :], ei[:, j, :]))
                link(dve.tensor_copy(ec[:, j, :], eci[:, j, :]))
            link(dve.tensor_copy(iof[:, :], ioi[:, :]))
            link(dve.tensor_copy(ioc[:, :], ioci[:, :]))
            link(dve.scalar_tensor_tensor(keyr[:, :], er[:, 0, :], float(E), iof[:, :], ALU.mult, ALU.add))
            link(dve.scalar_tensor_tensor(keyc[:, :], ec[:, 0, :], float(E), ioc[:, :], ALU.mult, ALU.add))
            for e in range(EB):
                link(dve.tensor_scalar(ttr[:, :], keyr[:, :], keyc[:, e:e + 1], None, ALU.is_lt, ALU.add,
                                       accum_out=rank[:, e:e + 1]))
                link(dve.tensor_scalar(perm[:, e, :], iof[:, :], rank[:, e:e + 1], None, ALU.is_equal))
                for j in range(2):
                    link(dve.tensor_scalar(bc[:, j, e, :], ones[:, :], ec[:, j, e:e + 1], None, ALU.mult), "perm")
            def stats1(t, u, k):
                dve.wait_ge(s["h_stored"], t + 1)
                for j in range(HB):
                    ins = dve.bn_stats(st1[:, j, cols(t, 6)], HID[j][:, cols(t, W)])
                ins.then_inc(s["stat1"], 1)
            over(dve, T, 0, stats1)
            dve.wait_ge(s["stat1"], T)
            for j in range(HB):
                ins = dve.bn_aggr(bn[:, j, 0:2], st1[:, j, :])
            ins.then_inc(s["stat1"], 1)
            dve.wait_ge(s["ach"], 2)
            link(dve.reciprocal(bn[:, 0:2, 3], bn[:, 0:2, 2]))
            link(dve.tensor_tensor(bn[:, 0:2, 4], bn[:, 0:2, 3], col1[:, 1, :], ALU.mult))
            link(dve.tensor_tensor(bn[:, 0:2, 6], bn[:, 0:2, 0], bn[:, 0:2, 4], ALU.mult))
            dve.tensor_tensor(bn[:, 0:2, 5], col1[:, 2, :], bn[:, 0:2, 6], ALU.subtract).then_inc(s["bn1"], 1)

            dve.wait_ge(s["setup_pe"], 2)
            for j in range(2):
                link(dve.tensor_copy(srow[:, j, :], bank[6][:, j * E:(j + 1) * E]))
                link(dve.tensor_copy(scol[:, j, :], bank[7][:, j * EB:(j + 1) * EB]))
            for m in range(NB):
                link(dve.tensor_scalar(srct[:, m, :], srow[:, 0, :], ioc[:, m:m + 1], None, ALU.is_equal))
                link(dve.tensor_scalar(dst1[:, m, :], srow[:, 1, :], ioc[:, m:m + 1], None, ALU.is_equal))
                link(dve.tensor_tensor(sum1[:, m, :], srct[:, m, :], dst1[:, m, :], ALU.add), "srct")
            for e in range(EB):
                link(dve.tensor_scalar(src1[:, e, :], iof[:, :], scol[:, 0, e:e + 1], None, ALU.is_equal))
                link(dve.tensor_scalar(dstc[:, e, :], iof[:, :], scol[:, 1, e:e + 1], None, ALU.is_equal))
            link(dve.tensor_copy(srk[:, :], srow[:, 0, :]))

            def stats2(t, u, k):
                dve.wait_ge(s["o_stored"], t + 1)
                dve.bn_stats(st2[:, cols(t, 6)], O[:, cols(t, W)]).then_inc(s["stat2"], 1)
            over(dve, T, 0, stats2)
            dve.wait_ge(s["stat2"], T)
            dve.bn_aggr(bn[:, 2, 0:2], st2[:, :]).then_inc(s["stat2"], 1)
            dve.wait_ge(s["ach"], 3)
            link(dve.reciprocal(bn[:, 2, 3:4], bn[:, 2, 2:3]))
            link(dve.tensor_tensor(bn[:, 2, 4:5], bn[:, 2, 3:4], col2[:, 1:2], ALU.mult))
            link(dve.tensor_tensor(bn[:, 2, 6:7], bn[:, 2, 0:1], bn[:, 2, 4:5], ALU.mult))
            link(dve.tensor_tensor(bn[:, 2, 5:6], col2[:, 2:3], bn[:, 2, 6:7], ALU.subtract))

            def norm(r, add):
                def body(t, u, k):
                    if inside(t, T):
                        if past(t, 4):
                            dve.wait_ge(s["cen" + r], t - 3)
                        add(t, u).then_inc(s["v" + r], 1)
                    old = older(t, u, k, 2, T, 4)
                    if old:
                        t2, u2, _ = old
                        dve.wait_ge(s["rs" + r], t2 + 1)
                        dve.tensor_tensor(X[:, cols(t2, W)], bank[u2][:, :], sq_r(u2), ALU.mult)\
                            .then_inc(s["ln" + r], 1)
                over(dve, T, 2, body, unroll=4)

            def add1(t, u):
                dve.tensor_scalar(v_r(u), O[:, cols(t, W)], bn[:, 2, 4:5], bn[:, 2, 5:6], ALU.mult, ALU.add)\
                    .then_inc(s["tmp_ready"], 1)
                dve.wait_ge(s["tmp_ready"], t + 1)
                return dve.tensor_tensor(v_r(u), v_r(u), X[:, cols(t, W)], ALU.add)
            dve.wait_ge(s["setup_pe"], 3)
            for e in range(EB):
                link(dve.tensor_tensor(ttr[:, :], bank[7][:, e * N:(e + 1) * N], dstc[:, e, :], ALU.mult))
                link(dve.tensor_reduce(lacol[:, e:e + 1], ttr[:, :], AX_X, ALU.add), "adje")

            dve.wait_ge(s["in_x"], 64)
            norm("1", add1)
            def gcn(t, u, k):
                old = older(t, u, k, 2, T)
                if old:
                    t2, u2, _ = old
                    dve.wait_ge(s["y1_done"], t2 + 1)
                    if past(t2, 2):
                        dve.wait_ge(s["z1_done"], t2 - 1)
                    dve.tensor_tensor(rows4(ring[:, 14 + u2, :]), rows4(bank[4 + u2][:, :]),
                                      bgb[:, 1].to_broadcast([P, 4, D]), ALU.add).then_inc(s["y1_copied"], 1)
                if inside(t, T):
                    dve.wait_ge(s["y0_done"], t + 1)
                    if past(t, 2):
                        dve.wait_ge(s["z0_done"], t - 1)
                    dve.tensor_tensor(rows4(ring[:, 10 + u, :]), rows4(bank[u][:, :]),
                                      bgb[:, 0].to_broadcast([P, 4, D]), ALU.add).then_inc(s["y0_copied"], 1)
            over(dve, T, 2, gcn)

            def lstm(p, i, chunks, width, base, base2):
                def body(c, u, k):
                    if inside(c, chunks):
                        dve.wait_ge(s["gates_read"], c + (base + 1))
                        cell = CELL[:, cols(c, width)]
                        ig, gg, fg = (ring[:, 2 * g + u, 0:width] for g in (0, 2, 1))
                        if i == 0:
                            dve.tensor_tensor(cell, ig, gg, ALU.mult).then_inc(s["c_done"], 1)
                        else:
                            dve.tensor_tensor(ring[:, 10 + u, 0:width], fg, cell, ALU.mult).then_inc(s["prod"], 1)
                            dve.tensor_tensor(ring[:, 12 + u, 0:width], ig, gg, ALU.mult).then_inc(s["prod"], 1)
                            dve.wait_ge(s["prod"], c * 2 + (2 * base2 + 2))
                            dve.tensor_tensor(cell, ring[:, 10 + u, 0:width], ring[:, 12 + u, 0:width], ALU.add)\
                                .then_inc(s["c_done"], 1)
                    old = older(c, u, k, 1, chunks)
                    if old:
                        c1, u1, _ = old
                        dve.wait_ge(s["tc_ready"], c1 + (base + 1))
                        o = win(p, i, c1) if i == p - 1 else HST[:, cols(c1, width)]
                        q = p if i == p - 1 else 1
                        dve.tensor_tensor(o, shaped(ring[:, 6 + u1, :], q, width), shaped(ring[:, 8 + u1, :], q, width),
                                          ALU.mult).then_inc(s["h_done"], 1)
                over(dve, chunks, 1, body, 2)
            for loop in LOOPS:
                lstm(*loop)
            dve.wait_ge(s["ach"], 4)
            for e in range(EB):
                link(dve.tensor_scalar(dgs[:, e, :], ident[:, :], lacol[:, 2 + e:3 + e], None, ALU.mult), "ladiag")
            dve.wait_ge(s["setup_pe"], 4)
            link(dve.tensor_copy(larow[:, :], bank[7][:, 0:E]))

            dve.wait_ge(s["h_done"], n_item)
            norm("2", lambda t, u: dve.tensor_tensor(v_r(u), X[:, cols(t, W)], HL[:, cols(t, W)], ALU.add))

            def attend(t, u, k):
                for j in range(8):
                    for at_j, pe_done, hi, lo, x, scale in ((Q_AT, "q_pe", "q_hi", "q_lo", 0, DH ** -0.5),
                                                            (K_AT, "k_pe", "k_hi", "k_lo", 1, 1.0)):
                        if j == at_j and inside(t, T):
                            dve.wait_ge(s[pe_done], t + 1)
                            dve.wait_ge(s[hi], t + 1)
                            if past(t, 2):
                                for g in range(2):
                                    dve.wait_ge(s[f"stk{g}{u}"], k * 128)
                            dve.scalar_tensor_tensor(spl[:, u, 2 * x + 1, :], bank[x][:, :], scale,
                                                     spl[:, u, 2 * x, :].bitcast(F32), ALU.mult, ALU.subtract)\
                                .then_inc(s[lo], 1)
                    w = unit(t, u, j, 0, T)
                    if w:
                        t0, _, j0 = w
                        dve.wait_ge(s["s_done"], 8 * t0 + (j0 + 1))
                        dve.tensor_reduce(den[:, j0, 0:2], bank[3 + j0 % 2][:, :].rearrange("p (h n) -> p h n", h=2),
                                          AX_X, ALU.max, negate=True).then_inc(s["mx"], 1)
                    w = unit(t, u, j, NORM_LAG, T)
                    if w:
                        t1, _, j1 = w
                        dve.wait_ge(s["ex"], 8 * t1 + (j1 + 1))
                        dve.reciprocal(den[:, j1, 4:6], den[:, j1, 2:4]).then_inc(s["rc"], 1)
                        dve.wait_ge(s["rc"], 8 * t1 + (j1 + 1))
                        for h in range(2):
                            ins = dve.tensor_scalar(pr(j1)[:, h * N:(h + 1) * N], pr(j1)[:, h * N:(h + 1) * N],
                                                    den[:, j1, 4 + h:5 + h], None, ALU.mult)
                        ins.then_inc(s["nrm"], 1)
                    if j == V_COPY_AT and inside(t, T):
                        dve.wait_ge(s["v_pe"], t + 1)
                        if past(t, 2):
                            dve.wait_ge(s["av"], 8 * (t - 1))
                        dve.tensor_copy(vr(u), bank[0][:, :]).then_inc(s["v_c"], 1)
                    if j == OUT_AT:
                        old = older(t, u, k, 2, T)
                        if old:
                            dve.wait_ge(s["av"], 8 * old[0] + 8)
                            dve.tensor_copy(HL[:, cols(old[0], W)], bank[7 - 5 * old[1]][:, :]).then_inc(s["av_c"], 1)
            over(dve, T, 2, attend, 4)
            dve.wait_ge(s["av_c"], T)
            norm("3", lambda t, u: dve.tensor_tensor(v_r(u), X[:, cols(t, W)], HL[:, cols(t, W)], ALU.add))

            def edges(t, u, k):
                if inside(t, T):
                    dve.wait_ge(s["xqv"], t + 1)
                    dve.tensor_copy(VV[:, cols(t, W)], bank[2 + u][:, :]).then_inc(s["xv_c"], 1)
                old = older(t, u, k, 1, T)
                if old:
                    t1, u1, _ = old
                    dve.wait_ge(s["z_c"], t1 + 1)
                    if past(t1, 2):
                        dve.wait_ge(s["e_done"], t1 - 1)
                    dve.tensor_tensor(ring[:, 14 + u1, :], bank[4 + u1][:, :], ring[:, 12 + u1, :], ALU.max)\
                        .then_inc(s["lr"], 1)
                old = older(t, u, k, 2, T)
                if old:
                    t2, u2, _ = old
                    dve.wait_ge(s["e_done"], t2 + 1)
                    dve.tensor_copy(ET[:, :, cols(t2, PAIR * HEADS)],
                                    bank[6 + u2][:, 0:EB * PAIR * HEADS].rearrange("p (e c) -> p e c", e=EB))\
                        .then_inc(s["e_c"], 1)
            over(dve, T, 2, edges)

            link(dve.tensor_tensor(same[:, 5, 1:E], srk[:, 1:E], srk[:, 0:E - 1], ALU.not_equal))
            for j in range(2):
                link(dve.memset(same[:, j, :], NEG))
                link(dve.memset(same[:, 2 + j, :], 0.0))
            link(dve.tensor_scalar(same[:, 0, 1:E], same[:, 5, 1:E], NEG, None, ALU.mult))
            link(dve.tensor_scalar(same[:, 1, 0:E - 1], same[:, 5, 1:E], NEG, None, ALU.mult))
            link(dve.tensor_scalar(same[:, 2, 1:E], same[:, 5, 1:E], -1.0, 1.0, ALU.mult, ALU.add))
            link(dve.tensor_scalar(same[:, 3, 0:E - 1], same[:, 5, 1:E], -1.0, 1.0, ALU.mult, ALU.add))
            link(dve.tensor_scalar(same[:, 4, :], same[:, 3, :], -1.0, 1.0, ALU.mult, ALU.add))

            def scan(o, x, y, first, op0, op1, back):
                v = (lambda z: z[:, ::-1]) if back else (lambda z: z)
                return dve.tensor_tensor_scan(v(o), v(x), v(y), first, op0, op1)
            dve.wait_ge(s["tr_e"], 1)
            link(dve.tensor_tensor(sm[:, 0, :], bank[0][:, 0:E], larow[:, :], ALU.add))
            link(scan(sm[:, 1, :], same[:, 0, :], sm[:, 0, :], NEG, ALU.add, ALU.max, False))
            link(scan(sm[:, 2, :], same[:, 1, :], sm[:, 1, :], NEG, ALU.add, ALU.max, True))
            dve.tensor_tensor(sm[:, 1, :], sm[:, 0, :], sm[:, 2, :], ALU.subtract).then_inc(s["sm_e"], 1)
            dve.wait_ge(s["exd"], 1)
            link(scan(sm[:, 0, :], same[:, 2, :], sm[:, 2, :], 0.0, ALU.mult, ALU.add, False))
            link(dve.tensor_tensor(sm[:, 1, :], sm[:, 0, :], same[:, 4, :], ALU.mult))
            link(scan(sm[:, 0, :], same[:, 3, :], sm[:, 1, :], 0.0, ALU.mult, ALU.add, True))
            link(dve.reciprocal(sm[:, 1, :], sm[:, 0, :]))
            dve.tensor_tensor(sm[:, 3, :], sm[:, 2, :], sm[:, 1, :], ALU.mult).then_inc(s["att"], 1)
            dve.wait_ge(s["tr_a"], 1)
            dve.tensor_copy(AT[:, :, :], bank[6][:, 0:EB * P].rearrange("p (e c) -> p e c", e=EB)).then_inc(s["at_c"], 1)
            dve.wait_ge(s["at_c"], 1)

            def rows(t, u, k):
                if inside(t, T):
                    dve.wait_ge(s["vt"], t + 1)
                    if past(t, 2):
                        dve.wait_ge(s["yt"], t - 1)
                    for e in range(EB):
                        w = AT[:, e, cols(t, PAIR * HEADS)].rearrange("p (c o) -> p c o", o=1)
                        ins = dve.tensor_tensor(ring[:, 10 + u, e * 256:(e + 1) * 256].rearrange("p (c d) -> p c d", d=DH),
                                                bank[u][:, e * 256:(e + 1) * 256].rearrange("p (c d) -> p c d", d=DH),
                                                w.to_broadcast([P, PAIR * HEADS, DH]), ALU.mult)
                    ins.then_inc(s["vt_c"], 1)
                old = older(t, u, k, 2, T)
                if old:
                    t2, u2, _ = old
                    dve.wait_ge(s["o_pe"], t2 + 1)
                    for q in range(4):
                        ins = dve.bn_stats(bst[:, u2, q, :], bank[4 + u2][:, q * P:(q + 1) * P])
                    ins.then_inc(s["bs"], 1)
                    dve.wait_ge(s["bs"], t2 + 1)
                    dve.sem_inc(s["aggr_on"], 1)
                    for q in range(4):
                        ins = dve.bn_aggr(mv[:, u2, q, :], bst[:, u2, q, :])
                    ins.then_inc(s["st3"], 1)
                old = older(t, u, k, 3, T)
                if old:
                    t3, u3, k3 = old
                    dve.wait_ge(s["rso"], t3 + 1)
                    dve.scalar_tensor_tensor(fin[:, u3, 8:12], mv[:, u3, :, 0], -1.0, fin[:, u3, 4:8], ALU.mult, ALU.mult)\
                        .then_inc(s["nm"], 1)
                    dve.wait_ge(s["nm"], t3 + 1)
                    if past(t3, 2):
                        dve.wait_ge(s[f"out{u3}"], k3 * (16 * PAIR))
                    for q in range(4):
                        ins = dve.tensor_scalar(ring[:, 14 + u3, q * P:(q + 1) * P], bank[4 + u3][:, q * P:(q + 1) * P],
                                                fin[:, u3, 4 + q:5 + q], fin[:, u3, 8 + q:9 + q], ALU.mult, ALU.add)
                    ins.then_inc(s["o_fin"], 1)
            over(dve, T, 3, rows)

        @block.scalar
        def _(act):
            n = 0

            def link(ins):
                nonlocal n
                n += 1
                ins.then_inc(s["ach"], 1)
                act.wait_ge(s["ach"], n)

            act.preload_act_table_set("sqrt_and_others")
            act.wait_ge(s["dch"], at["deg"])
            link(act.activation(deg[:, 6:8], deg[:, 4:6], ACT.Sqrt))

            def agg(t, u, k):
                if inside(t, T):
                    act.wait_ge(s["agg_ready"], t + 1)
                    if past(t, 2):
                        act.wait_ge(s["hpre_ready"], t - 1)
                    act.activation(agg_t(u), bank[u][:, :], ACT.Copy).then_inc(s["agg_copied"], 1)
                old = older(t, u, k, 1, T)
                if old:
                    t1, u1, _ = old
                    act.wait_ge(s["hpre_ready"], t1 + 1)
                    for j in range(HB):
                        ins = act.activation(HID[j][:, cols(t1, W)], bank[2 + 2 * u1 + j][:, :], ACT.Identity,
                                             bias=col1[:, 0, j:j + 1])
                    ins.then_inc(s["h_stored"], 1)
            act.wait_ge(s["in_e"], N_E)
            over(act, T, 1, agg)

            act.wait_ge(s["stat1"], T + 1)
            link(act.activation(bn[:, 0:2, 2], bn[:, 0:2, 1], ACT.Sqrt, bias=cst[:, 0:1]))
            act.wait_ge(s["bn1"], 1)

            def layer2(t, u, k):
                if inside(t, T):
                    if past(t, 2):
                        act.wait_ge(s["w2_done"], t - 1)
                    for j in range(HB):
                        ins = act.activation(h_r(u, j), HID[j][:, cols(t, W)], ACT.Relu, scale=bn[:, j, 4:5],
                                             bias=bn[:, j, 5:6])
                    ins.then_inc(s["relu_ready"], 1)
                old = older(t, u, k, 1, T)
                if old:
                    t1, u1, _ = old
                    act.wait_ge(s["w2_done"], t1 + 1)
                    act.activation(O[:, cols(t1, W)], bank[u1][:, :], ACT.Identity, bias=col2[:, 0:1])\
                        .then_inc(s["o_stored"], 1)
            over(act, T, 1, layer2)

            act.wait_ge(s["stat2"], T + 1)
            link(act.activation(bn[:, 2, 2:3], bn[:, 2, 1:2], ACT.Sqrt, bias=cst[:, 0:1]))

            def norm(r):
                def body(t, u, k):
                    if inside(t, T):
                        act.wait_ge(s["cen" + r], t + 1)
                        if past(t, 4):
                            act.wait_ge(s["ln" + r], t - 3)
                        act.activation(sq_r(u), bank[u][:, :], ACT.Square).then_inc(s["sq" + r], 1)
                    old = older(t, u, k, 1, T, 4)
                    if old:
                        t1, u1, _ = old
                        act.wait_ge(s["var" + r], t1 + 1)
                        act.activation(sq_r(u1), bank[4 + u1][:, :], ACT.Ln, bias=cst[:, 0:1])\
                            .then_inc(s["lg" + r], 1)
                        act.wait_ge(s["lg" + r], t1 + 1)
                        act.activation(sq_r(u1), sq_r(u1), ACT.Exp, scale=-0.5).then_inc(s["rs" + r], 1)
                over(act, T, 1, body, unroll=4)
            act.preload_act_table_set("natural_log_exp_and_others")
            norm("1")
            act.wait_ge(s["dch"], at["adje"])
            link(act.activation(lacol[:, 2:4], lacol[:, 0:2], ACT.Ln, bias=cst[:, 1:2]))

            def gcn(t, u, k):
                old = older(t, u, k, 3, T)
                if old:
                    t3, u3, _ = old
                    act.wait_ge(s["z1_done"], t3 + 1)
                    act.activation(HL[:, cols(t3, W)], bank[6 + u3][:, :], ACT.Relu).then_inc(s["z1_copied"], 1)
                old = older(t, u, k, 1, T)
                if old:
                    t1, u1, _ = old
                    act.wait_ge(s["z0_done"], t1 + 1)
                    if past(t1, 2):
                        act.wait_ge(s["y1_done"], t1 - 1)
                    act.activation(ring[:, 12 + u1, :], bank[2 + u1][:, :], ACT.Relu).then_inc(s["z0_copied"], 1)
            over(act, T, 3, gcn)

            def lstm(p, i, chunks, width, base, _):
                order = (0, 2, 3) if i == 0 else (0, 2, 1, 3)

                def body(c, u, k):
                    if inside(c, chunks):
                        act.wait_ge(s["gates_ready"], c + (base + 1))
                        if past(c, 2) or base:
                            act.wait_ge(s["h_done"], c + (base - 1))
                        for g in order:
                            ins = act.activation(shaped(ring[:, 2 * g + u, :], p, width),
                                                 shaped(bank[2 * g + u][:, :], p, width),
                                                 ACT.Tanh if g == 2 else ACT.Sigmoid, bias=bl[:, p - 1, g:g + 1])
                        ins.then_inc(s["gates_read"], 1)
                    old = older(c, u, k, 1, chunks)
                    if old:
                        c1, u1, _ = old
                        act.wait_ge(s["c_done"], c1 + (base + 1))
                        act.activation(ring[:, 8 + u1, 0:width], CELL[:, cols(c1, width)], ACT.Tanh)\
                            .then_inc(s["tc_ready"], 1)
                over(act, chunks, 1, body, 2)
            act.preload_act_table_set("sigmoid_and_others")
            for loop in LOOPS:
                lstm(*loop)
            act.preload_act_table_set("natural_log_exp_and_others")
            norm("2")

            def attend(t, u, k):
                for j in range(8):
                    for at_j, pe_done, hi, x, scale in ((Q_AT, "q_pe", "q_hi", 0, DH ** -0.5),
                                                        (K_AT, "k_pe", "k_hi", 1, 1.0)):
                        if j == at_j and inside(t, T):
                            act.wait_ge(s[pe_done], t + 1)
                            if past(t, 2):
                                for g in range(2):
                                    act.wait_ge(s[f"stk{g}{u}"], k * 128)
                            act.activation(spl[:, u, 2 * x, :], bank[x][:, :], ACT.Copy, scale=scale)\
                                .then_inc(s[hi], 1)
                    w = unit(t, u, j, EXP_LAG, T)
                    if w:
                        t0, _, j0 = w
                        act.wait_ge(s["mx"], 8 * t0 + (j0 + 1))
                        if j0 >= 4 or past(t0, 1):
                            act.wait_ge(s["tp"], 8 * t0 + (j0 - 3))
                        for h in range(2):
                            ins = act.activation(pr(j0)[:, h * N:(h + 1) * N],
                                                 bank[3 + j0 % 2][:, h * N:(h + 1) * N], ACT.Exp,
                                                 bias=den[:, j0, h:h + 1], accum_out=den[:, j0, 2 + h:3 + h])
                        ins.then_inc(s["ex"], 1)
                    w = unit(t, u, j, TURN_COPY_LAG, T)
                    if w:
                        t2, _, j2 = w
                        act.wait_ge(s["tp"], 8 * t2 + (j2 + 1))
                        if j2 >= 4 or past(t2, 1):
                            act.wait_ge(s["av"], 8 * t2 + (j2 - 3))
                        act.activation(pt(j2), bank[5 + j2 % 2][:, :], ACT.Copy).then_inc(s["tp_c"], 1)
            over(act, T, 2, attend, 4)
            norm("3")

            def edges(t, u, k):
                if inside(t, T):
                    act.wait_ge(s["xqv"], t + 1)
                    if past(t, 2):
                        act.wait_ge(s["z_done"], t - 1)
                    act.activation(ring[:, 10 + u, :], bank[u][:, :], ACT.Copy).then_inc(s["xq_c"], 1)
                old = older(t, u, k, 1, T)
                if old:
                    t1, u1, _ = old
                    act.wait_ge(s["z_done"], t1 + 1)
                    act.activation(ring[:, 12 + u1, :], bank[4 + u1][:, :], ACT.Copy, scale=SLOPE)\
                        .then_inc(s["z_c"], 1)
            over(act, T, 1, edges)

            act.wait_ge(s["sm_e"], 1)
            act.activation(sm[:, 2, :], sm[:, 1, :], ACT.Exp).then_inc(s["exd"], 1)

            def rows(t, u, k):
                old = older(t, u, k, 1, T)
                if old:
                    t1, u1, _ = old
                    act.wait_ge(s["yt"], t1 + 1)
                    if past(t1, 2):
                        act.wait_ge(s["o_pe"], t1 - 1)
                    act.activation(ring[:, 12 + u1, :], bank[2 + u1][:, :], ACT.Copy).then_inc(s["yt_c"], 1)
                old = older(t, u, k, 2, T)
                if old:
                    t2, u2, _ = old
                    act.wait_ge(s["st3"], t2 + 1)
                    act.activation(fin[:, u2, 0:4], mv[:, u2, :, 1], ACT.Ln, bias=cst[:, 0:1]).then_inc(s["lgo"], 1)
                    act.wait_ge(s["lgo"], t2 + 1)
                    act.activation(fin[:, u2, 4:8], fin[:, u2, 0:4], ACT.Exp, scale=-0.5).then_inc(s["rso"], 1)
            over(act, T, 2, rows)

        @block.tensor
        def _(pe):
            def mm(o, l, r, first=True, last=True):
                return pe.matmul(o, l, r, start=first, stop=last)

            pe.wait_ge(s["dch"], at["diag"])
            for m in range(NB):
                ins = mm(bank[7][:, m * P:(m + 1) * P], ones[:, :], dgs[:, m, :])
            ins.then_inc(s["setup_pe"], 1)

            pe.wait_ge(s["dch"], at["aht"])
            pe.wait_ge(s["in_w1"], 16)

            def agg(t, u, k):
                if inside(t, T):
                    pe.wait_ge(s[f"xa{u}"], 16 * PAIR * k + 16 * PAIR)
                    if past(t, 2):
                        pe.wait_ge(s["agg_copied"], t - 1)
                    for b in range(PAIR):
                        for m in range(NB):
                            ins = mm(bank[u][:, b * N:(b + 1) * N], x_r(u)[:, b, m, :], aht[:, m, :], m == 0, m == NB - 1)
                    ins.then_inc(s["agg_ready"], 1)
                old = older(t, u, k, 1, T)
                if old:
                    t1, u1, _ = old
                    pe.wait_ge(s["agg_copied"], t1 + 1)
                    if past(t1, 2):
                        pe.wait_ge(s["h_stored"], t1 - 1)
                    for j in range(HB):
                        ins = mm(bank[2 + 2 * u1 + j][:, :], w1[:, j * P:(j + 1) * P], agg_t(u1))
                    ins.then_inc(s["hpre_ready"], 1)
            over(pe, T, 1, agg)
            pe.wait_ge(s["dch"], at["perm"])
            for j in range(2):
                for e in range(EB):
                    mm(bank[6][:, j * E:(j + 1) * E], bc[:, j, e, :], perm[:, e, :], e == 0, e == EB - 1)
                for q in range(EB):
                    for e in range(EB):
                        ins = mm(bank[7][:, j * EB + q:j * EB + q + 1], perm[:, e, q * P:(q + 1) * P], ec[:, j, e:e + 1],
                                 e == 0, e == EB - 1)
            ins.then_inc(s["setup_pe"], 1)

            pe.wait_ge(s["in_w2"], 48)

            def layer2(t, u, k):
                if inside(t, T):
                    pe.wait_ge(s["relu_ready"], t + 1)
                    if past(t, 2):
                        pe.wait_ge(s["o_stored"], t - 1)
                    for j in range(HB):
                        ins = mm(bank[u][:, :], w2[:, j, :], h_r(u, j), j == 0, j == HB - 1)
                    ins.then_inc(s["w2_done"], 1)
            over(pe, T, 0, layer2)

            def norm(r):
                def body(t, u, k):
                    if inside(t, T):
                        pe.wait_ge(s["v" + r], t + 1)
                        if past(t, 4):
                            pe.wait_ge(s["ln" + r], t - 3)
                        mm(bank[u][:, :], cent[:, :], v_r(u)).then_inc(s["cen" + r], 1)
                    old = older(t, u, k, 1, T, 4)
                    if old:
                        t1, u1, _ = old
                        pe.wait_ge(s["sq" + r], t1 + 1)
                        if past(t1, 4):
                            pe.wait_ge(s["lg" + r], t1 - 3)
                        mm(bank[4 + u1][:, :], mean1[:, :], sq_r(u1)).then_inc(s["var" + r], 1)
                over(pe, T, 1, body, 8, unroll=4)
            pe.wait_ge(s["dch"], at["srct"])
            for e in range(EB):
                for m in range(NB):
                    ins = mm(bank[7][:, e * N:(e + 1) * N], srct[:, m, e * P:(e + 1) * P], adjs[:, m, :],
                             m == 0, m == NB - 1)
            ins.then_inc(s["setup_pe"], 1)
            pe.wait_ge(s["o_stored"], T)
            norm("1")

            def gcn(t, u, k):
                old = older(t, u, k, 3, T)
                if old:
                    t3, u3, _ = old
                    pe.wait_ge(s["y1_copied"], t3 + 1)
                    if past(t3, 2):
                        pe.wait_ge(s["z1_copied"], t3 - 1)
                    for b in range(PAIR):
                        for m in range(NB):
                            ins = mm(bank[6 + u3][:, b * N:(b + 1) * N],
                                     ring[:, 14 + u3, (b * NB + m) * P:(b * NB + m + 1) * P], adjt[:, m, :],
                                     m == 0, m == NB - 1)
                    ins.then_inc(s["z1_done"], 1)
                old = older(t, u, k, 2, T)
                if old:
                    t2, u2, _ = old
                    pe.wait_ge(s["z0_copied"], t2 + 1)
                    if past(t2, 2):
                        pe.wait_ge(s["y1_copied"], t2 - 1)
                    for q in range(4):
                        ins = mm(bank[4 + u2][:, q * P:(q + 1) * P], ring[:, 12 + u2, q * P:(q + 1) * P], wg[:, 1, :])
                    ins.then_inc(s["y1_done"], 1)
                old = older(t, u, k, 1, T)
                if old:
                    t1, u1, _ = old
                    pe.wait_ge(s["y0_copied"], t1 + 1)
                    if past(t1, 2):
                        pe.wait_ge(s["z0_copied"], t1 - 1)
                    for b in range(PAIR):
                        for m in range(NB):
                            ins = mm(bank[2 + u1][:, b * N:(b + 1) * N],
                                     ring[:, 10 + u1, (b * NB + m) * P:(b * NB + m + 1) * P], adjt[:, m, :],
                                     m == 0, m == NB - 1)
                    ins.then_inc(s["z0_done"], 1)
                if inside(t, T):
                    pe.wait_ge(s["xs_g"], t + 1)
                    if past(t, 2):
                        pe.wait_ge(s["y0_copied"], t - 1)
                    for q in range(4):
                        ins = mm(bank[u][:, q * P:(q + 1) * P], xs_r(u)[:, q * P:(q + 1) * P], wg[:, 0, :])
                    ins.then_inc(s["y0_done"], 1)
            pe.wait_ge(s["ln1"], T)
            over(pe, T, 3, gcn)

            def lstm(p, i, chunks, width, base, _):
                order = (0, 2, 3) if i == 0 else (0, 2, 1, 3)

                def body(c, u, k):
                    if p == 1:
                        pe.wait_ge(s["z1_copied"], c + 1)
                    elif i == 0 and p == 3:
                        pe.wait_ge(s["h_done"], c + (base - chunks + 1))
                    elif i == 0:
                        pe.wait_ge(s["h_done"], c * 2 + (base - 2 * chunks + 2))
                    if i:
                        pe.wait_ge(s["h_done"], c + (base - chunks + 1))
                    if past(c, 2) or base:
                        pe.wait_ge(s["gates_read"], c + (base - 1))
                    for g in order:
                        o = shaped(bank[2 * g + u][:, :], p, width)
                        ins = mm(o, wih[:, p - 1, g * D:(g + 1) * D], win(p, i, c), True, i == 0)
                        if i:
                            ins = mm(bank[2 * g + u][:, 0:width], whh[:, p - 1, g * D:(g + 1) * D],
                                     HST[:, cols(c, width)], False, True)
                    ins.then_inc(s["gates_ready"], 1)
                over(pe, chunks, 0, body)
            pe.wait_ge(s["z1_copied"], T)
            pe.wait_ge(s["in_w"], 96)
            for loop in LOOPS:
                lstm(*loop)
            pe.wait_ge(s["gates_read"], n_item)
            pe.wait_ge(s["dch"], at["ladiag"])
            for e in range(EB):
                ins = mm(bank[7][:, e * P:(e + 1) * P], ones[:, :], dgs[:, e, :])
            ins.then_inc(s["setup_pe"], 1)
            norm("2")

            def attend(t, u, k):
                for j in range(8):
                    for at_j, x, done in ((Q_AT, 0, "q_pe"), (K_AT, 1, "k_pe")):
                        if j == at_j and inside(t, T):
                            pe.wait_ge(s["xs_a"], t + 1)
                            if x == 0 and past(t, 1):
                                pe.wait_ge(s["v_c"], t)
                            if x == 1 and past(t, 1):
                                for name in ("k_hi", "k_lo"):
                                    pe.wait_ge(s[name], t)
                            mm(bank[x][:, :], wqkv[:, x * D:(x + 1) * D], xs_r(u)).then_inc(s[done], 1)
                    if j == V_AT and inside(t, T):
                        for name in ("q_hi", "q_lo"):
                            pe.wait_ge(s[name], t + 1)
                        for q in range(4):
                            ins = mm(bank[0][:, q * P:(q + 1) * P], xs_r(u)[:, q * P:(q + 1) * P], wqkv[:, 2 * D:3 * D])
                        ins.then_inc(s["v_pe"], 1)
                    w = unit(t, u, j, 0, T)
                    if w:
                        t0, u0, j0 = w
                        k0 = (u - 1) // 2 + k
                        hp, b, r = j0 // 4, j0 // 2 % 2, j0 % 2
                        if j0 % 4 == 0:
                            pe.wait_ge(s[f"stk{hp}{u0}"], k0 * 128 + 128)
                        if j0 >= 2 or past(t0, 1):
                            pe.wait_ge(s["ex"], 8 * t0 + (j0 - 1))
                        o = bank[3 + j0 % 2]
                        mm(o[:, :], identb[:, :], mbias[:, r].rearrange("p a n -> p (a n)"), True, False)
                        for h in range(2):
                            ins = mm(o[:, h * N:(h + 1) * N], stk[:, u0, 0, 2 * hp + h, b * N + r * P:b * N + (r + 1) * P],
                                     stk[:, u0, 1, 2 * hp + h, b * N:(b + 1) * N], False, h == 1)
                        ins.then_inc(s["s_done"], 1)
                    w = unit(t, u, j, TURN_LAG, T)
                    if w:
                        t2, u2, j2 = w
                        pe.wait_ge(s["nrm"], 8 * t2 + (j2 + 1))
                        if j2 >= 2 or past(t2, 1):
                            pe.wait_ge(s["tp_c"], 8 * t2 + (j2 - 1))
                        for q in range(4):
                            ins = pe.transpose(bank[5 + j2 % 2][:, q * P:(q + 1) * P],
                                               pr(j2)[:, q * P:(q + 1) * P], ident[:, :])
                        ins.then_inc(s["tp"], 1)
                    w = unit(t, u, j, AV_LAG, T)
                    if w:
                        t3, u3, j3 = w
                        hp, b, r = j3 // 4, j3 // 2 % 2, j3 % 2
                        pe.wait_ge(s["tp_c"], 8 * t3 + (j3 + 1))
                        if j3 == 0:
                            pe.wait_ge(s["v_c"], t3 + 1)
                        if j3 == 0 and past(t3, 2):
                            pe.wait_ge(s["av_c"], t3 - 1)
                        for h in range(2):
                            c = DH * (2 * hp + h)
                            for m in range(NB):
                                ins = mm(bank[7 - 5 * u3][c:c + DH, b * N + r * P:b * N + (r + 1) * P],
                                         vr(u3)[:, (b * NB + m) * D + c:(b * NB + m) * D + c + DH],
                                         pt(j3)[:, (h * NB + m) * P:(h * NB + m + 1) * P], m == 0, m == NB - 1)
                        ins.then_inc(s["av"], 1)
            pe.wait_ge(s["ln2"], T)
            over(pe, T, 2, attend, 4)
            pe.wait_ge(s["av_c"], T)
            norm("3")

            def edges(t, u, k):
                if inside(t, T):
                    pe.wait_ge(s["xs_e"], t + 1)
                    if past(t, 2):
                        pe.wait_ge(s["xq_c"], t - 1)
                        pe.wait_ge(s["xv_c"], t - 1)
                    for q in range(4):
                        mm(bank[u][:, q * P:(q + 1) * P], xs_r(u)[:, q * P:(q + 1) * P], wlin[:, :])
                    for q in range(4):
                        ins = mm(bank[2 + u][:, q * P:(q + 1) * P], xs_r(u)[:, q * P:(q + 1) * P], wval[:, :])
                    ins.then_inc(s["xqv"], 1)
                old = older(t, u, k, 1, T)
                if old:
                    t1, u1, _ = old
                    pe.wait_ge(s["xq_c"], t1 + 1)
                    if past(t1, 2):
                        pe.wait_ge(s["lr"], t1 - 1)
                    for b in range(PAIR):
                        for m in range(NB):
                            ins = mm(bank[4 + u1][:, b * E:(b + 1) * E],
                                     ring[:, 10 + u1, (b * NB + m) * P:(b * NB + m + 1) * P],
                                     sum1[:, m, :], m == 0, m == NB - 1)
                    ins.then_inc(s["z_done"], 1)
                old = older(t, u, k, 2, T)
                if old:
                    t2, u2, _ = old
                    pe.wait_ge(s["lr"], t2 + 1)
                    if past(t2, 2):
                        pe.wait_ge(s["e_c"], t2 - 1)
                    for e in range(EB):
                        for b in range(PAIR):
                            c = (e * PAIR + b) * HEADS
                            ins = mm(bank[6 + u2][:, c:c + HEADS],
                                     ring[:, 14 + u2, b * E + e * P:b * E + (e + 1) * P], abd[:, :])
                    ins.then_inc(s["e_done"], 1)
            pe.wait_ge(s["ln3"], T)
            over(pe, T, 2, edges)
            pe.wait_ge(s["e_c"], T)
            for e in range(EB):
                ins = pe.transpose(bank[0][:, e * P:(e + 1) * P], ET[:, e, :], ident[:, :])
            ins.then_inc(s["tr_e"], 1)
            pe.wait_ge(s["att"], 1)
            for e in range(EB):
                ins = pe.transpose(bank[6][:, e * P:(e + 1) * P], sm[:, 3, e * P:(e + 1) * P], ident[:, :])
            ins.then_inc(s["tr_a"], 1)
            pe.wait_ge(s["at_c"], 1)

            def rows(t, u, k):
                if inside(t, T):
                    if past(t, 2):
                        pe.wait_ge(s["vt_c"], t - 1)
                    v = VV[:, cols(t, W)].rearrange("p (b m f) -> p b m f", b=PAIR, m=NB)
                    for e in range(EB):
                        for m in range(NB):
                            ins = mm(bank[u][:, e * 256:(e + 1) * 256].rearrange("p (b f) -> p b f", b=PAIR),
                                     dst1[:, m, e * P:(e + 1) * P], v[:, :, m, :], m == 0, m == NB - 1)
                    ins.then_inc(s["vt"], 1)
                old = older(t, u, k, 1, T)
                if old:
                    t1, u1, _ = old
                    pe.wait_ge(s["vt_c"], t1 + 1)
                    if past(t1, 2):
                        pe.wait_ge(s["yt_c"], t1 - 1)
                    for b in range(PAIR):
                        for e in range(EB):
                            ins = mm(bank[2 + u1][:, b * N:(b + 1) * N],
                                     ring[:, 10 + u1, (e * PAIR + b) * P:(e * PAIR + b + 1) * P], src1[:, e, :],
                                     e == 0, e == EB - 1)
                    ins.then_inc(s["yt"], 1)
                old = older(t, u, k, 2, T)
                if old:
                    t2, u2, _ = old
                    pe.wait_ge(s["yt_c"], t2 + 1)
                    pe.wait_ge(s["xs_o"], t2 + 1)
                    if past(t2, 2):
                        pe.wait_ge(s["o_fin"], t2 - 1)
                    for q in range(4):
                        mm(bank[4 + u2][:, q * P:(q + 1) * P], xs_r(u2)[:, q * P:(q + 1) * P], ident[:, :], True, False)
                        ins = mm(bank[4 + u2][:, q * P:(q + 1) * P], ring[:, 12 + u2, q * P:(q + 1) * P], wout[:, :],
                                 False, True)
                    ins.then_inc(s["o_pe"], 1)
            over(pe, T, 2, rows)
    return nc


def kernel(**inputs):
    import numpy as np
    import concourse.bacc as bacc
    from concourse.bass_utils import run_bass_kernel_spmd

    a = {k: np.asarray(v) for k, v in inputs.items()}
    x = a["x"]
    laid = {
        "x_tok": x,
        "x_feat": x.transpose(2, 0, 1).reshape(x.shape[2], -1),
        "adj": a["adj"],
        "adj_t": a["adj"].T,
        "w1_t": a["L0_gnn_W1"].T, "w2_t": a["L0_gnn_W2"].T,
        "cols1": np.stack([a["L0_gnn_b1"], a["L0_gnn_g1"], a["L0_gnn_be1"]]).reshape(3, -1, P).transpose(2, 0, 1),
        "cols2": np.stack([a["L0_gnn_b2"], a["L0_gnn_g2"], a["L0_gnn_be2"]]).T,
        "wg0": a["L1_gnn_Wg0"], "bg0": a["L1_gnn_bg0"], "wg1": a["L1_gnn_Wg1"], "bg1": a["L1_gnn_bg1"],
        "wih_t": a["L1_gnn_Wih"].transpose(0, 2, 1), "whh_t": a["L1_gnn_Whh"].transpose(0, 2, 1),
        "bih": a["L1_gnn_bih"].reshape(4, 4, P).transpose(2, 0, 1),
        "bhh": a["L1_gnn_bhh"].reshape(4, 4, P).transpose(2, 0, 1),
        "w_qkv": a["L2_gnn_W"],
        "w_lin_t": a["L3_gnn_W_lin"].T, "w_val_t": a["L3_gnn_W_val"].T, "a": a["L3_gnn_a"],
        "w_out_t": a["L3_gnn_W_out"].T, "src": a["L3_gnn_src"], "dst": a["L3_gnn_dst"],
        "edge_cols": np.stack([a["L3_gnn_src"], a["L3_gnn_dst"]]).reshape(2, -1, P).transpose(2, 0, 1),
    }
    nc = bacc.Bacc("TRN2", target_bir_lowering=False, num_devices=1)
    arrays, aps = {}, {}
    for name, v in laid.items():
        arrays["in_" + name] = np.ascontiguousarray(v)
        aps[name] = nc.dram_tensor("in_" + name, v.shape, mybir.dt.from_np(v.dtype), kind="ExternalInput").ap()
    aps["out"] = nc.dram_tensor("out_x", x.shape, F32, kind="ExternalOutput").ap()
    build_program(nc, **aps)
    r = run_bass_kernel_spmd(nc, [arrays], core_ids=[0])
    return r.results[0]["out_x"]
```

```python
from contextlib import ExitStack

import concourse.bass as bass
from concourse import mybir

F32 = mybir.dt.float32
F32R = mybir.dt.float32r
BF16 = mybir.dt.bfloat16
I32 = mybir.dt.int32
ALU = mybir.AluOpType
ACT = mybir.ActivationFunctionType
AX_X = mybir.AxisListType.X

P = 128
EPS = 1e-5
LOG_EPS = 1e-8
NEG = -1e30
PAIR = 2
SLOPE = 0.2


def past(t, k):
    return not isinstance(t, int) or t >= k


def over(eng, total, lag, body, ahead=None, unroll=2):
    ahead = ahead or -(-(lag + 2) // unroll) * unroll
    for t in range(ahead):
        body(t, t % unroll, t // unroll)
    with eng.Fori(ahead // unroll, total // unroll) as k:
        for u in range(unroll):
            body(k * unroll + u, u, k)
    for t in range(total, total + lag):
        body(t, t % unroll, t // unroll)


def inside(t, total):
    return not isinstance(t, int) or 0 <= t < total


def older(t, u, k, lag, total, unroll=2):
    if isinstance(t, int):
        if not 0 <= t - lag < total:
            return None
        return t - lag, (t - lag) % unroll, (t - lag) // unroll
    return t - lag, (u - lag) % unroll, k + (u - lag) // unroll


def cols(t, n):
    return slice(t * n, (t + 1) * n) if isinstance(t, int) else bass.ds(t * n, n)


def build_program(nc, x_tok, x_feat, adj, adj_t, w1_t, w2_t, cols1, cols2, wg0, bg0, wg1, bg1,
                  wih_t, whh_t, bih, bhh, w_qkv, w_lin_t, w_val_t, a, w_out_t, src, dst, edge_cols, out):
    B, N, D = x_tok.shape
    H1 = w1_t.shape[1]
    HB = H1 // P
    NB = N // P
    TOK = B * N
    T = B // PAIR
    W = PAIR * N
    STEPS = wih_t.shape[0]
    HEADS, DH = a.shape
    E = src.shape[0]
    EB = E // P
    assert D == P and W == 512 and HEADS * DH == P and B * HEADS == P and E == N

    with ExitStack() as ctx:
        def sb(name, shape, dt=F32):
            return ctx.enter_context(nc.sbuf_tensor(name, shape, dt))

        def sem(name):
            return ctx.enter_context(nc.semaphore(name))

        bank = [ctx.enter_context(nc.psum_tensor(f"bank{i}", [P, 512], F32)) for i in range(8)]

        X = sb("X", [P, TOK])

        w1 = sb("w1", [P, H1])
        w2 = sb("w2", [P, HB, D])
        wg = sb("wg", [P, 2, D])
        bgb = sb("bgb", [P, 2, 1, D])
        w_hi = sb("w_hi", [P, 2, 2, 4 * D], F32R)
        w_lo = sb("w_lo", [P, 2, 2, 4 * D], F32R)
        bi = sb("bi", [P, STEPS, 4])
        bh = sb("bh", [P, STEPS, 4])
        bl = sb("bl", [P, STEPS, 4])
        wqkv = sb("wqkv", [P, 3 * D])
        wlin = sb("wlin", [P, D])
        wval = sb("wval", [P, D])
        wout = sb("wout", [P, D])
        abd = sb("abd", [P, HEADS])
        col1 = sb("col1", [P, 3, HB])
        col2 = sb("col2", [P, 3])
        adjs = sb("adjs", [P, NB, N])
        adjt = sb("adjt", [P, NB, N])
        aht = sb("aht", [P, NB, N])
        ident = sb("ident", [P, P])
        identb = sb("identb", [P, P], BF16)
        cent = sb("cent", [P, P])
        mean1 = sb("mean1", [P, P])
        ones = sb("ones", [P, P])
        mbias = sb("mbias", [P, NB, 2, N], BF16)
        cst = sb("cst", [P, 4])
        deg = sb("deg", [P, 8])
        dinv = sb("dinv", [P, NB])
        ttr = sb("ttr", [P, N])

        ring = sb("ring", [P, 16, 512])
        st1 = sb("st1", [P, HB, T * 6])
        st2 = sb("st2", [P, T * 6])
        bn = sb("bn", [P, 3, 8])

        eci = sb("eci", [P, 2, EB], I32)
        ec = sb("ec", [P, 2, EB])
        iof = sb("iof", [P, E])
        ioi = sb("ioi", [P, E], I32)
        ioc = sb("ioc", [P, EB])
        ioci = sb("ioci", [P, EB], I32)
        keyc = sb("keyc", [P, EB])
        rank = sb("rank", [P, EB])
        scol = sb("scol", [P, 2, EB])
        dst1 = sb("dst1", [P, NB, E], F32R)
        sum1 = sb("sum1", [P, NB, E], F32R)
        src1 = sb("src1", [P, EB, N], F32R)
        early = lambda i: ring[:, 8 + i, :].rearrange("p (a e) -> p a e", a=2)
        ei = early(0).bitcast(I32)
        er, perm, srow, srct, dstc = (early(i) for i in range(1, 6))
        keyr = ring[:, 15, 0:E]
        bc = ring[:, 14, :].rearrange("p (j e c) -> p j e c", j=2, e=EB)
        lacol = sb("lacol", [P, 4])
        larow = sb("larow", [P, E])
        srk = sb("srk", [P, E])
        same = ring[:, 2:5, :].rearrange("p a (b e) -> p (a b) e", b=2)
        ET = aht[:, 0, :].rearrange("p (e c) -> p e c", e=EB)
        AT = aht[:, 1, :].rearrange("p (e c) -> p e c", e=EB)
        den = sb("den", [P, 8, 6])
        dgs = sb("dgs", [P, 2, P])
        bst = sb("bst", [P, 2, 4, 6])
        mv = sb("mv", [P, 4, 4, 2])
        fin = sb("fin", [P, 4, 12])

        def stage(*tensors):
            with ExitStack() as only:
                return [only.enter_context(nc.sbuf_tensor(name, shape, dt)) for name, shape, dt in tensors]

        H1A, H1B, O = stage(("H1A", [P, TOK], F32), ("H1B", [P, TOK], F32), ("O", [P, TOK], F32))
        HID = (H1A, H1B)
        CELLS = B * (N // 3)
        assert 3 * CELLS <= TOK
        hl_hi, CELL, hs_hi, hs_lo, _, hl_lo = stage(
            ("hl_hi", [P, TOK], F32R), ("CELL", [P, CELLS], F32), ("hs_hi", [P, CELLS], F32R),
            ("hs_lo", [P, CELLS], F32R), ("spare", [P, TOK - 3 * CELLS], F32), ("hl_lo", [P, TOK], F32R))
        att_out, stk, spl = stage(("att_out", [P, TOK], F32), ("stk", [P, 2, 2, HEADS, 512], F32R),
                                  ("spl", [P, 2, 4, 512], F32R))
        vv_hi, vv_lo, e_hi, e_lo = stage(("vv_hi", [P, TOK], F32R), ("vv_lo", [P, TOK], F32R),
                                         ("e_hi", [P, 4, 512], F32R), ("e_lo", [P, 4, 512], F32R))

        names = ["in_adj", "in_w1", "in_w2", "in_x", "in_w", "in_wl", "w_h", "w_l", "in_e", "pool_c", "setup_pe", "dch", "ach", "xa0", "xa1",
                 "agg_ready", "agg_copied", "hpre_ready", "h_stored", "stat1", "bn1", "relu_ready", "w2_done",
                 "o_stored", "stat2", "bn2", "tmp_ready"]
        for r in "123":
            names += [f"v{r}", f"cen{r}", f"sq{r}", f"var{r}", f"lg{r}", f"rs{r}", f"ln{r}"]
        names += ["xs_g", "y0_done", "y0_copied", "z0_done", "z0_copied", "y1_done", "y1_copied", "z1_done",
                  "z1_copied", "z1_low", "gates_ready", "gates_read", "prod", "c_done", "tc_ready", "h_new",
                  "h_high", "h_done"]
        names += ["xs_a", "q_pe", "k_pe", "v_pe", "q_hi", "k_hi", "q_lo", "k_lo", "v_c", "stk00", "stk01", "stk10", "stk11", "s_done",
                  "mx", "ex", "tp", "tp_c", "av", "rc", "nrm", "av_c"]
        names += ["xs_e", "xqv", "xq_c", "xv_c", "xq_l", "xv_l", "z_done", "z_c", "lr", "e_done", "e_c",
                  "tr_e", "sm_e", "exd", "att", "tr_a", "at_c",
                  "xs_o", "vt", "vt_c", "vt_h", "vt_l", "yt", "yt_c", "o_pe", "bs", "nm", "aggr_on", "st3", "lgo", "rso", "o_fin", "out0", "out1"]
        s = {n: sem(n) for n in names}
        block = ctx.enter_context(nc.Block())

        sm = ring[:, 0:2, :].rearrange("p a (b e) -> p (a b) e", b=2)
        w_stage = lambda q: ring[:, 2 * q:2 * q + 2, :] if q < 2 else ring[:, 14:16, :]
        WC = 2 * 2 * 4 * D // T
        w_first = ring[:, 0:4, :].rearrange("p (q j) g -> p q j g", q=2)
        w_part = lambda w, t: w.rearrange("p q j g -> p (q j g)")[:, cols(t, WC)]
        agg_t = lambda u: ring[:, u, :]
        h_r = lambda u, j: ring[:, 2 + 2 * u + j, :]
        x_r = lambda u: ring[:, 6 + u, :].rearrange("p (b m f) -> p b m f", b=PAIR, m=NB)
        rows4 = lambda v: v.rearrange("p (q f) -> p q f", q=4)
        v_r = lambda u: ring[:, u, :]
        sq_r = lambda u: ring[:, 4 + u, :]
        xs_r = lambda u: ring[:, 8 + u, :]

        pr = lambda j: ring[:, j % 4, :]
        pt = lambda j: ring[:, 4 + j % 4, :]
        vr = lambda u: ring[:, 10 + u, :]

        Q_AT, K_AT, V_AT, OUT_AT, V_COPY_AT = 0, 1, 3, 5, 6
        EXP_LAG, NORM_LAG, TURN_LAG, TURN_COPY_LAG, AV_LAG = 1, 2, 3, 3, 5

        def unit(t, u, j, lag, total):
            back = 1 if j >= lag else 2
            if isinstance(t, int) and not 0 <= t - back < total:
                return None
            return t - back, (u - back) % 2, (j - lag) % 8

        def win(x, p, i, c):
            if p == 1:
                return x[:, cols(c, 512)]
            if p == 3:
                v = x[:, cols(c, 4 * N)].rearrange("f (b w) -> f w b", b=4)
                return v[:, i:3 * (N // 3):3, :]
            return x[:, cols(c, 512 * p)].rearrange("f (w p) -> f w p", p=p)[:, :, i]

        LOOPS = []
        n_item = n_prod = n_gate = 0
        GATES_BEFORE = {}
        LENGTH_END = []
        last = {}
        for p in range(1, STEPS + 1):
            chunks = {1: TOK // 512, 2: TOK // 1024, 3: B // 4, 4: TOK // 2048}[p]
            width = 4 * (N // 3) if p == 3 else 512
            half = chunks // 2
            steps = [(i, 0, chunks) for i in range(p)]
            if p == 2:
                steps = [(i, g * half, half) for g in range(2) for i in range(p)]
            if p == 3:
                steps = [(0, 0, half), (0, half, half), (1, 0, chunks), (2, 0, chunks)]
            for i, c0, n in steps:
                if i:
                    need = [last[p, c0 + c] for c in range(n)]
                elif p > 1:
                    need = [last[p - 1, c0 + c] if p == 3 else last[p - 1, 2 * (c0 + c) + 1] for c in range(n)]
                else:
                    need = [0, 0]
                f = need[1] - need[0]
                assert all(need[0] + f * c == x for c, x in enumerate(need))
                LOOPS.append((p, i, c0, n, c0 if p == 3 else 0, width, n_item, n_prod, n_gate, (f, need[0])))
                n_gate += n * (4 if i else 3)
                GATES_BEFORE[n_item + n] = 4 if i else 3
                for c in range(n):
                    last[p, c0 + c] = n_item + c + 1
                n_item += n
                n_prod += n if i else 0
            LENGTH_END.append(n_gate)

        def shaped(ap, p, width):
            ap = ap[:, 0:width]
            return ap.rearrange("f (w b) -> f w b", b=4) if p == 3 else ap

        N_E = 16 * (9 + HEADS)
        pool_steps = 0

        @block.sync
        def _(sp):
            for d, v in ((adjs[:, :, :], adj.rearrange("(b p) m -> p b m", p=P)),
                         (adjt[:, :, :], adj_t.rearrange("(b p) m -> p b m", p=P))):
                sp.dma_start(d, v).then_inc(s["in_adj"], 16)
            sp.dma_start(w1[:, :], w1_t).then_inc(s["in_w1"], 16)


            def load(t, u, k):
                if past(t, 2):
                    sp.wait_ge(s["agg_ready"], t - 1)
                src_ap = x_tok[t * PAIR:(t + 1) * PAIR] if isinstance(t, int) else x_tok[bass.ds(t * PAIR, PAIR)]
                for b in range(PAIR):
                    sp.dma_start(x_r(u)[:, b], src_ap[b].rearrange("(m p) f -> p m f", p=P)).then_inc(s[f"xa{u}"], 16)
            over(sp, T, 0, load)
            for d, v in ((w2[:, :, :], w2_t.rearrange("(b p) m -> p b m", p=P)),
                         (wg[:, 0, :], wg0), (wg[:, 1, :], wg1)):
                sp.dma_start(d, v).then_inc(s["in_w2"], 16)
            for c in range(4):
                sp.dma_start(X[:, c * TOK // 4:(c + 1) * TOK // 4],
                             x_feat[:, c * TOK // 4:(c + 1) * TOK // 4]).then_inc(s["in_x"], 16)
            for d, v in ((wqkv[:, :], w_qkv), (wlin[:, :], w_lin_t), (wval[:, :], w_val_t), (wout[:, :], w_out_t)):
                sp.dma_start(d, v).then_inc(s["in_w"], 16)

            sp.wait_ge(s["ln1"], T)
            for q in range(STEPS):
                if q == 2:
                    sp.wait_ge(s["z1_done"], T)
                if q == 3:
                    sp.wait_ge(s["w_l"], T + 2)
                for j, v in enumerate((wih_t, whh_t)):
                    sp.dma_start(w_stage(q)[:, j], v[q]).then_inc(s["in_wl"], 16)

            def stack(t, u, k):
                for name in ("q_hi", "k_hi", "q_lo", "k_lo"):
                    sp.wait_ge(s[name], t + 1)
                for h in range(HEADS):
                    if h % 2 == 0 and past(t, 2):
                        sp.wait_ge(s["s_done"], 8 * t + (4 * (h // 2) - 12))
                    for r, (q, w) in enumerate(((0, 2), (0, 3), (1, 2), (1, 3))):
                        sp.dma_start(stk[r * DH:(r + 1) * DH, u, :, h, :].bitcast(F32),
                                     spl[h * DH:(h + 1) * DH, u, q:w + 1:w - q, :].bitcast(F32))\
                            .then_inc(s[f"stk{h // 2}{u}"], 16)
            over(sp, T, 0, stack)

            def store(t, u, k):
                sp.wait_ge(s["o_fin"], t + 1)
                dst_ap = out[t * PAIR:(t + 1) * PAIR] if isinstance(t, int) else out[bass.ds(t * PAIR, PAIR)]
                for b in range(PAIR):
                    sp.dma_start(dst_ap[b].rearrange("(m p) f -> p m f", p=P),
                                 ring[:, 14 + u, :].rearrange("p (b m f) -> p b m f", b=PAIR, m=NB)[:, b])\
                        .then_inc(s[f"out{u}"], 16)
            over(sp, T, 0, store)
            for u in range(2):
                sp.wait_ge(s[f"out{u}"], 16 * PAIR * T // 2)

        @block.gpsimd
        def _(pool):
            nonlocal pool_steps
            n = 0

            def made(ins):
                nonlocal n
                n += 1
                ins.then_inc(s["pool_c"], 1)
                pool.wait_ge(s["pool_c"], n)

            for d, v in ((col1[:, :, :], cols1), (col2[:, :], cols2), (bi[:, :, :], bih), (bh[:, :, :], bhh),
                         (eci[:, :, :], edge_cols)):
                pool.dma_start(d, v).then_inc(s["in_e"], 16)
            for j, v in enumerate((bg0, bg1)):
                pool.dma_start(bgb[:, j, 0, :], v.rearrange("(a f) -> a f", a=1).to_broadcast([P, D]))\
                    .then_inc(s["in_e"], 16)
            for j, v in enumerate((src, dst)):
                pool.dma_start(ei[:, j, :], v.rearrange("(a f) -> a f", a=1).to_broadcast([P, E]))\
                    .then_inc(s["in_e"], 16)
            made(pool.memset(abd[:, :], 0.0))
            for h in range(HEADS):
                pool.dma_start(abd[h * DH:(h + 1) * DH, h:h + 1], a[h].rearrange("(p o) -> p o", o=1))\
                    .then_inc(s["in_e"], 16)
            made(pool.memset(ident[:, :], 0.0))
            made(pool.affine_select(out=ident[:, :], in_=ident[:, :], compare_op=ALU.not_equal, fill=1.0, base=0,
                                    pattern=[[-1, P]], channel_multiplier=1))
            made(pool.memset(ones[:, :], 1.0))
            made(pool.memset(mean1[:, :], 1.0 / D))
            made(pool.memset(cst[:, 0:1], EPS))
            made(pool.memset(cst[:, 1:2], LOG_EPS))
            made(pool.iota(ioi[:, :], pattern=[[1, E]], base=0, channel_multiplier=0))
            made(pool.iota(ioci[:, :], pattern=[[P, EB]], base=0, channel_multiplier=1))
            pool_steps = n

            def copies(ln, slot_free, ready):
                def body(t, u, k):
                    pool.wait_ge(s[ln], t + 1)
                    if past(t, 2):
                        pool.wait_ge(s[slot_free], t - 1)
                    pool.tensor_copy(xs_r(u), X[:, cols(t, W)]).then_inc(s[ready], 1)
                over(pool, T, 0, body)
            copies("ln1", "y0_done", "xs_g")

            for q in (2, 3):
                pool.wait_ge(s["in_wl"], 32 * q + 32)
                pool.wait_ge(s["gates_ready"], LENGTH_END[q - 2])
                for j in range(2):
                    m = 2 * (q - 2) + j + 1
                    pool.tensor_copy(w_hi[:, q % 2, j], w_stage(q)[:, j]).then_inc(s["w_h"], 1)
                    pool.wait_ge(s["w_h"], T + m)
                    pool.tensor_tensor(w_lo[:, q % 2, j], w_stage(q)[:, j], w_hi[:, q % 2, j].bitcast(F32),
                                       ALU.subtract).then_inc(s["w_l"], 1)
            copies("ln2", "v_pe", "xs_a")
            copies("ln3", "xqv", "xs_e")
            pool.wait_ge(s["xqv"], T)
            copies("ln3", "o_pe", "xs_o")


        at = {}

        @block.vector
        def _(dve):
            n = 0

            def link(ins, name=None):
                nonlocal n
                n += 1
                ins.then_inc(s["dch"], 1)
                dve.wait_ge(s["dch"], n)
                if name:
                    at[name] = n

            dve.wait_ge(s["in_adj"], 32)
            dve.wait_ge(s["in_e"], N_E)
            dve.wait_ge(s["pool_c"], pool_steps)

            link(dve.tensor_reduce(deg[:, 0:2], adjs[:, :, :], AX_X, ALU.add))
            link(dve.tensor_reduce(deg[:, 2:4], adjt[:, :, :], AX_X, ALU.add))
            for m in range(NB):
                link(dve.tensor_tensor_reduce(ttr[:, 0:P], adjs[:, m, m * P:(m + 1) * P], ident[:, :], 1.0, 0.0,
                                              ALU.mult, ALU.add, deg[:, 4 + m:5 + m]))
            link(dve.tensor_tensor(deg[:, 0:2], deg[:, 0:2], deg[:, 2:4], ALU.add))
            link(dve.tensor_tensor(deg[:, 0:2], deg[:, 0:2], deg[:, 4:6], ALU.subtract))
            link(dve.tensor_scalar(deg[:, 4:6], deg[:, 0:2], 1.0, None, ALU.add), "deg")
            dve.wait_ge(s["ach"], 1)
            link(dve.reciprocal(dinv[:, :], deg[:, 6:8]))
            for m in range(NB):
                link(dve.tensor_scalar(dgs[:, m, :], ident[:, :], dinv[:, m:m + 1], None, ALU.mult), "diag")
            for m in range(NB):
                link(dve.tensor_copy(aht[:, m, :], adjt[:, m, :]))
                link(dve.tensor_tensor(aht[:, m, m * P:(m + 1) * P], adjt[:, m, m * P:(m + 1) * P], ident[:, :],
                                       ALU.add))
            dve.wait_ge(s["setup_pe"], 1)
            for m in range(NB):
                link(dve.scalar_tensor_tensor(aht[:, m, :], aht[:, m, :], dinv[:, m:m + 1], bank[7][:, 0:N],
                                              ALU.mult, ALU.mult), "aht")

            for m in range(NB):
                for h in range(2):
                    link(dve.tensor_scalar(mbias[:, m, h, :], adjs[:, m, :], 0.0, NEG, ALU.is_equal, ALU.mult))
            link(dve.tensor_copy(identb[:, :], ident[:, :]))
            link(dve.tensor_tensor(cent[:, :], ident[:, :], mean1[:, :], ALU.subtract))
            link(dve.tensor_tensor(bl[:, :, :], bi[:, :, :], bh[:, :, :], ALU.add))

            for j in range(2):
                link(dve.tensor_copy(er[:, j, :], ei[:, j, :]))
                link(dve.tensor_copy(ec[:, j, :], eci[:, j, :]))
            link(dve.tensor_copy(iof[:, :], ioi[:, :]))
            link(dve.tensor_copy(ioc[:, :], ioci[:, :]))
            link(dve.scalar_tensor_tensor(keyr[:, :], er[:, 0, :], float(E), iof[:, :], ALU.mult, ALU.add))
            link(dve.scalar_tensor_tensor(keyc[:, :], ec[:, 0, :], float(E), ioc[:, :], ALU.mult, ALU.add))
            for e in range(EB):
                link(dve.tensor_scalar(ttr[:, :], keyr[:, :], keyc[:, e:e + 1], None, ALU.is_lt, ALU.add,
                                       accum_out=rank[:, e:e + 1]))
                link(dve.tensor_scalar(perm[:, e, :], iof[:, :], rank[:, e:e + 1], None, ALU.is_equal))
                for j in range(2):
                    link(dve.tensor_scalar(bc[:, j, e, :], ones[:, :], ec[:, j, e:e + 1], None, ALU.mult), "perm")
            def stats1(t, u, k):
                dve.wait_ge(s["h_stored"], t + 1)
                for j in range(HB):
                    ins = dve.bn_stats(st1[:, j, cols(t, 6)], HID[j][:, cols(t, W)])
                ins.then_inc(s["stat1"], 1)
            over(dve, T, 0, stats1)
            dve.wait_ge(s["stat1"], T)
            for j in range(HB):
                ins = dve.bn_aggr(bn[:, j, 0:2], st1[:, j, :])
            ins.then_inc(s["stat1"], 1)
            dve.wait_ge(s["ach"], 2)
            link(dve.reciprocal(bn[:, 0:2, 3], bn[:, 0:2, 2]))
            link(dve.tensor_tensor(bn[:, 0:2, 4], bn[:, 0:2, 3], col1[:, 1, :], ALU.mult))
            link(dve.tensor_tensor(bn[:, 0:2, 6], bn[:, 0:2, 0], bn[:, 0:2, 4], ALU.mult))
            dve.tensor_tensor(bn[:, 0:2, 5], col1[:, 2, :], bn[:, 0:2, 6], ALU.subtract).then_inc(s["bn1"], 1)

            dve.wait_ge(s["setup_pe"], 2)
            for j in range(2):
                link(dve.tensor_copy(srow[:, j, :], bank[6][:, j * E:(j + 1) * E]))
                link(dve.tensor_copy(scol[:, j, :], bank[7][:, j * EB:(j + 1) * EB]))
            for m in range(NB):
                link(dve.tensor_scalar(srct[:, m, :], srow[:, 0, :], ioc[:, m:m + 1], None, ALU.is_equal))
                link(dve.tensor_scalar(dst1[:, m, :], srow[:, 1, :], ioc[:, m:m + 1], None, ALU.is_equal))
                link(dve.tensor_tensor(sum1[:, m, :], srct[:, m, :], dst1[:, m, :].bitcast(F32), ALU.add), "srct")
            for e in range(EB):
                link(dve.tensor_scalar(src1[:, e, :], iof[:, :], scol[:, 0, e:e + 1], None, ALU.is_equal))
                link(dve.tensor_scalar(dstc[:, e, :], iof[:, :], scol[:, 1, e:e + 1], None, ALU.is_equal))
            link(dve.tensor_copy(srk[:, :], srow[:, 0, :]))

            def stats2(t, u, k):
                dve.wait_ge(s["o_stored"], t + 1)
                dve.bn_stats(st2[:, cols(t, 6)], O[:, cols(t, W)]).then_inc(s["stat2"], 1)
            over(dve, T, 0, stats2)
            dve.wait_ge(s["stat2"], T)
            dve.bn_aggr(bn[:, 2, 0:2], st2[:, :]).then_inc(s["stat2"], 1)
            dve.wait_ge(s["ach"], 3)
            link(dve.reciprocal(bn[:, 2, 3:4], bn[:, 2, 2:3]))
            link(dve.tensor_tensor(bn[:, 2, 4:5], bn[:, 2, 3:4], col2[:, 1:2], ALU.mult))
            link(dve.tensor_tensor(bn[:, 2, 6:7], bn[:, 2, 0:1], bn[:, 2, 4:5], ALU.mult))
            link(dve.tensor_tensor(bn[:, 2, 5:6], col2[:, 2:3], bn[:, 2, 6:7], ALU.subtract))

            def norm(r, add):
                def body(t, u, k):
                    if inside(t, T):
                        if past(t, 4):
                            dve.wait_ge(s["cen" + r], t - 3)
                        add(t, u).then_inc(s["v" + r], 1)
                    old = older(t, u, k, 3, T, 4)
                    if old:
                        t3, u3, _ = old
                        dve.wait_ge(s["rs" + r], t3 + 1)
                        dve.tensor_tensor(X[:, cols(t3, W)], bank[u3][:, :], sq_r(u3), ALU.mult)\
                            .then_inc(s["ln" + r], 1)
                over(dve, T, 3, body, 8, unroll=4)

            def add1(t, u):
                dve.tensor_scalar(v_r(u), O[:, cols(t, W)], bn[:, 2, 4:5], bn[:, 2, 5:6], ALU.mult, ALU.add)\
                    .then_inc(s["tmp_ready"], 1)
                dve.wait_ge(s["tmp_ready"], t + 1)
                return dve.tensor_tensor(v_r(u), v_r(u), X[:, cols(t, W)], ALU.add)
            dve.wait_ge(s["setup_pe"], 3)
            for e in range(EB):
                link(dve.tensor_tensor(ttr[:, :], bank[7][:, e * N:(e + 1) * N], dstc[:, e, :], ALU.mult))
                link(dve.tensor_reduce(lacol[:, e:e + 1], ttr[:, :], AX_X, ALU.add), "adje")

            dve.wait_ge(s["in_x"], 64)
            norm("1", add1)
            def gcn(t, u, k):
                old = older(t, u, k, 3, T)
                if old:
                    t3, u3, _ = old
                    dve.wait_ge(s["z1_copied"], t3 + 1)
                    hi = hl_hi[:, cols(t3, W)].bitcast(F32)
                    dve.scalar_tensor_tensor(hl_lo[:, cols(t3, W)], bank[6 + u3][:, :], 0.0, hi, ALU.max, ALU.subtract)\
                        .then_inc(s["z1_low"], 1)
                    dve.wait_ge(s["w_h"], t3 + 1)
                    dve.tensor_tensor(w_part(w_lo, t3), w_part(w_first, t3), w_part(w_hi, t3).bitcast(F32),
                                      ALU.subtract).then_inc(s["w_l"], 1)
                old = older(t, u, k, 2, T)
                if old:
                    t2, u2, _ = old
                    dve.wait_ge(s["y1_done"], t2 + 1)
                    if past(t2, 2):
                        dve.wait_ge(s["z1_done"], t2 - 1)
                    dve.tensor_tensor(rows4(ring[:, 14 + u2, :]), rows4(bank[4 + u2][:, :]),
                                      bgb[:, 1].to_broadcast([P, 4, D]), ALU.add).then_inc(s["y1_copied"], 1)
                if inside(t, T):
                    dve.wait_ge(s["y0_done"], t + 1)
                    if past(t, 2):
                        dve.wait_ge(s["z0_done"], t - 1)
                    dve.tensor_tensor(rows4(ring[:, 10 + u, :]), rows4(bank[u][:, :]),
                                      bgb[:, 0].to_broadcast([P, 4, D]), ALU.add).then_inc(s["y0_copied"], 1)
            over(dve, T, 3, gcn)

            def lstm(p, i, c0, chunks, cell0, width, base, base2, gates, _):
                n = 3 if i == 0 else 4

                def body(c, u, k):
                    old, new = older(c, u, k, 1, chunks), inside(c, chunks)
                    if old:
                        c1, u1, _ = old
                        if i == p - 1:
                            hi, lo = (win(x, p, i, c1 + c0) for x in (hl_hi, hl_lo))
                        else:
                            hi, lo = (x[:, cols(c1 + cell0, width)] for x in (hs_hi, hs_lo))
                        h = ring[:, 8 + u1, :]
                        h_shaped = shaped(h, p if i == p - 1 else 1, width)
                        dve.wait_ge(s["tc_ready"], c1 + (base + 1))
                        dve.tensor_tensor(h[:, 0:width], ring[:, 6 + u1, 0:width], h[:, 0:width], ALU.mult)\
                            .then_inc(s["h_new"], 1)
                    if new:
                        dve.wait_ge(s["gates_read"], (c + 1) * n + gates)
                        cell = CELL[:, cols(u if p == 1 else c + cell0, width)]
                        ig, gg, fg = (ring[:, 2 * g + u, 0:width] for g in (0, 2, 1))
                        if i:
                            dve.tensor_tensor(ring[:, 10 + u, 0:width], fg, cell, ALU.mult).then_inc(s["prod"], 1)
                            dve.tensor_tensor(ring[:, 12 + u, 0:width], ig, gg, ALU.mult).then_inc(s["prod"], 1)
                        else:
                            dve.tensor_tensor(cell, ig, gg, ALU.mult).then_inc(s["c_done"], 1)
                    if old:
                        dve.wait_ge(s["h_new"], c1 + (base + 1))
                        dve.tensor_copy(hi, h_shaped).then_inc(s["h_high"], 1)
                    if new and i:
                        dve.wait_ge(s["prod"], c * 2 + (2 * base2 + 2))
                        dve.tensor_tensor(cell, ring[:, 10 + u, 0:width], ring[:, 12 + u, 0:width], ALU.add)\
                            .then_inc(s["c_done"], 1)
                    if old:
                        dve.wait_ge(s["h_high"], c1 + (base + 1))
                        dve.tensor_tensor(lo, h_shaped, hi.bitcast(F32), ALU.subtract).then_inc(s["h_done"], 1)
                over(dve, chunks, 1, body, 2)
            for loop in LOOPS:
                lstm(*loop)
            dve.wait_ge(s["ach"], 4)
            for e in range(EB):
                link(dve.tensor_scalar(dgs[:, e, :], ident[:, :], lacol[:, 2 + e:3 + e], None, ALU.mult), "ladiag")
            dve.wait_ge(s["setup_pe"], 4)
            link(dve.tensor_copy(larow[:, :], bank[7][:, 0:E]))

            dve.wait_ge(s["h_done"], n_item)

            def add2(t, u):
                dve.tensor_tensor(v_r(u), X[:, cols(t, W)], hl_lo[:, cols(t, W)].bitcast(F32), ALU.add)\
                    .then_inc(s["tmp_ready"], 1)
                dve.wait_ge(s["tmp_ready"], t + (T + 1))
                return dve.tensor_tensor(v_r(u), v_r(u), hl_hi[:, cols(t, W)].bitcast(F32), ALU.add)
            norm("2", add2)

            def attend(t, u, k):
                for j in range(8):
                    w = unit(t, u, j, 0, T)
                    if w:
                        t0, _, j0 = w
                        dve.wait_ge(s["s_done"], 8 * t0 + (j0 + 1))
                        dve.tensor_reduce(den[:, j0, 0:2], bank[3 + j0 % 2][:, :].rearrange("p (h n) -> p h n", h=2),
                                          AX_X, ALU.max, negate=True).then_inc(s["mx"], 1)
                    w = unit(t, u, j, NORM_LAG, T)
                    if w:
                        t1, _, j1 = w
                        dve.wait_ge(s["ex"], 8 * t1 + (j1 + 1))
                        dve.reciprocal(den[:, j1, 4:6], den[:, j1, 2:4]).then_inc(s["rc"], 1)
                        dve.wait_ge(s["rc"], 8 * t1 + (j1 + 1))
                        for h in range(2):
                            ins = dve.tensor_scalar(pr(j1)[:, h * N:(h + 1) * N], pr(j1)[:, h * N:(h + 1) * N],
                                                    den[:, j1, 4 + h:5 + h], None, ALU.mult)
                        ins.then_inc(s["nrm"], 1)
                    if j == OUT_AT:
                        old = older(t, u, k, 2, T)
                        if old:
                            dve.wait_ge(s["av"], 8 * old[0] + 8)
                            dve.tensor_copy(att_out[:, cols(old[0], W)], bank[7 - 5 * old[1]][:, :]).then_inc(s["av_c"], 1)
                    for at_j, pe_done, hi, lo, x, scale in ((Q_AT, "q_pe", "q_hi", "q_lo", 0, DH ** -0.5),
                                                            (K_AT, "k_pe", "k_hi", "k_lo", 1, 1.0)):
                        if j == at_j and inside(t, T):
                            dve.wait_ge(s[pe_done], t + 1)
                            dve.wait_ge(s[hi], t + 1)
                            if past(t, 2):
                                for g in range(2):
                                    dve.wait_ge(s[f"stk{g}{u}"], k * 128)
                            dve.scalar_tensor_tensor(spl[:, u, 2 * x + 1, :], bank[x][:, :], scale,
                                                     spl[:, u, 2 * x, :].bitcast(F32), ALU.mult, ALU.subtract)\
                                .then_inc(s[lo], 1)
            over(dve, T, 2, attend, 4)
            dve.wait_ge(s["av_c"], T)
            norm("3", lambda t, u: dve.tensor_tensor(v_r(u), X[:, cols(t, W)], att_out[:, cols(t, W)], ALU.add))

            def edges(t, u, k):
                if inside(t, T):
                    dve.wait_ge(s["xq_c"], t + 1)
                    dve.tensor_tensor(e_lo[:, u, :], bank[u][:, :], e_hi[:, u, :].bitcast(F32), ALU.subtract)\
                        .then_inc(s["xq_l"], 1)
                    dve.wait_ge(s["xv_c"], t + 1)
                    dve.tensor_tensor(vv_lo[:, cols(t, W)], bank[2 + u][:, :], vv_hi[:, cols(t, W)].bitcast(F32),
                                      ALU.subtract).then_inc(s["xv_l"], 1)
                old = older(t, u, k, 1, T)
                if old:
                    t1, u1, _ = old
                    dve.wait_ge(s["z_c"], t1 + 1)
                    if past(t1, 2):
                        dve.wait_ge(s["e_done"], t1 - 1)
                    dve.tensor_tensor(ring[:, 14 + u1, :], bank[4 + u1][:, :], ring[:, 12 + u1, :], ALU.max)\
                        .then_inc(s["lr"], 1)
                old = older(t, u, k, 2, T)
                if old:
                    t2, u2, _ = old
                    dve.wait_ge(s["e_done"], t2 + 1)
                    dve.tensor_copy(ET[:, :, cols(t2, PAIR * HEADS)],
                                    bank[6 + u2][:, 0:EB * PAIR * HEADS].rearrange("p (e c) -> p e c", e=EB))\
                        .then_inc(s["e_c"], 1)
            over(dve, T, 2, edges)

            link(dve.tensor_tensor(same[:, 5, 1:E], srk[:, 1:E], srk[:, 0:E - 1], ALU.not_equal))
            for j in range(2):
                link(dve.memset(same[:, j, :], NEG))
                link(dve.memset(same[:, 2 + j, :], 0.0))
            link(dve.tensor_scalar(same[:, 0, 1:E], same[:, 5, 1:E], NEG, None, ALU.mult))
            link(dve.tensor_scalar(same[:, 1, 0:E - 1], same[:, 5, 1:E], NEG, None, ALU.mult))
            link(dve.tensor_scalar(same[:, 2, 1:E], same[:, 5, 1:E], -1.0, 1.0, ALU.mult, ALU.add))
            link(dve.tensor_scalar(same[:, 3, 0:E - 1], same[:, 5, 1:E], -1.0, 1.0, ALU.mult, ALU.add))
            link(dve.tensor_scalar(same[:, 4, :], same[:, 3, :], -1.0, 1.0, ALU.mult, ALU.add))

            def scan(o, x, y, first, op0, op1, back):
                v = (lambda z: z[:, ::-1]) if back else (lambda z: z)
                return dve.tensor_tensor_scan(v(o), v(x), v(y), first, op0, op1)
            dve.wait_ge(s["tr_e"], 1)
            link(dve.tensor_tensor(sm[:, 0, :], bank[0][:, 0:E], larow[:, :], ALU.add))
            link(scan(sm[:, 1, :], same[:, 0, :], sm[:, 0, :], NEG, ALU.add, ALU.max, False))
            link(scan(sm[:, 2, :], same[:, 1, :], sm[:, 1, :], NEG, ALU.add, ALU.max, True))
            dve.tensor_tensor(sm[:, 1, :], sm[:, 0, :], sm[:, 2, :], ALU.subtract).then_inc(s["sm_e"], 1)
            dve.wait_ge(s["exd"], 1)
            link(scan(sm[:, 0, :], same[:, 2, :], sm[:, 2, :], 0.0, ALU.mult, ALU.add, False))
            link(dve.tensor_tensor(sm[:, 1, :], sm[:, 0, :], same[:, 4, :], ALU.mult))
            link(scan(sm[:, 0, :], same[:, 3, :], sm[:, 1, :], 0.0, ALU.mult, ALU.add, True))
            link(dve.reciprocal(sm[:, 1, :], sm[:, 0, :]))
            dve.tensor_tensor(sm[:, 3, :], sm[:, 2, :], sm[:, 1, :], ALU.mult).then_inc(s["att"], 1)
            dve.wait_ge(s["tr_a"], 1)
            dve.tensor_copy(AT[:, :, :], bank[6][:, 0:EB * P].rearrange("p (e c) -> p e c", e=EB)).then_inc(s["at_c"], 1)
            dve.wait_ge(s["at_c"], 1)

            def rows(t, u, k):
                if inside(t, T):
                    dve.wait_ge(s["vt"], t + 1)
                    if past(t, 2):
                        dve.wait_ge(s["vt_l"], t - 1)
                    for e in range(EB):
                        w = AT[:, e, cols(t, PAIR * HEADS)].rearrange("p (c o) -> p c o", o=1)
                        ins = dve.tensor_tensor(ring[:, 10 + u % 2, e * 256:(e + 1) * 256].rearrange("p (c d) -> p c d", d=DH),
                                                bank[u % 2][:, e * 256:(e + 1) * 256].rearrange("p (c d) -> p c d", d=DH),
                                                w.to_broadcast([P, PAIR * HEADS, DH]), ALU.mult)
                    ins.then_inc(s["vt_c"], 1)
                old = older(t, u, k, 1, T, 4)
                if old:
                    t1, u1, _ = old
                    dve.wait_ge(s["vt_h"], t1 + 1)
                    dve.tensor_tensor(e_lo[:, 2 + u1 % 2, :], ring[:, 10 + u1 % 2, :], e_hi[:, 2 + u1 % 2, :].bitcast(F32),
                                      ALU.subtract).then_inc(s["vt_l"], 1)
                old = older(t, u, k, 4, T, 4)
                if old:
                    t4, u4, _ = old
                    dve.wait_ge(s["rso"], t4 + 1)
                    dve.scalar_tensor_tensor(fin[:, u4, 8:12], mv[:, u4, :, 0], -1.0, fin[:, u4, 4:8], ALU.mult, ALU.mult)\
                        .then_inc(s["nm"], 1)
                old = older(t, u, k, 3, T, 4)
                if old:
                    t3, u3, _ = old
                    dve.wait_ge(s["o_pe"], t3 + 1)
                    for q in range(4):
                        ins = dve.bn_stats(bst[:, u3 % 2, q, :], bank[4 + u3][:, q * P:(q + 1) * P])
                    ins.then_inc(s["bs"], 1)
                    dve.wait_ge(s["bs"], t3 + 1)
                    dve.sem_inc(s["aggr_on"], 1)
                    for q in range(4):
                        ins = dve.bn_aggr(mv[:, u3, q, :], bst[:, u3 % 2, q, :])
                    ins.then_inc(s["st3"], 1)
            over(dve, T, 4, rows, 8, unroll=4)

        @block.scalar
        def _(act):
            n = 0

            def link(ins):
                nonlocal n
                n += 1
                ins.then_inc(s["ach"], 1)
                act.wait_ge(s["ach"], n)

            act.preload_act_table_set("sqrt_and_others")
            act.wait_ge(s["dch"], at["deg"])
            link(act.activation(deg[:, 6:8], deg[:, 4:6], ACT.Sqrt))

            def agg(t, u, k):
                if inside(t, T):
                    act.wait_ge(s["agg_ready"], t + 1)
                    if past(t, 2):
                        act.wait_ge(s["hpre_ready"], t - 1)
                    act.activation(agg_t(u), bank[u][:, :], ACT.Copy).then_inc(s["agg_copied"], 1)
                old = older(t, u, k, 1, T)
                if old:
                    t1, u1, _ = old
                    act.wait_ge(s["hpre_ready"], t1 + 1)
                    for j in range(HB):
                        ins = act.activation(HID[j][:, cols(t1, W)], bank[2 + 2 * u1 + j][:, :], ACT.Identity,
                                             bias=col1[:, 0, j:j + 1])
                    ins.then_inc(s["h_stored"], 1)
            act.wait_ge(s["in_e"], N_E)
            over(act, T, 1, agg)

            act.wait_ge(s["stat1"], T + 1)
            link(act.activation(bn[:, 0:2, 2], bn[:, 0:2, 1], ACT.Sqrt, bias=cst[:, 0:1]))
            act.wait_ge(s["bn1"], 1)

            def layer2(t, u, k):
                if inside(t, T):
                    if past(t, 2):
                        act.wait_ge(s["w2_done"], t - 1)
                    for j in range(HB):
                        ins = act.activation(h_r(u, j), HID[j][:, cols(t, W)], ACT.Relu, scale=bn[:, j, 4:5],
                                             bias=bn[:, j, 5:6])
                    ins.then_inc(s["relu_ready"], 1)
                old = older(t, u, k, 1, T)
                if old:
                    t1, u1, _ = old
                    act.wait_ge(s["w2_done"], t1 + 1)
                    act.activation(O[:, cols(t1, W)], bank[u1][:, :], ACT.Identity, bias=col2[:, 0:1])\
                        .then_inc(s["o_stored"], 1)
            over(act, T, 1, layer2)

            act.wait_ge(s["stat2"], T + 1)
            link(act.activation(bn[:, 2, 2:3], bn[:, 2, 1:2], ACT.Sqrt, bias=cst[:, 0:1]))

            def norm(r):
                def body(t, u, k):
                    if inside(t, T):
                        act.wait_ge(s["cen" + r], t + 1)
                        if past(t, 4):
                            act.wait_ge(s["ln" + r], t - 3)
                        act.activation(sq_r(u), bank[u][:, :], ACT.Square).then_inc(s["sq" + r], 1)
                    old = older(t, u, k, 1, T, 4)
                    if old:
                        t1, u1, _ = old
                        act.wait_ge(s["var" + r], t1 + 1)
                        act.activation(sq_r(u1), bank[4 + u1][:, :], ACT.Ln, bias=cst[:, 0:1])\
                            .then_inc(s["lg" + r], 1)
                        act.wait_ge(s["lg" + r], t1 + 1)
                        act.activation(sq_r(u1), sq_r(u1), ACT.Exp, scale=-0.5).then_inc(s["rs" + r], 1)
                over(act, T, 1, body, unroll=4)
            act.preload_act_table_set("natural_log_exp_and_others")
            norm("1")
            act.wait_ge(s["dch"], at["adje"])
            link(act.activation(lacol[:, 2:4], lacol[:, 0:2], ACT.Ln, bias=cst[:, 1:2]))

            act.wait_ge(s["in_wl"], 64)
            def gcn(t, u, k):
                old = older(t, u, k, 3, T)
                if old:
                    t3, u3, _ = old
                    act.wait_ge(s["z1_done"], t3 + 1)
                    act.activation(hl_hi[:, cols(t3, W)], bank[6 + u3][:, :], ACT.Relu).then_inc(s["z1_copied"], 1)
                    act.activation(w_part(w_hi, t3), w_part(w_first, t3), ACT.Copy).then_inc(s["w_h"], 1)
                old = older(t, u, k, 1, T)
                if old:
                    t1, u1, _ = old
                    act.wait_ge(s["z0_done"], t1 + 1)
                    if past(t1, 2):
                        act.wait_ge(s["y1_done"], t1 - 1)
                    act.activation(ring[:, 12 + u1, :], bank[2 + u1][:, :], ACT.Relu).then_inc(s["z0_copied"], 1)
            over(act, T, 3, gcn)

            def lstm(p, i, c0, chunks, cell0, width, base, _, gates, need):
                order = (0, 2, 3) if i == 0 else (0, 2, 1, 3)
                n = len(order)

                def body(c, u, k):
                    if inside(c, chunks):
                        for q, g in enumerate(order):
                            act.wait_ge(s["gates_ready"], c * n + (gates + q + 1))
                            if (past(c, 2) or base) and g == 0:
                                act.wait_ge(s["c_done"], c + (base - 1))
                            if (past(c, 2) or base) and g == 3:
                                act.wait_ge(s["h_new"], c + (base - 1))
                            act.activation(shaped(ring[:, 2 * g + u, :], p, width),
                                                 shaped(bank[2 * g + u][:, :], p, width),
                                                 ACT.Tanh if g == 2 else ACT.Sigmoid, bias=bl[:, p - 1, g:g + 1])\
                                .then_inc(s["gates_read"], 1)
                    old = older(c, u, k, 1, chunks)
                    if old:
                        c1, u1, _ = old
                        act.wait_ge(s["c_done"], c1 + (base + 1))
                        if past(c1, 2) or base:
                            act.wait_ge(s["h_done"], c1 + (base - 1))
                        act.activation(ring[:, 8 + u1, 0:width], CELL[:, cols(u1 if p == 1 else c1 + cell0, width)],
                                       ACT.Tanh)\
                            .then_inc(s["tc_ready"], 1)
                over(act, chunks, 1, body, 2)
            act.preload_act_table_set("sigmoid_and_others")
            for loop in LOOPS:
                lstm(*loop)
            act.preload_act_table_set("natural_log_exp_and_others")
            norm("2")

            def attend(t, u, k):
                for j in range(8):
                    w = unit(t, u, j, EXP_LAG, T)
                    if w:
                        t0, _, j0 = w
                        act.wait_ge(s["mx"], 8 * t0 + (j0 + 1))
                        if j0 >= 4 or past(t0, 1):
                            act.wait_ge(s["tp"], 8 * t0 + (j0 - 3))
                        for h in range(2):
                            ins = act.activation(pr(j0)[:, h * N:(h + 1) * N],
                                                 bank[3 + j0 % 2][:, h * N:(h + 1) * N], ACT.Exp,
                                                 bias=den[:, j0, h:h + 1], accum_out=den[:, j0, 2 + h:3 + h])
                        ins.then_inc(s["ex"], 1)
                    w = unit(t, u, j, TURN_COPY_LAG, T)
                    if w:
                        t2, _, j2 = w
                        act.wait_ge(s["tp"], 8 * t2 + (j2 + 1))
                        if j2 >= 4 or past(t2, 1):
                            act.wait_ge(s["av"], 8 * t2 + (j2 - 3))
                        act.activation(pt(j2), bank[5 + j2 % 2][:, :], ACT.Copy).then_inc(s["tp_c"], 1)
                    if j == V_COPY_AT and inside(t, T):
                        act.wait_ge(s["v_pe"], t + 1)
                        if past(t, 2):
                            act.wait_ge(s["av"], 8 * (t - 1))
                        act.activation(vr(u), bank[0][:, :], ACT.Copy).then_inc(s["v_c"], 1)
                    for at_j, pe_done, hi, x, scale in ((Q_AT, "q_pe", "q_hi", 0, DH ** -0.5),
                                                        (K_AT, "k_pe", "k_hi", 1, 1.0)):
                        if j == at_j and inside(t, T):
                            act.wait_ge(s[pe_done], t + 1)
                            if past(t, 2):
                                for g in range(2):
                                    act.wait_ge(s[f"stk{g}{u}"], k * 128)
                            act.activation(spl[:, u, 2 * x, :], bank[x][:, :], ACT.Copy, scale=scale)\
                                .then_inc(s[hi], 1)
            over(act, T, 2, attend, 4)
            norm("3")

            def edges(t, u, k):
                if inside(t, T):
                    act.wait_ge(s["xqv"], t + 1)
                    if past(t, 2):
                        act.wait_ge(s["z_done"], t - 1)
                    act.activation(e_hi[:, u, :], bank[u][:, :], ACT.Copy).then_inc(s["xq_c"], 1)
                    act.activation(vv_hi[:, cols(t, W)], bank[2 + u][:, :], ACT.Copy).then_inc(s["xv_c"], 1)
                old = older(t, u, k, 1, T)
                if old:
                    t1, u1, _ = old
                    act.wait_ge(s["z_done"], t1 + 1)
                    act.activation(ring[:, 12 + u1, :], bank[4 + u1][:, :], ACT.Copy, scale=SLOPE)\
                        .then_inc(s["z_c"], 1)
            over(act, T, 1, edges)

            act.wait_ge(s["sm_e"], 1)
            act.activation(sm[:, 2, :], sm[:, 1, :], ACT.Exp).then_inc(s["exd"], 1)

            def rows(t, u, k):
                if inside(t, T):
                    act.wait_ge(s["vt_c"], t + 1)
                    if past(t, 2):
                        act.wait_ge(s["yt"], t - 1)
                    act.activation(e_hi[:, 2 + u % 2, :], ring[:, 10 + u % 2, :], ACT.Copy).then_inc(s["vt_h"], 1)
                old = older(t, u, k, 2, T, 4)
                if old:
                    t2, u2, _ = old
                    act.wait_ge(s["yt"], t2 + 1)
                    if past(t2, 2):
                        act.wait_ge(s["o_pe"], t2 - 1)
                    act.activation(ring[:, 12 + u2 % 2, :], bank[2 + u2 % 2][:, :], ACT.Copy).then_inc(s["yt_c"], 1)
                old = older(t, u, k, 3, T, 4)
                if old:
                    t3, u3, _ = old
                    act.wait_ge(s["st3"], t3 + 1)
                    act.activation(fin[:, u3, 0:4], mv[:, u3, :, 1], ACT.Ln, bias=cst[:, 0:1]).then_inc(s["lgo"], 1)
                    act.wait_ge(s["lgo"], t3 + 1)
                    act.activation(fin[:, u3, 4:8], fin[:, u3, 0:4], ACT.Exp, scale=-0.5).then_inc(s["rso"], 1)
                old = older(t, u, k, 4, T, 4)
                if old:
                    t4, u4, k4 = old
                    act.wait_ge(s["nm"], t4 + 1)
                    if past(t4, 2):
                        act.wait_ge(s[f"out{u4 % 2}"], k4 * (32 * PAIR) + u4 // 2 * (16 * PAIR))
                    for q in range(4):
                        ins = act.activation(ring[:, 14 + u4 % 2, q * P:(q + 1) * P], bank[4 + u4][:, q * P:(q + 1) * P],
                                             ACT.Identity, scale=fin[:, u4, 4 + q:5 + q], bias=fin[:, u4, 8 + q:9 + q])
                    ins.then_inc(s["o_fin"], 1)
            over(act, T, 4, rows, 8, unroll=4)

        @block.tensor
        def _(pe):
            def mm(o, l, r, first=True, last=True):
                return pe.matmul(o, l, r, start=first, stop=last)

            pe.wait_ge(s["dch"], at["diag"])
            for m in range(NB):
                ins = mm(bank[7][:, m * P:(m + 1) * P], ones[:, :], dgs[:, m, :])
            ins.then_inc(s["setup_pe"], 1)

            pe.wait_ge(s["dch"], at["aht"])
            pe.wait_ge(s["in_w1"], 16)

            def agg(t, u, k):
                if inside(t, T):
                    pe.wait_ge(s[f"xa{u}"], 16 * PAIR * k + 16 * PAIR)
                    if past(t, 2):
                        pe.wait_ge(s["agg_copied"], t - 1)
                    for b in range(PAIR):
                        for m in range(NB):
                            ins = mm(bank[u][:, b * N:(b + 1) * N], x_r(u)[:, b, m, :], aht[:, m, :], m == 0, m == NB - 1)
                    ins.then_inc(s["agg_ready"], 1)
                old = older(t, u, k, 1, T)
                if old:
                    t1, u1, _ = old
                    pe.wait_ge(s["agg_copied"], t1 + 1)
                    if past(t1, 2):
                        pe.wait_ge(s["h_stored"], t1 - 1)
                    for j in range(HB):
                        ins = mm(bank[2 + 2 * u1 + j][:, :], w1[:, j * P:(j + 1) * P], agg_t(u1))
                    ins.then_inc(s["hpre_ready"], 1)
            over(pe, T, 1, agg)
            pe.wait_ge(s["dch"], at["perm"])
            for j in range(2):
                for e in range(EB):
                    mm(bank[6][:, j * E:(j + 1) * E], bc[:, j, e, :], perm[:, e, :], e == 0, e == EB - 1)
                for q in range(EB):
                    for e in range(EB):
                        ins = mm(bank[7][:, j * EB + q:j * EB + q + 1], perm[:, e, q * P:(q + 1) * P], ec[:, j, e:e + 1],
                                 e == 0, e == EB - 1)
            ins.then_inc(s["setup_pe"], 1)

            pe.wait_ge(s["in_w2"], 48)

            def layer2(t, u, k):
                if inside(t, T):
                    pe.wait_ge(s["relu_ready"], t + 1)
                    if past(t, 2):
                        pe.wait_ge(s["o_stored"], t - 1)
                    for j in range(HB):
                        ins = mm(bank[u][:, :], w2[:, j, :], h_r(u, j), j == 0, j == HB - 1)
                    ins.then_inc(s["w2_done"], 1)
            over(pe, T, 0, layer2)

            def norm(r):
                def body(t, u, k):
                    if inside(t, T):
                        pe.wait_ge(s["v" + r], t + 1)
                        if past(t, 4):
                            pe.wait_ge(s["ln" + r], t - 3)
                        mm(bank[u][:, :], cent[:, :], v_r(u)).then_inc(s["cen" + r], 1)
                    old = older(t, u, k, 1, T, 4)
                    if old:
                        t1, u1, _ = old
                        pe.wait_ge(s["sq" + r], t1 + 1)
                        if past(t1, 4):
                            pe.wait_ge(s["lg" + r], t1 - 3)
                        mm(bank[4 + u1][:, :], mean1[:, :], sq_r(u1)).then_inc(s["var" + r], 1)
                over(pe, T, 1, body, 8, unroll=4)
            pe.wait_ge(s["dch"], at["srct"])
            for e in range(EB):
                for m in range(NB):
                    ins = mm(bank[7][:, e * N:(e + 1) * N], srct[:, m, e * P:(e + 1) * P], adjs[:, m, :],
                             m == 0, m == NB - 1)
            ins.then_inc(s["setup_pe"], 1)
            pe.wait_ge(s["o_stored"], T)
            norm("1")

            def gcn(t, u, k):
                old = older(t, u, k, 3, T)
                if old:
                    t3, u3, _ = old
                    pe.wait_ge(s["y1_copied"], t3 + 1)
                    if past(t3, 2):
                        pe.wait_ge(s["z1_copied"], t3 - 1)
                        pe.wait_ge(s["z1_low"], t3 - 1)
                    for b in range(PAIR):
                        for m in range(NB):
                            ins = mm(bank[6 + u3][:, b * N:(b + 1) * N],
                                     ring[:, 14 + u3, (b * NB + m) * P:(b * NB + m + 1) * P], adjt[:, m, :],
                                     m == 0, m == NB - 1)
                    ins.then_inc(s["z1_done"], 1)
                old = older(t, u, k, 2, T)
                if old:
                    t2, u2, _ = old
                    pe.wait_ge(s["z0_copied"], t2 + 1)
                    if past(t2, 2):
                        pe.wait_ge(s["y1_copied"], t2 - 1)
                    for q in range(4):
                        ins = mm(bank[4 + u2][:, q * P:(q + 1) * P], ring[:, 12 + u2, q * P:(q + 1) * P], wg[:, 1, :])
                    ins.then_inc(s["y1_done"], 1)
                old = older(t, u, k, 1, T)
                if old:
                    t1, u1, _ = old
                    pe.wait_ge(s["y0_copied"], t1 + 1)
                    if past(t1, 2):
                        pe.wait_ge(s["z0_copied"], t1 - 1)
                    for b in range(PAIR):
                        for m in range(NB):
                            ins = mm(bank[2 + u1][:, b * N:(b + 1) * N],
                                     ring[:, 10 + u1, (b * NB + m) * P:(b * NB + m + 1) * P], adjt[:, m, :],
                                     m == 0, m == NB - 1)
                    ins.then_inc(s["z0_done"], 1)
                if inside(t, T):
                    pe.wait_ge(s["xs_g"], t + 1)
                    if past(t, 2):
                        pe.wait_ge(s["y0_copied"], t - 1)
                    for q in range(4):
                        ins = mm(bank[u][:, q * P:(q + 1) * P], xs_r(u)[:, q * P:(q + 1) * P], wg[:, 0, :])
                    ins.then_inc(s["y0_done"], 1)
            pe.wait_ge(s["ln1"], T)
            over(pe, T, 3, gcn)

            def lstm(p, i, c0, chunks, cell0, width, base, _, gates, need):
                order = (0, 2, 3) if i == 0 else (0, 2, 1, 3)
                n = len(order)

                if p > 2 and i == 0 and c0 == 0:
                    pe.wait_ge(s["w_l"], T + 2 * (p - 2))

                def body(c, u, k):
                    if p > 1:
                        pe.wait_ge(s["h_done"], c * need[0] + need[1])
                    for q, g in enumerate(order):
                        if past(c, 2):
                            pe.wait_ge(s["gates_read"], c * n + (gates + q + 1 - 2 * n))
                        elif base and q == 0:
                            pe.wait_ge(s["gates_read"], gates if c else gates - GATES_BEFORE[base])
                        o = shaped(bank[2 * g + u][:, :], p, width)
                        w = [x[:, (p - 1) % 2, 0, g * D:(g + 1) * D] for x in (w_hi, w_lo)]
                        x = [win(v, p, i, c + c0) for v in (hl_hi, hl_lo)]
                        mm(o, w[0], x[0], True, False)
                        mm(o, w[0], x[1], False, False)
                        ins = mm(o, w[1], x[0], False, i == 0)
                        if i:
                            o = bank[2 * g + u][:, 0:width]
                            w = [x[:, (p - 1) % 2, 1, g * D:(g + 1) * D] for x in (w_hi, w_lo)]
                            x = [v[:, cols(c + cell0, width)] for v in (hs_hi, hs_lo)]
                            mm(o, w[0], x[0], False, False)
                            mm(o, w[0], x[1], False, False)
                            ins = mm(o, w[1], x[0], False, True)
                        ins.then_inc(s["gates_ready"], 1)
                over(pe, chunks, 0, body)
            pe.wait_ge(s["z1_copied"], T)
            pe.wait_ge(s["z1_low"], T)
            pe.wait_ge(s["w_l"], T)
            pe.wait_ge(s["in_w"], 64)
            for loop in LOOPS:
                lstm(*loop)
            pe.wait_ge(s["gates_read"], n_gate)
            pe.wait_ge(s["dch"], at["ladiag"])
            for e in range(EB):
                ins = mm(bank[7][:, e * P:(e + 1) * P], ones[:, :], dgs[:, e, :])
            ins.then_inc(s["setup_pe"], 1)
            norm("2")

            def attend(t, u, k):
                for j in range(8):
                    for at_j, x, done in ((Q_AT, 0, "q_pe"), (K_AT, 1, "k_pe")):
                        if j == at_j and inside(t, T):
                            pe.wait_ge(s["xs_a"], t + 1)
                            if x == 0 and past(t, 1):
                                pe.wait_ge(s["v_c"], t)
                            if x == 1 and past(t, 1):
                                for name in ("k_hi", "k_lo"):
                                    pe.wait_ge(s[name], t)
                            mm(bank[x][:, :], wqkv[:, x * D:(x + 1) * D], xs_r(u)).then_inc(s[done], 1)
                    if j == V_AT and inside(t, T):
                        for name in ("q_hi", "q_lo"):
                            pe.wait_ge(s[name], t + 1)
                        for q in range(4):
                            ins = mm(bank[0][:, q * P:(q + 1) * P], xs_r(u)[:, q * P:(q + 1) * P], wqkv[:, 2 * D:3 * D])
                        ins.then_inc(s["v_pe"], 1)
                    w = unit(t, u, j, 0, T)
                    if w:
                        t0, u0, j0 = w
                        k0 = (u - 1) // 2 + k
                        hp, b, r = j0 // 4, j0 // 2 % 2, j0 % 2
                        if j0 % 4 == 0:
                            pe.wait_ge(s[f"stk{hp}{u0}"], k0 * 128 + 128)
                        if j0 >= 2 or past(t0, 1):
                            pe.wait_ge(s["ex"], 8 * t0 + (j0 - 1))
                        o = bank[3 + j0 % 2]
                        mm(o[:, :], identb[:, :], mbias[:, r].rearrange("p a n -> p (a n)"), True, False)
                        for h in range(2):
                            ins = mm(o[:, h * N:(h + 1) * N], stk[:, u0, 0, 2 * hp + h, b * N + r * P:b * N + (r + 1) * P],
                                     stk[:, u0, 1, 2 * hp + h, b * N:(b + 1) * N], False, h == 1)
                        ins.then_inc(s["s_done"], 1)
                    w = unit(t, u, j, TURN_LAG, T)
                    if w:
                        t2, u2, j2 = w
                        pe.wait_ge(s["nrm"], 8 * t2 + (j2 + 1))
                        if j2 >= 2 or past(t2, 1):
                            pe.wait_ge(s["tp_c"], 8 * t2 + (j2 - 1))
                        for q in range(4):
                            ins = pe.transpose(bank[5 + j2 % 2][:, q * P:(q + 1) * P],
                                               pr(j2)[:, q * P:(q + 1) * P], ident[:, :])
                        ins.then_inc(s["tp"], 1)
                    w = unit(t, u, j, AV_LAG, T)
                    if w:
                        t3, u3, j3 = w
                        hp, b, r = j3 // 4, j3 // 2 % 2, j3 % 2
                        pe.wait_ge(s["tp_c"], 8 * t3 + (j3 + 1))
                        if j3 == 0:
                            pe.wait_ge(s["v_c"], t3 + 1)
                        if j3 == 0 and past(t3, 2):
                            pe.wait_ge(s["av_c"], t3 - 1)
                        for h in range(2):
                            c = DH * (2 * hp + h)
                            for m in range(NB):
                                ins = mm(bank[7 - 5 * u3][c:c + DH, b * N + r * P:b * N + (r + 1) * P],
                                         vr(u3)[:, (b * NB + m) * D + c:(b * NB + m) * D + c + DH],
                                         pt(j3)[:, (h * NB + m) * P:(h * NB + m + 1) * P], m == 0, m == NB - 1)
                        ins.then_inc(s["av"], 1)
            pe.wait_ge(s["ln2"], T)
            over(pe, T, 2, attend, 4)
            pe.wait_ge(s["av_c"], T)
            norm("3")

            def edges(t, u, k):
                if inside(t, T):
                    pe.wait_ge(s["xs_e"], t + 1)
                    if past(t, 2):
                        for name in ("xq_c", "xv_c", "xq_l", "xv_l"):
                            pe.wait_ge(s[name], t - 1)
                    for q in range(4):
                        mm(bank[u][:, q * P:(q + 1) * P], xs_r(u)[:, q * P:(q + 1) * P], wlin[:, :])
                    for q in range(4):
                        ins = mm(bank[2 + u][:, q * P:(q + 1) * P], xs_r(u)[:, q * P:(q + 1) * P], wval[:, :])
                    ins.then_inc(s["xqv"], 1)
                old = older(t, u, k, 1, T)
                if old:
                    t1, u1, _ = old
                    pe.wait_ge(s["xq_c"], t1 + 1)
                    pe.wait_ge(s["xq_l"], t1 + 1)
                    if past(t1, 2):
                        pe.wait_ge(s["lr"], t1 - 1)
                    for b in range(PAIR):
                        for m in range(NB):
                            for part in (e_hi, e_lo):
                                ins = mm(bank[4 + u1][:, b * E:(b + 1) * E],
                                         part[:, u1, (b * NB + m) * P:(b * NB + m + 1) * P], sum1[:, m, :],
                                         m == 0 and part is e_hi, m == NB - 1 and part is e_lo)
                    ins.then_inc(s["z_done"], 1)
                old = older(t, u, k, 2, T)
                if old:
                    t2, u2, _ = old
                    pe.wait_ge(s["lr"], t2 + 1)
                    if past(t2, 2):
                        pe.wait_ge(s["e_c"], t2 - 1)
                    for e in range(EB):
                        for b in range(PAIR):
                            c = (e * PAIR + b) * HEADS
                            ins = mm(bank[6 + u2][:, c:c + HEADS],
                                     ring[:, 14 + u2, b * E + e * P:b * E + (e + 1) * P], abd[:, :])
                    ins.then_inc(s["e_done"], 1)
            pe.wait_ge(s["ln3"], T)
            over(pe, T, 2, edges)
            pe.wait_ge(s["e_c"], T)
            for e in range(EB):
                ins = pe.transpose(bank[0][:, e * P:(e + 1) * P], ET[:, e, :], ident[:, :])
            ins.then_inc(s["tr_e"], 1)
            pe.wait_ge(s["att"], 1)
            for e in range(EB):
                ins = pe.transpose(bank[6][:, e * P:(e + 1) * P], sm[:, 3, e * P:(e + 1) * P], ident[:, :])
            ins.then_inc(s["tr_a"], 1)
            pe.wait_ge(s["at_c"], 1)

            def rows(t, u, k):
                if inside(t, T):
                    if past(t, 2):
                        pe.wait_ge(s["vt_c"], t - 1)
                    for e in range(EB):
                        for m in range(NB):
                            for x in (vv_hi, vv_lo):
                                v = x[:, cols(t, W)].rearrange("p (b m f) -> p b m f", b=PAIR, m=NB)
                                ins = mm(bank[u % 2][:, e * 256:(e + 1) * 256].rearrange("p (b f) -> p b f", b=PAIR),
                                         dst1[:, m, e * P:(e + 1) * P], v[:, :, m, :],
                                         m == 0 and x is vv_hi, m == NB - 1 and x is vv_lo)
                    ins.then_inc(s["vt"], 1)
                old = older(t, u, k, 2, T, 4)
                if old:
                    t2, u2, _ = old
                    pe.wait_ge(s["vt_l"], t2 + 1)
                    if past(t2, 2):
                        pe.wait_ge(s["yt_c"], t2 - 1)
                    for b in range(PAIR):
                        for e in range(EB):
                            for part in (e_hi, e_lo):
                                ins = mm(bank[2 + u2 % 2][:, b * N:(b + 1) * N],
                                         part[:, 2 + u2 % 2, (e * PAIR + b) * P:(e * PAIR + b + 1) * P], src1[:, e, :],
                                         e == 0 and part is e_hi, e == EB - 1 and part is e_lo)
                    ins.then_inc(s["yt"], 1)
                old = older(t, u, k, 3, T, 4)
                if old:
                    t3, u3, _ = old
                    pe.wait_ge(s["yt_c"], t3 + 1)
                    pe.wait_ge(s["xs_o"], t3 + 1)
                    if past(t3, 4):
                        pe.wait_ge(s["o_fin"], t3 - 3)
                    for q in range(4):
                        mm(bank[4 + u3][:, q * P:(q + 1) * P], xs_r(u3 % 2)[:, q * P:(q + 1) * P], ident[:, :], True, False)
                        ins = mm(bank[4 + u3][:, q * P:(q + 1) * P], ring[:, 12 + u3 % 2, q * P:(q + 1) * P], wout[:, :],
                                 False, True)
                    ins.then_inc(s["o_pe"], 1)
            over(pe, T, 3, rows, 8, unroll=4)
    return nc


def kernel(**inputs):
    import numpy as np
    import concourse.bacc as bacc
    from concourse.bass_utils import run_bass_kernel_spmd

    a = {k: np.asarray(v) for k, v in inputs.items()}
    x = a["x"]
    laid = {
        "x_tok": x,
        "x_feat": x.transpose(2, 0, 1).reshape(x.shape[2], -1),
        "adj": a["adj"],
        "adj_t": a["adj"].T,
        "w1_t": a["L0_gnn_W1"].T, "w2_t": a["L0_gnn_W2"].T,
        "cols1": np.stack([a["L0_gnn_b1"], a["L0_gnn_g1"], a["L0_gnn_be1"]]).reshape(3, -1, P).transpose(2, 0, 1),
        "cols2": np.stack([a["L0_gnn_b2"], a["L0_gnn_g2"], a["L0_gnn_be2"]]).T,
        "wg0": a["L1_gnn_Wg0"], "bg0": a["L1_gnn_bg0"], "wg1": a["L1_gnn_Wg1"], "bg1": a["L1_gnn_bg1"],
        "wih_t": a["L1_gnn_Wih"].transpose(0, 2, 1), "whh_t": a["L1_gnn_Whh"].transpose(0, 2, 1),
        "bih": a["L1_gnn_bih"].reshape(4, 4, P).transpose(2, 0, 1),
        "bhh": a["L1_gnn_bhh"].reshape(4, 4, P).transpose(2, 0, 1),
        "w_qkv": a["L2_gnn_W"],
        "w_lin_t": a["L3_gnn_W_lin"].T, "w_val_t": a["L3_gnn_W_val"].T, "a": a["L3_gnn_a"],
        "w_out_t": a["L3_gnn_W_out"].T, "src": a["L3_gnn_src"], "dst": a["L3_gnn_dst"],
        "edge_cols": np.stack([a["L3_gnn_src"], a["L3_gnn_dst"]]).reshape(2, -1, P).transpose(2, 0, 1),
    }
    nc = bacc.Bacc("TRN2", target_bir_lowering=False, num_devices=1)
    arrays, aps = {}, {}
    for name, v in laid.items():
        arrays["in_" + name] = np.ascontiguousarray(v)
        aps[name] = nc.dram_tensor("in_" + name, v.shape, mybir.dt.from_np(v.dtype), kind="ExternalInput").ap()
    aps["out"] = nc.dram_tensor("out_x", x.shape, F32, kind="ExternalOutput").ap()
    build_program(nc, **aps)
    r = run_bass_kernel_spmd(nc, [arrays], core_ids=[0])
    return r.results[0]["out_x"]
```
